# Optimizing a Trainium2 kernel written in Bass

```python
import numpy as np
import jax
import jax.numpy as jnp

def _softmax(x, axis=-1):
    return jax.nn.softmax(x, axis=axis)

def _gelu(x):
    return jax.nn.gelu(x, approximate=True)

def _silu(x):
    return jax.nn.silu(x)

def _sigmoid(x):
    return jax.nn.sigmoid(x)

def _layernorm(x, axis=-1, eps=1e-05):
    m = jnp.mean(x, axis=axis, keepdims=True)
    v = jnp.var(x, axis=axis, keepdims=True)
    return (x - m) / jnp.sqrt(v + eps)

def _scatter_add(tgt, idx, src, axis=0):
    return tgt.at[idx].add(src)

def _segment_sum(src, seg, n):
    return jax.ops.segment_sum(src, seg, n)
kernel_name = 'mk_xattn_ffn_d2_seqx_r4_f8dcd1'

def setup_inputs(seed: int=0):
    np.random.seed(seed)
    _w = jnp.asarray

    def _rec_inputs():
        import jax
        import jax.numpy as jnp
        _rk = jax.random.key(seed)
        x = 0.002226 + 0.9996 * jax.random.normal(jax.random.fold_in(_rk, 1), (64, 128, 256), jnp.float32)
        _lenS = 128 - jax.random.randint(jax.random.fold_in(_rk, 7), (64,), 0, max(1, 128 // 4) + 1, jnp.int32)
        _lenS2 = 128 - jax.random.randint(jax.random.fold_in(_rk, 8), (64,), 0, max(1, 128 // 4) + 1, jnp.int32)
        _ctx_1024P = jax.random.normal(jax.random.fold_in(_rk, 11), (64, 16, 256), jnp.float32)
        _ctx_1024c = jax.random.dirichlet(jax.random.fold_in(_rk, 511), 0.3 * jnp.ones((16,), jnp.float32), (64, 128))
        _ctx_1024t = jnp.einsum('bsk,bkd->bsd', _ctx_1024c, _ctx_1024P)
        _ctx_1024t = _ctx_1024t * jax.lax.rsqrt(jnp.mean(jnp.square(_ctx_1024t)) + 1e-12) * 0.953939
        ctx_1024 = -0.000125008 + 0.999885 * (_ctx_1024t + 0.3 * jax.random.normal(jax.random.fold_in(_rk, 611), (64, 128, 256), jnp.float32))
        return (x, ctx_1024)
    x, ctx_1024 = _rec_inputs()

    def _L0_xattn_setup():
        import jax, jax.numpy as jnp
        import numpy as np
        DIM = 256
        HEADS = 16
        DIM_HEAD = 64
        INNER = HEADS * DIM_HEAD
        EPS = 1e-05

        def _layernorm(x, w, b):
            m = jnp.mean(x, axis=-1, keepdims=True)
            v = jnp.mean(jnp.square(x - m), axis=-1, keepdims=True)
            return (x - m) * jax.lax.rsqrt(v + EPS) * w + b
        key = jax.random.key(seed)
        ks = jax.random.split(key, 9)
        B, N, L = (8, 1024, 64)
        x = jax.random.normal(ks[0], (B, N, DIM), dtype=jnp.float32)
        latents = jax.random.normal(ks[1], (B, L, DIM), dtype=jnp.float32)
        s = 1.0 / np.sqrt(DIM)
        Wq = jax.random.normal(ks[2], (DIM, INNER), dtype=jnp.float32) * s
        Wkv = jax.random.normal(ks[3], (DIM, 2 * INNER), dtype=jnp.float32) * s
        Wo = jax.random.normal(ks[4], (INNER, DIM), dtype=jnp.float32) * (1.0 / np.sqrt(INNER))
        ln1_w = jnp.ones((DIM,), jnp.float32)
        ln1_b = jnp.zeros((DIM,), jnp.float32)
        ln2_w = jnp.ones((DIM,), jnp.float32)
        ln2_b = jnp.zeros((DIM,), jnp.float32)
        return {'x': x, 'latents': latents, 'Wq': Wq, 'Wkv': Wkv, 'Wo': Wo, 'ln1_w': ln1_w, 'ln1_b': ln1_b, 'ln2_w': ln2_w, 'ln2_b': ln2_b}
    _L0_xattn_all = _L0_xattn_setup()
    _L0_xattn_in = {k: v for k, v in _L0_xattn_all.items() if k in ('Wq', 'Wkv', 'Wo', 'ln1_w', 'ln1_b', 'ln2_w', 'ln2_b')}
    del _L0_xattn_all

    def _L0_ffn_setup():
        import jax, jax.numpy as jnp
        import numpy as np
        E = 16
        G = 4
        EPG = E // G
        K = 4
        TOPK_GROUP = 2
        PER_GROUP_K = K // TOPK_GROUP

        def _route(xf, router_w, correction_bias):
            S = xf.shape[0]
            logits = xf @ router_w.T
            scores = jax.nn.sigmoid(logits)
            sb = scores + correction_bias
            grp_top = jax.lax.top_k(sb.reshape(S, G, EPG), PER_GROUP_K)[0]
            group_scores = grp_top.sum(axis=-1)
            _, group_idx = jax.lax.top_k(group_scores, TOPK_GROUP)
            group_mask = jnp.zeros((S, G), sb.dtype).at[jnp.arange(S)[:, None], group_idx].set(1.0)
            score_mask = jnp.broadcast_to(group_mask[:, :, None], (S, G, EPG)).reshape(S, E)
            masked = jnp.where(score_mask > 0, sb, -jnp.inf)
            _, topk_idx = jax.lax.top_k(masked, K)
            w = jnp.take_along_axis(scores, topk_idx, axis=1)
            w = w / (w.sum(axis=-1, keepdims=True) + 1e-20)
            return (topk_idx, w, scores)
        key = jax.random.key(seed)
        ks = jax.random.split(key, 9)
        B, T, C, H, HS = (2, 256, 256, 64, 512)
        std = 0.02
        return {'x': jax.random.normal(ks[0], (B, T, C), jnp.float32), 'router_w': jax.random.normal(ks[1], (E, C), jnp.float32) * std, 'correction_bias': jnp.zeros((E,), jnp.float32), 'gate_w': jax.random.normal(ks[2], (E, C, H), jnp.float32) * std, 'up_w': jax.random.normal(ks[3], (E, C, H), jnp.float32) * std, 'down_w': jax.random.normal(ks[4], (E, H, C), jnp.float32) * std, 'shared_gate_w': jax.random.normal(ks[5], (HS, C), jnp.float32) * std, 'shared_up_w': jax.random.normal(ks[6], (HS, C), jnp.float32) * std, 'shared_down_w': jax.random.normal(ks[7], (C, HS), jnp.float32) * std}
    _L0_ffn_all = _L0_ffn_setup()
    _L0_ffn_in = {k: v for k, v in _L0_ffn_all.items() if k in ('router_w', 'correction_bias', 'gate_w', 'up_w', 'down_w', 'shared_gate_w', 'shared_up_w', 'shared_down_w')}
    del _L0_ffn_all

    def _L1_xattn_setup():
        import jax, jax.numpy as jnp
        import numpy as np
        from jax import lax
        BIG = jnp.float32(1e+30)

        def _pairwise_euclidean(a, b):
            aa = jnp.sum(a * a, axis=-1)[:, None]
            bb = jnp.sum(b * b, axis=-1)[None, :]
            ab = a @ b.T
            return jnp.sqrt(jnp.maximum(aa + bb - 2.0 * ab, 0.0))

        def _dtw_cost(D):
            row0 = jnp.cumsum(D[0])

            def row_step(prev_row, d_row):
                first = d_row[0] + prev_row[0]

                def col_step(left, inp):
                    d_ij, up, diag = inp
                    r = d_ij + jnp.minimum(jnp.minimum(up, left), diag)
                    return (r, r)
                _, rest = lax.scan(col_step, first, (d_row[1:], prev_row[1:], prev_row[:-1]))
                row = jnp.concatenate([first[None], rest])
                return (row, row)
            _, rows = lax.scan(row_step, row0, D[1:])
            return jnp.concatenate([row0[None], rows], axis=0)

        def _backtrack(R, T1, T2):
            L = T1 + T2 - 1

            def step(carry, _):
                i, j, done = carry
                valid = jnp.logical_not(done)
                cd = jnp.where((i > 0) & (j > 0), R[jnp.maximum(i - 1, 0), jnp.maximum(j - 1, 0)], BIG)
                cu = jnp.where(i > 0, R[jnp.maximum(i - 1, 0), j], BIG)
                cl = jnp.where(j > 0, R[i, jnp.maximum(j - 1, 0)], BIG)
                choice = jnp.argmin(jnp.stack([cd, cu, cl]))
                ni = jnp.where(choice <= 1, i - 1, i)
                nj = jnp.where((choice == 0) | (choice == 2), j - 1, j)
                at_origin = (i == 0) & (j == 0)
                ni = jnp.where(at_origin, 0, ni)
                nj = jnp.where(at_origin, 0, nj)
                return ((ni, nj, done | at_origin), (i, j, valid))
            init = (jnp.int32(T1 - 1), jnp.int32(T2 - 1), jnp.bool_(False))
            _, (i_idx, j_idx, valid) = lax.scan(step, init, None, length=L)
            return (i_idx, j_idx, valid)

        def _align_one(small, large):
            T_small, d = small.shape
            T_large = large.shape[0]
            D = _pairwise_euclidean(small, large)
            R = _dtw_cost(D)
            i_idx, j_idx, valid = _backtrack(R, T_small, T_large)
            contrib = small[i_idx] * valid[:, None].astype(small.dtype)
            expanded = jnp.zeros((T_large, d), dtype=small.dtype).at[j_idx].add(contrib)
            return expanded
        key = jax.random.key(seed)
        k1, k2 = jax.random.split(key)
        teacher = jax.random.normal(k1, (16, 100, 256), dtype=jnp.float32)
        student = jax.random.normal(k2, (16, 150, 256), dtype=jnp.float32)
        return {'teacher_features': teacher, 'student_features': student}
    _L1_xattn_all = _L1_xattn_setup()
    _L1_xattn_in = {k: v for k, v in _L1_xattn_all.items() if k in ()}
    del _L1_xattn_all

    def _L1_ffn_setup():
        import jax, jax.numpy as jnp
        import numpy as np
        B, S, D_MODEL, D_HIDDEN = (4, 512, 256, 1024)

        def act_quant(x):
            scale = 127.0 / jnp.clip(jnp.max(jnp.abs(x), axis=-1, keepdims=True), 1e-05)
            return jnp.clip(jnp.round(x * scale), -128, 127) / scale

        def weight_quant(w):
            scale = 1.0 / jnp.clip(jnp.mean(jnp.abs(w)), 1e-05)
            return jnp.clip(jnp.round(w * scale), -1, 1) / scale

        def bit_linear(x, w):
            xq = x + jax.lax.stop_gradient(act_quant(x) - x)
            wq = w + jax.lax.stop_gradient(weight_quant(w) - w)
            return jnp.einsum('bsd,hd->bsh', xq, wq)

        def depthwise_conv1d(x_bcl, w, b):
            y = jax.lax.conv_general_dilated(x_bcl, w, window_strides=(1,), padding=[(1, 1)], dimension_numbers=('NCH', 'OIH', 'NCH'), feature_group_count=x_bcl.shape[1])
            return y + b[None, :, None]
        key = jax.random.key(seed)
        ks = jax.random.split(key, 5)
        lim1 = 1.0 / np.sqrt(D_MODEL)
        lim2 = 1.0 / np.sqrt(D_HIDDEN)
        limc = 1.0 / np.sqrt(3.0)
        return {'x': jax.random.normal(ks[0], (B, S, D_MODEL), dtype=jnp.float32), 'w1': jax.random.uniform(ks[1], (D_HIDDEN, D_MODEL), jnp.float32, -lim1, lim1), 'conv_w': jax.random.uniform(ks[2], (D_HIDDEN, 1, 3), jnp.float32, -limc, limc), 'conv_b': jax.random.uniform(ks[3], (D_HIDDEN,), jnp.float32, -limc, limc), 'w2': jax.random.uniform(ks[4], (D_MODEL, D_HIDDEN), jnp.float32, -lim2, lim2)}
    _L1_ffn_all = _L1_ffn_setup()
    _L1_ffn_in = {k: v for k, v in _L1_ffn_all.items() if k in ('w1', 'conv_w', 'conv_b', 'w2')}
    del _L1_ffn_all
    return {'x': x, 'ctx_1024': ctx_1024, 'L0_xattn_Wq': _L0_xattn_in['Wq'], 'L0_xattn_Wkv': _L0_xattn_in['Wkv'], 'L0_xattn_Wo': _L0_xattn_in['Wo'], 'L0_xattn_ln1_w': _L0_xattn_in['ln1_w'], 'L0_xattn_ln1_b': _L0_xattn_in['ln1_b'], 'L0_xattn_ln2_w': _L0_xattn_in['ln2_w'], 'L0_xattn_ln2_b': _L0_xattn_in['ln2_b'], 'L0_ffn_router_w': _L0_ffn_in['router_w'], 'L0_ffn_correction_bias': _L0_ffn_in['correction_bias'], 'L0_ffn_gate_w': _L0_ffn_in['gate_w'], 'L0_ffn_up_w': _L0_ffn_in['up_w'], 'L0_ffn_down_w': _L0_ffn_in['down_w'], 'L0_ffn_shared_gate_w': _L0_ffn_in['shared_gate_w'], 'L0_ffn_shared_up_w': _L0_ffn_in['shared_up_w'], 'L0_ffn_shared_down_w': _L0_ffn_in['shared_down_w'], 'L1_ffn_w1': _L1_ffn_in['w1'], 'L1_ffn_conv_w': _L1_ffn_in['conv_w'], 'L1_ffn_conv_b': _L1_ffn_in['conv_b'], 'L1_ffn_w2': _L1_ffn_in['w2']}

def reference(x, ctx_1024, L0_xattn_Wq, L0_xattn_Wkv, L0_xattn_Wo, L0_xattn_ln1_w, L0_xattn_ln1_b, L0_xattn_ln2_w, L0_xattn_ln2_b, L0_ffn_router_w, L0_ffn_correction_bias, L0_ffn_gate_w, L0_ffn_up_w, L0_ffn_down_w, L0_ffn_shared_gate_w, L0_ffn_shared_up_w, L0_ffn_shared_down_w, L1_ffn_w1, L1_ffn_conv_w, L1_ffn_conv_b, L1_ffn_w2):
    import jax
    import jax.numpy as jnp

    def _L0_xattn_ref(x, latents, Wq, Wkv, Wo, ln1_w, ln1_b, ln2_w, ln2_b):
        import jax, jax.numpy as jnp
        import numpy as np
        DIM = 256
        HEADS = 16
        DIM_HEAD = 64
        INNER = HEADS * DIM_HEAD
        EPS = 1e-05

        def _layernorm(x, w, b):
            m = jnp.mean(x, axis=-1, keepdims=True)
            v = jnp.mean(jnp.square(x - m), axis=-1, keepdims=True)
            return (x - m) * jax.lax.rsqrt(v + EPS) * w + b
        B, L, _ = latents.shape
        xn = _layernorm(x, ln1_w, ln1_b)
        ln = _layernorm(latents, ln2_w, ln2_b)
        q = ln @ Wq
        kv_input = jnp.concatenate([xn, ln], axis=-2)
        kv = kv_input @ Wkv
        k, v = jnp.split(kv, 2, axis=-1)

        def heads(t):
            b, s, _ = t.shape
            return t.reshape(b, s, HEADS, DIM_HEAD).transpose(0, 2, 1, 3)
        q, k, v = (heads(q), heads(k), heads(v))
        scale = 1.0 / np.sqrt(np.sqrt(DIM_HEAD))
        logits = jnp.einsum('bhld,bhsd->bhls', q * scale, k * scale)
        w = jax.nn.softmax(logits.astype(jnp.float32), axis=-1).astype(logits.dtype)
        out = jnp.einsum('bhls,bhsd->bhld', w, v)
        out = out.transpose(0, 2, 1, 3).reshape(B, L, INNER)
        return out @ Wo

    def _L0_ffn_ref(x, router_w, correction_bias, gate_w, up_w, down_w, shared_gate_w, shared_up_w, shared_down_w):
        import jax, jax.numpy as jnp
        import numpy as np
        E = 16
        G = 4
        EPG = E // G
        K = 4
        TOPK_GROUP = 2
        PER_GROUP_K = K // TOPK_GROUP

        def _route(xf, router_w, correction_bias):
            S = xf.shape[0]
            logits = xf @ router_w.T
            scores = jax.nn.sigmoid(logits)
            sb = scores + correction_bias
            grp_top = jax.lax.top_k(sb.reshape(S, G, EPG), PER_GROUP_K)[0]
            group_scores = grp_top.sum(axis=-1)
            _, group_idx = jax.lax.top_k(group_scores, TOPK_GROUP)
            group_mask = jnp.zeros((S, G), sb.dtype).at[jnp.arange(S)[:, None], group_idx].set(1.0)
            score_mask = jnp.broadcast_to(group_mask[:, :, None], (S, G, EPG)).reshape(S, E)
            masked = jnp.where(score_mask > 0, sb, -jnp.inf)
            _, topk_idx = jax.lax.top_k(masked, K)
            w = jnp.take_along_axis(scores, topk_idx, axis=1)
            w = w / (w.sum(axis=-1, keepdims=True) + 1e-20)
            return (topk_idx, w, scores)
        B, T, C = x.shape
        S = B * T
        xf = x.reshape(S, C)
        sg = xf @ shared_gate_w.T
        su = xf @ shared_up_w.T
        shared_out = jax.nn.silu(sg) * su @ shared_down_w.T
        topk_idx, w, _scores = _route(xf, router_w, correction_bias)
        combine = jnp.zeros((S, E), xf.dtype).at[jnp.arange(S)[:, None], topk_idx].add(w)
        g = jnp.einsum('sc,ech->esh', xf, gate_w)
        u = jnp.einsum('sc,ech->esh', xf, up_w)
        h = jax.nn.silu(g) * u
        hw = h * combine.T[:, :, None]
        routed = jnp.einsum('esh,ehc->sc', hw, down_w)
        return (shared_out + routed).reshape(B, T, C)

    def _L1_xattn_ref(teacher_features, student_features):
        import jax, jax.numpy as jnp
        import numpy as np
        from jax import lax
        BIG = jnp.float32(1e+30)

        def _pairwise_euclidean(a, b):
            aa = jnp.sum(a * a, axis=-1)[:, None]
            bb = jnp.sum(b * b, axis=-1)[None, :]
            ab = a @ b.T
            return jnp.sqrt(jnp.maximum(aa + bb - 2.0 * ab, 0.0))

        def _dtw_cost(D):
            row0 = jnp.cumsum(D[0])

            def row_step(prev_row, d_row):
                first = d_row[0] + prev_row[0]

                def col_step(left, inp):
                    d_ij, up, diag = inp
                    r = d_ij + jnp.minimum(jnp.minimum(up, left), diag)
                    return (r, r)
                _, rest = lax.scan(col_step, first, (d_row[1:], prev_row[1:], prev_row[:-1]))
                row = jnp.concatenate([first[None], rest])
                return (row, row)
            _, rows = lax.scan(row_step, row0, D[1:])
            return jnp.concatenate([row0[None], rows], axis=0)

        def _backtrack(R, T1, T2):
            L = T1 + T2 - 1

            def step(carry, _):
                i, j, done = carry
                valid = jnp.logical_not(done)
                cd = jnp.where((i > 0) & (j > 0), R[jnp.maximum(i - 1, 0), jnp.maximum(j - 1, 0)], BIG)
                cu = jnp.where(i > 0, R[jnp.maximum(i - 1, 0), j], BIG)
                cl = jnp.where(j > 0, R[i, jnp.maximum(j - 1, 0)], BIG)
                choice = jnp.argmin(jnp.stack([cd, cu, cl]))
                ni = jnp.where(choice <= 1, i - 1, i)
                nj = jnp.where((choice == 0) | (choice == 2), j - 1, j)
                at_origin = (i == 0) & (j == 0)
                ni = jnp.where(at_origin, 0, ni)
                nj = jnp.where(at_origin, 0, nj)
                return ((ni, nj, done | at_origin), (i, j, valid))
            init = (jnp.int32(T1 - 1), jnp.int32(T2 - 1), jnp.bool_(False))
            _, (i_idx, j_idx, valid) = lax.scan(step, init, None, length=L)
            return (i_idx, j_idx, valid)

        def _align_one(small, large):
            T_small, d = small.shape
            T_large = large.shape[0]
            D = _pairwise_euclidean(small, large)
            R = _dtw_cost(D)
            i_idx, j_idx, valid = _backtrack(R, T_small, T_large)
            contrib = small[i_idx] * valid[:, None].astype(small.dtype)
            expanded = jnp.zeros((T_large, d), dtype=small.dtype).at[j_idx].add(contrib)
            return expanded
        return jax.vmap(_align_one)(teacher_features, student_features)

    def _L1_ffn_ref(x, w1, conv_w, conv_b, w2):
        import jax, jax.numpy as jnp
        import numpy as np
        B, S, D_MODEL, D_HIDDEN = (4, 512, 256, 1024)

        def act_quant(x):
            scale = 127.0 / jnp.clip(jnp.max(jnp.abs(x), axis=-1, keepdims=True), 1e-05)
            return jnp.clip(jnp.round(x * scale), -128, 127) / scale

        def weight_quant(w):
            scale = 1.0 / jnp.clip(jnp.mean(jnp.abs(w)), 1e-05)
            return jnp.clip(jnp.round(w * scale), -1, 1) / scale

        def bit_linear(x, w):
            xq = x + jax.lax.stop_gradient(act_quant(x) - x)
            wq = w + jax.lax.stop_gradient(weight_quant(w) - w)
            return jnp.einsum('bsd,hd->bsh', xq, wq)

        def depthwise_conv1d(x_bcl, w, b):
            y = jax.lax.conv_general_dilated(x_bcl, w, window_strides=(1,), padding=[(1, 1)], dimension_numbers=('NCH', 'OIH', 'NCH'), feature_group_count=x_bcl.shape[1])
            return y + b[None, :, None]
        h = bit_linear(x, w1)
        h = depthwise_conv1d(h.transpose(0, 2, 1), conv_w, conv_b)
        h = h.transpose(0, 2, 1)
        h = jax.nn.silu(h)
        return bit_linear(h, w2)
    x = x + _L0_xattn_ref(ctx_1024, _layernorm(x, axis=-1), L0_xattn_Wq, L0_xattn_Wkv, L0_xattn_Wo, L0_xattn_ln1_w, L0_xattn_ln1_b, L0_xattn_ln2_w, L0_xattn_ln2_b)
    x = x + _L0_ffn_ref(_layernorm(x, axis=-1), L0_ffn_router_w, L0_ffn_correction_bias, L0_ffn_gate_w, L0_ffn_up_w, L0_ffn_down_w, L0_ffn_shared_gate_w, L0_ffn_shared_up_w, L0_ffn_shared_down_w)
    x = x + _L1_xattn_ref(ctx_1024, _layernorm(x, axis=-1))
    x = x + _L1_ffn_ref(_layernorm(x, axis=-1), L1_ffn_w1, L1_ffn_conv_w, L1_ffn_conv_b, L1_ffn_w2)
    return x

_drawn_inputs = setup_inputs


def setup_inputs(seed=0):
    import zlib

    import numpy as np

    out = dict(_drawn_inputs(seed))
    spreads = {'L0_xattn_ln1_w': (1.0, 0.2),
     'L0_xattn_ln1_b': (0.0, 0.1),
     'L0_xattn_ln2_w': (1.0, 0.6),
     'L0_xattn_ln2_b': (0.0, 0.1),
     'L0_ffn_correction_bias': (0.0, 0.8)}
    factors = {'L0_ffn_router_w': 8.0,
     'L0_ffn_gate_w': 8.0,
     'L0_ffn_up_w': 8.0,
     'L0_ffn_down_w': 8.0,
     'L0_ffn_shared_up_w': 3.418,
     'L0_ffn_shared_down_w': 3.428,
     'L1_ffn_w1': 3.558,
     'L1_ffn_conv_w': 3.541,
     'L1_ffn_conv_b': 2.999}
    for name, (base, spread) in spreads.items():
        noise = np.random.default_rng([zlib.crc32(name.encode()), seed]).standard_normal(out[name].shape)
        drawn = base * np.exp(spread * noise) if base else spread * noise
        out[name] = jnp.asarray(drawn.astype(out[name].dtype))
    for name, factor in factors.items():
        out[name] = (out[name] * factor).astype(out[name].dtype)
    return out
```

```python
from contextlib import ExitStack

import numpy as np

import concourse.bass as bass
from concourse import mybir

F32 = mybir.dt.float32
F32R = mybir.dt.float32r
BF16 = mybir.dt.bfloat16
ALU = mybir.AluOpType
ACT = mybir.ActivationFunctionType
AX = mybir.AxisListType

P = 128
SEQS, TOK, DIM = 64, 128, 256
KD = DIM // P
HEADS, HEAD = 16, 64
INNER = HEADS * HEAD
EXPERTS, HID, SHARED = 16, 64, 512
ROUTED = EXPERTS * HID
GROUPS, PICK_GROUPS, PICK = 4, 2, 4
CONV_HID = 1024
EPS = 1e-5
BIG = 1e30
ROUND = 1.5 * 2.0 ** 23
GB = 4
NG = SEQS // GB


class Queue:

    def __init__(self, sem):
        self.sem, self.count, self.items, self.known = sem, 0, [], {}

    def do(self, build, *args, **kwargs):
        self.items.append([build, args, kwargs, None])
        return self

    def mark(self):
        self.count += 1
        self.items[-1][3] = (self.sem, 1)
        return (self.sem, self.count)

    def wait(self, *counts):
        for sem, value in counts:
            if self.known.get(sem.name, 0) < value:
                self.known[sem.name] = value
                self.items.append([None, (sem, value), None, None])
        return self

    def dma(self, build, lane, out, in_):
        lane[1] += 16
        self.items.append([build, (out, in_), {}, (lane[0], 16)])
        return (lane[0], lane[1])

    def replay(self, engine):
        for build, args, kwargs, inc in self.items:
            if build is None:
                engine.wait_ge(*args)
            else:
                made = build(*args, **kwargs)
                if inc:
                    made.then_inc(*inc)


class Stage:

    def __init__(self, nc, name):
        self.nc, self.name, self.ctx = nc, name, ExitStack()

    def __enter__(self):
        self.pe, self.act, self.dve, self.pool, self.sp = (
            Queue(self.sem(n)) for n in ("pe", "act", "dve", "pool", "sp"))
        return self

    def sem(self, n):
        return self.ctx.enter_context(self.nc.semaphore(f"{self.name}_{n}_done"))

    def lane(self, n):
        return [self.sem(n), 0]

    def sb(self, n, shape, dt=F32):
        return self.ctx.enter_context(self.nc.sbuf_tensor(f"{self.name}_{n}", shape, dt))

    def bank(self, n, dt=F32):
        return self.ctx.enter_context(
            self.nc.psum_tensor(f"{self.name}_{n}", [P, 2048 // mybir.dt.size(dt)], dt))

    def __exit__(self, kind, *rest):
        if kind is None:
            with self.nc.Block() as block:
                block.sync(self.sp.replay)
                block.tensor(self.pe.replay)
                block.scalar(self.act.replay)
                block.vector(self.dve.replay)
                block.gpsimd(self.pool.replay)
        return self.ctx.__exit__(kind, *rest)


def pipeline(count, *steps):
    for t in range(count + len(steps) - 1):
        for s in reversed(range(len(steps))):
            if 0 <= t - s < count:
                steps[s](t - s)


def split_weight(st, lane, stage, stage_free, src, hi, lo, width):
    nc = st.nc
    st.sp.wait(*stage_free)
    landed = st.sp.dma(nc.sync.dma_start, lane, stage, src)
    st.dve.wait(landed)
    high = st.dve.do(nc.vector.tensor_copy, hi, stage).mark()
    st.dve.wait(high)
    return st.dve.do(nc.vector.tensor_tensor, lo, stage, hi.bitcast(F32), ALU.subtract).mark()


def rsqrt_var(st, mv, var_eps, rstd, half, n, ready, free=()):
    nc = st.nc
    st.pool.wait(*ready, *free)
    a = st.pool.do(nc.gpsimd.tensor_scalar, var_eps, mv[:, 0:n, 1], EPS, None, ALU.add).mark()
    st.pool.wait(a)
    return st.pool.do(nc.gpsimd.tensor_tensor, rstd, var_eps, half[:, 0:n], ALU.pow).mark()


def stats(st, tiles, raw, mv):
    nc = st.nc
    for n, t in enumerate(tiles):
        st.dve.do(nc.vector.bn_stats, raw[:, n, :], t)
    done = st.dve.mark()
    st.dve.wait(done)
    for n in range(len(tiles)):
        st.dve.do(nc.vector.bn_aggr, mv[:, n, :], raw[:, n, :])
    return st.dve.mark()


def normalise(st, outs, tiles, mv, rstd, ready):
    nc = st.nc
    st.dve.wait(*ready)
    for n, t in enumerate(tiles):
        st.dve.do(nc.vector.tensor_scalar, outs[n], t, mv[:, n, 0:1], rstd[:, n:n + 1],
                  ALU.subtract, ALU.mult)
    return st.dve.mark()


def attention(nc, x_all, ident, half, x, ctx, wq, wkv, wo, ln_cols):
    QUADS = HEADS // 4
    with Stage(nc, "attention") as st:
        pe, act, dve, pool, sp = st.pe, st.act, st.dve, st.pool, st.sp
        wq_hi, wq_lo = (st.sb(n, [P, KD, INNER], F32R) for n in ("wq_hi", "wq_lo"))
        wkv_hi, wkv_lo = (st.sb(n, [P, KD, 2 * INNER], F32R) for n in ("wkv_hi", "wkv_lo"))
        wo_sb = st.sb("wo", [P, INNER // P, DIM])
        cols = st.sb("ln_cols", [P, 4, KD])
        ctx_sb = [st.sb(f"ctx{i}", [P, 2, DIM]) for i in range(2)]
        lat = [st.sb(f"latents{i}", [P, 2, DIM]) for i in range(2)]
        raw = st.sb("raw_stats", [P, 4, 6])
        mv = [st.sb(f"mean_var{i}", [P, 4, 2]) for i in range(2)]
        var_eps = [st.sb(f"var_eps{i}", [P, 4]) for i in range(2)]
        rstd = [st.sb(f"rstd{i}", [P, 4]) for i in range(2)]
        kv_full = st.sb("kv_full", [P, KD, 2 * TOK])
        kv_hi = [st.sb(f"kv_hi{i}", [P, KD, 2 * TOK], F32R) for i in range(2)]
        kv_lo = [st.sb(f"kv_lo{i}", [P, KD, 2 * TOK], F32R) for i in range(2)]
        qT = [st.sb(f"qT{i}", [P, INNER // P, TOK]) for i in range(2)]
        kT = [st.sb(f"kT{i}", [P, INNER // P, 2 * TOK]) for i in range(2)]
        v = [st.sb(f"v{i}", [P, 2, INNER]) for i in range(2)]
        prob = [st.sb(f"prob{i}", [P, 4, 2 * TOK]) for i in range(2)]
        probT = [st.sb(f"probT{i}", [P, 4, 2, TOK]) for i in range(2)]
        neg_max = st.sb("neg_max", [P, 2, 4])
        sums = st.sb("row_sums", [P, 2, HEADS])
        inv = st.sb("inv_sums", [P, 2, HEADS])
        att = st.sb("att", [P, INNER])
        attT = st.sb("attT", [P, INNER // P, TOK])
        proj = [st.bank(f"proj{i}") for i in range(3)]
        scores = [st.bank(f"scores{i}") for i in range(2)]
        turned = [st.bank(f"turned{i}") for i in range(2)]
        heads_out = st.bank("heads_out")

        x_lane = st.lane("x_load")
        for g in range(0, SEQS, 8):
            x_in = sp.dma(nc.sync.dma_start, x_lane, x_all[:, g:g + 8, :],
                          x[g:g + 8].rearrange("b t d -> t b d"))
        w_lane = st.lane("weight_load")
        sp.dma(nc.sync.dma_start, w_lane, cols[:, :, :], ln_cols)
        w_in = sp.dma(nc.sync.dma_start, w_lane, wo_sb[:, :, :], wo.rearrange("(k p) n -> p k n", p=P))
        pool.do(nc.gpsimd.memset, half[:, :], -0.5)
        zero = pool.do(nc.gpsimd.memset, ident[:, :], 0.0).mark()
        pool.wait(zero)
        const = pool.do(nc.gpsimd.affine_select, out=ident[:, :], in_=ident[:, :],
                        compare_op=ALU.not_equal, fill=1.0, base=0, pattern=[[-1, P]],
                        channel_multiplier=1).mark()
        stage_lane = [st.lane(f"stage_load{i}") for i in range(2)]
        staged = []
        at = 0
        for src, hi, lo, width in ((wq, wq_hi, wq_lo, INNER), (wkv, wkv_hi, wkv_lo, 2 * INNER)):
            for k in range(KD):
                for c in range(0, width, INNER):
                    buf = prob[at % 2][:, :, :].rearrange("p a b -> p (a b)")
                    free = staged[at - 2:at - 1] if at >= 2 else ()
                    w = slice(c, c + INNER)
                    staged.append(split_weight(st, stage_lane[at % 2], buf, free,
                                               src[k * P:(k + 1) * P, w], hi[:, k, w], lo[:, k, w], INNER))
                    at += 1
        w_split = staged[-1]

        ctx_lane = [st.lane(f"ctx_load{i}") for i in range(2)]
        normed, turned_in, ctx_in = {}, {}, {}
        kv_ready, q_ready, k_ready, v_ready = {}, {}, {}, {}
        proj_free = {}
        n_proj = [0]
        proj_read = {}
        kv_used, q_used, v_used = {}, {}, {}
        max_done, exp_done, score_done, t_done, t_copied, pv_done = {}, {}, {}, {}, {}, {}
        turn_free = {}
        n_turn = [0]
        norm_done, attT_done, added = {}, {}, {}

        def take_proj():
            i = n_proj[0] % len(proj)
            n_proj[0] += 1
            if i in proj_free:
                pe.wait(proj_free[i])
            return i, proj[i]

        def norm_pair(b):
            s = (b // 2) % 2
            if b >= 4:
                sp.wait(turned_in[b - 4], turned_in[b - 3])
            ctx_in[b] = sp.dma(nc.sync.dma_start, ctx_lane[s], ctx_sb[s][:, :, :],
                               ctx[b:b + 2].rearrange("b t d -> t b d"))
            xs = [x_all[:, b + i, :] for i in range(2)]
            cs = [ctx_sb[s][:, i, :] for i in range(2)]
            ls = [lat[s][:, i, :] for i in range(2)]
            dve.wait(x_in, ctx_in[b])
            got = stats(st, xs + cs, raw, mv[0])
            r = rsqrt_var(st, mv[0], var_eps[0][:, :], rstd[0][:, :], half, 4, (got, const))
            if b >= 4:
                dve.wait(turned_in[b - 4], turned_in[b - 3])
            one = normalise(st, ls + cs, xs + cs, mv[0], rstd[0], (r,))
            dve.wait(one)
            got = stats(st, ls, raw, mv[1])
            r = rsqrt_var(st, mv[1], var_eps[1][:, 0:2], rstd[1][:, 0:2], half, 2, (got,))
            normed[b] = normed[b + 1] = normalise(st, ls, ls, mv[1], rstd[1], (r,))

        def turn_inputs(b):
            s, i = (b // 2) % 2, b % 2
            at, bank = take_proj()
            pe.wait(normed[b], const)
            view = bank[:, :].rearrange("p (k c t) -> p k c t", k=KD, c=2)
            for k in range(KD):
                for c, src in enumerate((ctx_sb[s], lat[s])):
                    pe.do(nc.tensor.transpose, view[:, k, c, :], src[:, i, k * P:(k + 1) * P], ident[:, :])
            turned_in[b] = pe.mark()
            dve.wait(turned_in[b], w_in)
            if b:
                dve.wait(kv_ready[b - 1])
            for k in range(KD):
                for c in range(2):
                    dve.do(nc.vector.tensor_scalar, kv_full[:, k, c * TOK:(c + 1) * TOK], view[:, k, c, :],
                           cols[:, 2 * c, k:k + 1], cols[:, 2 * c + 1, k:k + 1], ALU.mult, ALU.add)
            full = proj_free[at] = dve.mark()
            act.wait(full)
            pool.wait(full)
            if b >= 2:
                act.wait(kv_used[b - 2])
                pool.wait(kv_used[b - 2])
            high = act.do(nc.scalar.activation, kv_hi[b % 2][:, :, :], kv_full[:, :, :], ACT.Copy).mark()
            pool.wait(high)
            kv_ready[b] = pool.do(nc.gpsimd.tensor_tensor, kv_lo[b % 2][:, :, :], kv_full[:, :, :],
                                  kv_hi[b % 2][:, :, :].bitcast(F32), ALU.subtract).mark()

        def three_pass(out, l_hi, l_lo, r_hi, r_lo, first, last):
            for n, (l, r) in enumerate(((l_hi, r_hi), (l_hi, r_lo), (l_lo, r_hi))):
                pe.do(nc.tensor.matmul, out, l, r, start=first and n == 0, stop=last and n == 2)

        def project(b, part):
            s = b % 2
            pe.wait(kv_ready[b], w_split)
            hi, lo = kv_hi[s], kv_lo[s]
            jobs = ([("q", 0), ("k", 0), ("k", 1)], [("q", 1), ("k", 2), ("k", 3)],
                    [("v", 0), ("v", 2)], [("v", 1), ("v", 3)])[part]
            for kind, j in jobs:
                at, bank = take_proj()
                if kind == "q":
                    for m in range(4):
                        w = slice((4 * j + m) * P, (4 * j + m + 1) * P)
                        for k in range(KD):
                            three_pass(bank[:, m * TOK:(m + 1) * TOK], wq_hi[:, k, w], wq_lo[:, k, w],
                                       hi[:, k, TOK:], lo[:, k, TOK:], k == 0, k == KD - 1)
                elif kind == "k":
                    for m in range(2):
                        w = slice((2 * j + m) * P, (2 * j + m + 1) * P)
                        for k in range(KD):
                            three_pass(bank[:, m * 2 * TOK:(m + 1) * 2 * TOK], wkv_hi[:, k, w],
                                       wkv_lo[:, k, w], hi[:, k, :], lo[:, k, :], k == 0, k == KD - 1)
                else:
                    t, w = j % 2, slice(INNER + (j // 2) * 512, INNER + (j // 2) * 512 + 512)
                    ts = slice(t * TOK, (t + 1) * TOK)
                    for k in range(KD):
                        three_pass(bank[:, :], hi[:, k, ts], lo[:, k, ts], wkv_hi[:, k, w],
                                   wkv_lo[:, k, w], k == 0, k == KD - 1)
                made = pe.mark()
                if part == 3:
                    kv_used[b] = made
                act.wait(made)
                if kind == "q":
                    if b >= 2:
                        act.wait(q_used[b - 2])
                    proj_free[at] = q_ready[b] = act.do(
                        nc.scalar.activation, qT[s][:, 4 * j:4 * j + 4, :],
                        bank[:, :].rearrange("p (m t) -> p m t", m=4), ACT.Copy, scale=HEAD ** -0.5).mark()
                elif kind == "k":
                    if b >= 2:
                        act.wait(q_used[b - 2])
                    proj_free[at] = k_ready[b] = act.do(
                        nc.scalar.activation, kT[s][:, 2 * j:2 * j + 2, :],
                        bank[:, :].rearrange("p (m t) -> p m t", m=2), ACT.Copy).mark()
                else:
                    if b >= 2:
                        act.wait(v_used[b - 2])
                    proj_free[at] = v_ready[b] = act.do(
                        nc.scalar.activation, v[s][:, t, (j // 2) * 512:(j // 2) * 512 + 512],
                        bank[:, :], ACT.Copy).mark()

        def score(n):
            b, i = divmod(n, QUADS)
            s = b % 2
            pe.wait(q_ready[b], k_ready[b])
            if n:
                pe.wait(exp_done[n - 1])
            for h in range(4):
                m, half_of = 2 * i + h // 2, h % 2
                r = slice(half_of * HEAD, (half_of + 1) * HEAD)
                pe.do(nc.tensor.matmul, scores[half_of][:, (h // 2) * 256:(h // 2) * 256 + 256],
                      qT[s][r, m, :], kT[s][r, m, :], start=True, stop=True)
            score_done[n] = pe.mark()
            if i == QUADS - 1:
                q_used[b] = score_done[n]
            dve.wait(score_done[n])
            if n >= 2:
                dve.wait(exp_done[n - 2])
            for e in range(2):
                dve.do(nc.vector.tensor_reduce, neg_max[:, n % 2, 2 * e:2 * e + 2],
                       scores[e][:, :].rearrange("p (h c) -> p h c", h=2), AX.X, ALU.max, negate=True)
            max_done[n] = dve.mark()
            act.wait(max_done[n])
            if n >= 2:
                act.wait(t_done[n - 2])
            if i == 0 and b >= 2:
                act.wait(norm_done[b - 2])
            for h in range(4):
                e = h % 2
                head = 4 * i + h
                act.do(nc.scalar.activation, prob[n % 2][:, h, :],
                       scores[e][:, (h // 2) * 256:(h // 2) * 256 + 256], ACT.Exp,
                       bias=neg_max[:, n % 2, 2 * e + h // 2:2 * e + h // 2 + 1],
                       accum_out=sums[:, s, head:head + 1])
            exp_done[n] = act.mark()

        def turn_probs(n):
            pe.wait(exp_done[n])
            for p2 in range(2):
                i = n_turn[0] % 2
                n_turn[0] += 1
                if i in turn_free:
                    pe.wait(turn_free[i])
                for h in range(2):
                    for t in range(2):
                        pe.do(nc.tensor.transpose, turned[i][:, (2 * h + t) * P:(2 * h + t + 1) * P],
                              prob[n % 2][:, 2 * p2 + h, t * P:(t + 1) * P], ident[:, :])
                t_done[n] = pe.mark()
                q, copy = ((dve, nc.vector.tensor_copy), (act, nc.scalar.copy))[p2]
                q.wait(t_done[n])
                if n >= 2:
                    q.wait(pv_done[n - 2])
                turn_free[i] = q.do(
                    copy, probT[n % 2][:, 2 * p2:2 * p2 + 2, :, :],
                    turned[i][:, :].rearrange("p (h t c) -> p h t c", h=2, t=2)).mark()
                t_copied[n, p2] = turn_free[i]

        def weigh_values(n):
            b, i = divmod(n, QUADS)
            s = b % 2
            pe.wait(t_copied[n, 0], t_copied[n, 1], v_ready[b])
            if i % 2 == 0 and (b, 1 - i // 2) in norm_done:
                pe.wait(norm_done[b, 1 - i // 2])
            if i == 0 and b:
                pe.wait(norm_done[b - 1])
            if i == 2:
                pe.wait(norm_done[b, 0])
            for h in range(4):
                head = 4 * i + h
                for t in range(2):
                    pe.do(nc.tensor.matmul, heads_out[:, (head % 8) * HEAD:(head % 8 + 1) * HEAD],
                          probT[n % 2][:, h, t, :], v[s][:, t, head * HEAD:(head + 1) * HEAD],
                          start=t == 0, stop=t == 1)
            pv_done[n] = pe.mark()
            if i % 2:
                o = i // 2
                hs = slice(8 * o, 8 * o + 8)
                dve.wait(exp_done[n])
                if o == 0 and b >= 2:
                    dve.wait(norm_done[b - 2])
                r = dve.do(nc.vector.reciprocal, inv[:, s, hs], sums[:, s, hs]).mark()
                dve.wait(r, pv_done[n])
                if b:
                    dve.wait(attT_done[b - 1, 'read'])
                norm_done[b, o] = dve.do(
                    nc.vector.tensor_tensor, att[:, 512 * o:512 * o + 512].rearrange("p (h c) -> p h c", h=8),
                    heads_out[:, :].rearrange("p (h c) -> p h c", h=8),
                    inv[:, s, hs].unsqueeze(2).broadcast_to([P, 8, HEAD]), ALU.mult).mark()
                if o:
                    norm_done[b] = norm_done[b, 1]
                    v_used[b] = pv_done[n]

        def turn_heads(b):
            pe.wait(norm_done[b])
            for o in range(2):
                at, bank = take_proj()
                for m in range(4):
                    pe.do(nc.tensor.transpose, bank[:, m * P:(m + 1) * P],
                          att[:, (4 * o + m) * P:(4 * o + m + 1) * P], ident[:, :])
                attT_done[b, 'read'] = pe.mark()
                q, copy = ((dve, nc.vector.tensor_copy), (act, nc.scalar.copy))[o]
                q.wait(attT_done[b, 'read'])
                if b:
                    q.wait(added[b - 1, 'mm'])
                proj_free[at] = attT_done[b, o] = q.do(
                    copy, attT[:, 4 * o:4 * o + 4, :],
                    bank[:, :].rearrange("p (m t) -> p m t", m=4)).mark()

        def output(b):
            pe.wait(attT_done[b, 0], attT_done[b, 1], w_in)
            at, bank = take_proj()
            for m in range(INNER // P):
                pe.do(nc.tensor.matmul, bank[:, 0:DIM], attT[:, m, :], wo_sb[:, m, :],
                      start=m == 0, stop=m == INNER // P - 1)
            added[b, 'mm'] = pe.mark()
            dve.wait(added[b, 'mm'])
            proj_free[at] = dve.do(nc.vector.tensor_tensor, x_all[:, b, :], x_all[:, b, :],
                                   bank[:, 0:DIM], ALU.add).mark()

        norm_pair(0)
        norm_pair(2)
        turn_inputs(0)
        for part in range(4):
            project(0, part)
        turn_inputs(1)
        last = SEQS * QUADS
        for n in range(last + 6):
            b, i = divmod(n, QUADS)
            if n < last:
                score(n)
            if b + 1 < SEQS:
                project(b + 1, i)
            if 1 <= n <= last:
                turn_probs(n - 1)
            if i == 0 and b % 2 == 0 and b + 4 < SEQS:
                norm_pair(b + 4)
            if i == 3 and b + 2 < SEQS:
                turn_inputs(b + 2)
            if 2 <= n <= last + 1:
                weigh_values(n - 2)
            if i == 2 and 1 <= b <= SEQS:
                turn_heads(b - 1)
            if i == 3 and 1 <= b <= SEQS:
                output(b - 1)
        if (SEQS - 1) not in [k for k in added if isinstance(k, int)] and (SEQS - 1, 'mm') not in added:
            if (SEQS - 1, 'read') not in attT_done:
                turn_heads(SEQS - 1)
            output(SEQS - 1)


def experts(nc, x_all, ident, half, router, bias, gate, up, down, s_gate, s_up, s_down):
    TILES = ROUTED // P
    STILES = SHARED // P
    with Stage(nc, "experts") as st:
        pe, act, dve, pool, sp = st.pe, st.act, st.dve, st.pool, st.sp
        gate_w = [st.sb(f"gate_{n}", [P, KD, ROUTED + SHARED], F32R) for n in ("hi", "lo")]
        up_w = [st.sb(f"up_{n}", [P, KD, ROUTED + SHARED], F32R) for n in ("hi", "lo")]
        down_w = st.sb("down", [P, TILES + STILES, DIM])
        router_w = st.sb("router", [P, KD, EXPERTS])
        bias_w = st.sb("bias", [P, EXPERTS])
        below = st.sb("below", [P, EXPERTS, EXPERTS])
        xn = st.sb("xn", [P, GB, DIM])
        raw = st.sb("raw_stats", [P, GB, 6])
        mv = st.sb("mean_var", [P, GB, 2])
        var_eps = st.sb("var_eps", [P, GB])
        rstd = st.sb("rstd", [P, GB])
        xT = st.sb("xT", [P, KD, GB * TOK])
        xT_hi = [st.sb(f"xT_hi{i}", [P, KD, GB * TOK], F32R) for i in range(2)]
        xT_lo = [st.sb(f"xT_lo{i}", [P, KD, GB * TOK], F32R) for i in range(2)]
        comb_x = st.sb("comb_spread", [P, GB, EXPERTS, HID])
        silu = [st.sb(f"silu{i}", [P, GB * TOK]) for i in range(2)]
        hid = [st.sb(f"hidden{i}", [P, GB * TOK]) for i in range(3)]
        sc, sb_, tmp = (st.sb(n, [P, GB, EXPERTS]) for n in ("score", "biased", "small"))
        pq = st.sb("pair", [P, 2, GB * GROUPS, 2])
        tops = st.sb("tops", [P, 4, GB * GROUPS])
        gs = st.sb("group_score", [P, GB, GROUPS])
        gcmp = st.sb("group_compare", [P, 2, GB, GROUPS, GROUPS])
        gmask = st.sb("group_mask", [P, GB, GROUPS])
        gneg = st.sb("group_neg", [P, GB, GROUPS])
        masked = st.sb("masked", [P, GB, EXPERTS])
        cmp_ge = st.sb("compare_ge", [P, GB, EXPERTS, EXPERTS], BF16)
        cmp_gt = st.sb("compare_gt", [P, GB, EXPERTS, EXPERTS], BF16)
        rank = st.sb("rank", [P, GB, EXPERTS])
        comb = st.sb("combine", [P, GB, EXPERTS])
        wsum = st.sb("weight_sum", [P, 2, GB])
        misc = st.bank("misc")
        g_ps = [st.bank(f"gate{i}") for i in range(2)]
        u_ps = [st.bank(f"up{i}") for i in range(2)]
        c_ps = st.bank("combine_turned")
        out_ps = [st.bank(f"out{i}") for i in range(2)]

        w_lane = st.lane("weight_load")
        for src, dst in ((down.rearrange("(m p) n -> p m n", p=P), down_w[:, 0:TILES, :]),
                         (s_down.rearrange("(m p) n -> p m n", p=P), down_w[:, TILES:, :]),
                         (router.rearrange("(k p) n -> p k n", p=P), router_w[:, :, :]), (bias, bias_w[:, :])):
            w_in = sp.dma(nc.sync.dma_start, w_lane, dst, src)
        ones = pool.do(nc.gpsimd.memset, below[:, :, :], 1.0).mark()
        pool.wait(ones)
        const = pool.do(nc.gpsimd.affine_select, out=below[:, :, :], in_=below[:, :, :],
                        compare_op=ALU.is_gt, fill=0.0, base=0, pattern=[[1, EXPERTS], [-1, EXPERTS]],
                        channel_multiplier=0).mark()
        stage_lane = [st.lane(f"stage_load{i}") for i in range(4)]
        stage = comb_x[:, :, :, :].rearrange("p b e h -> p (b e h)")
        staged = []
        for src, (hi, lo), at, width in ((gate, gate_w, 0, ROUTED), (up, up_w, 0, ROUTED),
                                         (s_gate, gate_w, ROUTED, SHARED), (s_up, up_w, ROUTED, SHARED)):
            for k in range(KD):
                n = len(staged)
                s = (n % 4) * 1024
                w = slice(at, at + width)
                staged.append(split_weight(st, stage_lane[n % 4], stage[:, s:s + width],
                                           staged[n - 4:n - 3] if n >= 4 else (),
                                           src[k * P:(k + 1) * P, :], hi[:, k, w], lo[:, k, w], width))
        w_split = staged[-1]
        stage_free = w_split

        normed, turned, x_ready, routed, spread = {}, {}, {}, {}, {}
        misc_free = [None]
        full_read = {}
        x_used, xn_used, comb_read, out_added = {}, {}, {}, {}

        def norm(g):
            xs = [x_all[:, GB * g + i, :] for i in range(GB)]
            got = stats(st, xs, raw, mv)
            r = rsqrt_var(st, mv, var_eps[:, :], rstd[:, :], half, GB, (got,))
            if g:
                dve.wait(xn_used[g - 1])
            normed[g] = normalise(st, [xn[:, i, :] for i in range(GB)], xs, mv, rstd, (r,))

        def turn(g):
            s = g % 2
            pe.wait(normed[g])
            for k in range(KD):
                if misc_free[0]:
                    pe.wait(misc_free[0])
                for i in range(GB):
                    pe.do(nc.tensor.transpose, misc[:, i * P:(i + 1) * P], xn[:, i, k * P:(k + 1) * P], ident[:, :])
                xn_used[g] = pe.mark()
                act.wait(xn_used[g])
                if g:
                    act.wait(full_read[g - 1], x_ready[g - 1])
                misc_free[0] = full = act.do(nc.scalar.copy, xT[:, k, :], misc[:, :]).mark()
            act.wait(full)
            if g >= 2:
                act.wait(x_used[g - 2])
            high = act.do(nc.scalar.activation, xT_hi[s][:, :, :], xT[:, :, :], ACT.Copy).mark()
            pool.wait(high)
            x_ready[g] = pool.do(nc.gpsimd.tensor_tensor, xT_lo[s][:, :, :], xT[:, :, :],
                                 xT_hi[s][:, :, :].bitcast(F32), ALU.subtract).mark()
            pe.wait(full, w_in)
            for i in range(GB):
                for k in range(KD):
                    pe.do(nc.tensor.matmul, misc[:, i * EXPERTS:(i + 1) * EXPERTS],
                          xT[:, k, i * TOK:(i + 1) * TOK], router_w[:, k, :], start=k == 0, stop=k == KD - 1)
            full_read[g] = pe.mark()
            act.wait(full_read[g])
            if g:
                act.wait(routed[g - 1])
            misc_free[0] = act.do(nc.scalar.activation, tmp[:, :, :],
                                  misc[:, 0:GB * EXPERTS].rearrange("p (b e) -> p b e", b=GB),
                                  ACT.Tanh, scale=0.5).mark()

        def chain(build, *a, **k):
            done = dve.do(build, *a, **k).mark()
            dve.wait(done)
            return done

        def route(g):
            V = nc.vector
            tt, ts = V.tensor_tensor, V.tensor_scalar
            dve.wait(misc_free[0], w_in, const)
            if g:
                dve.wait(spread[g - 1])
            chain(ts, sc[:, :, :], tmp[:, :, :], 0.5, 0.5, ALU.mult, ALU.add)
            chain(tt, sb_[:, :, :], sc[:, :, :], bias_w[:, :].unsqueeze(1).broadcast_to([P, GB, EXPERTS]), ALU.add)
            quad = sb_[:, :, :].rearrange("p b (g a c) -> p (b g) a c", g=GROUPS, a=2)
            dve.do(tt, pq[:, 0, :, :], quad[:, :, :, 0], quad[:, :, :, 1], ALU.max)
            chain(tt, pq[:, 1, :, :], quad[:, :, :, 0], quad[:, :, :, 1], ALU.min)
            dve.do(tt, tops[:, 0, :], pq[:, 0, :, 0], pq[:, 0, :, 1], ALU.max)
            dve.do(tt, tops[:, 1, :], pq[:, 0, :, 0], pq[:, 0, :, 1], ALU.min)
            chain(tt, tops[:, 2, :], pq[:, 1, :, 0], pq[:, 1, :, 1], ALU.max)
            chain(tt, tops[:, 3, :], tops[:, 1, :], tops[:, 2, :], ALU.max)
            chain(tt, gs[:, :, :].rearrange("p b g -> p (b g)"), tops[:, 0, :], tops[:, 3, :], ALU.add)

            def ranks(value, n, ge, gt, out):
                for i in range(GB):
                    e = value[:, i, :].unsqueeze(2).broadcast_to([P, n, n])
                    j = value[:, i, :].unsqueeze(1).broadcast_to([P, n, n])
                    dve.do(tt, ge[:, i], j, e, ALU.is_ge)
                    last = dve.do(tt, gt[:, i], j, e, ALU.is_gt)
                last = dve.mark()
                dve.wait(last)
                for i in range(GB):
                    dve.do(tt, ge[:, i], ge[:, i], below[:, 0:n, 0:n], ALU.mult)
                last = dve.mark()
                dve.wait(last)
                chain(tt, ge, ge, gt, ALU.max)
                chain(V.tensor_reduce, out, ge, AX.X, ALU.add)

            ranks(gs[:, :, :], GROUPS, gcmp[:, 0], gcmp[:, 1], gmask[:, :, :])
            chain(ts, gmask[:, :, :], gmask[:, :, :], PICK_GROUPS - 0.5, None, ALU.is_lt)
            chain(ts, gneg[:, :, :], gmask[:, :, :], 1.0, BIG, ALU.subtract, ALU.mult)
            g4 = lambda t: t[:, :, :].rearrange("p b g -> p (b g)").unsqueeze(2).broadcast_to(
                [P, GB * GROUPS, EXPERTS // GROUPS])
            flat = lambda t: t[:, :, :].rearrange("p b (g c) -> p (b g) c", g=GROUPS)
            chain(tt, flat(masked), flat(sb_), g4(gmask), ALU.mult)
            chain(tt, flat(masked), flat(masked), g4(gneg), ALU.add)
            ranks(masked[:, :, :], EXPERTS, cmp_ge[:, :], cmp_gt[:, :], rank[:, :, :])
            chain(ts, rank[:, :, :], rank[:, :, :], PICK - 0.5, None, ALU.is_lt)
            chain(tt, comb[:, :, :], sc[:, :, :], rank[:, :, :], ALU.mult)
            chain(V.tensor_reduce, wsum[:, 0, :], comb[:, :, :], AX.X, ALU.add)
            chain(ts, wsum[:, 0, :], wsum[:, 0, :], 1e-20, None, ALU.add)
            chain(V.reciprocal, wsum[:, 1, :], wsum[:, 0, :])
            routed[g] = chain(tt, comb[:, :, :], comb[:, :, :],
                              wsum[:, 1, :].unsqueeze(2).broadcast_to([P, GB, EXPERTS]), ALU.mult)

        def spread_weights(g):
            pool.wait(routed[g], stage_free)
            if g:
                pool.wait(comb_read[g - 1])
            for i in range(GB):
                pool.do(nc.gpsimd.tensor_copy, comb_x[:, i, :, :],
                        comb[:, i, :].unsqueeze(2).broadcast_to([P, EXPERTS, HID]))
            spread[g] = pool.mark()

        units = []
        hid_ready, hid_used, gate_read, up_read, turn_read, silu_read = {}, {}, {}, {}, {}, {}
        order = list(range(TILES, TILES + STILES)) + list(range(TILES))

        def up_gate(n):
            g, t = divmod(n, TILES + STILES)
            m = order[t]
            s, r = n % 2, g % 2
            w = slice(m * P, (m + 1) * P)
            pe.wait(x_ready[g], w_split)
            for ps, (hi, lo), read in ((g_ps[s], gate_w, gate_read), (u_ps[s], up_w, up_read)):
                if n >= 2:
                    pe.wait(read[n - 2])
                step = 0
                for k in range(KD):
                    for l, x_ in ((hi, xT_hi[r]), (hi, xT_lo[r]), (lo, xT_hi[r])):
                        pe.do(nc.tensor.matmul, ps[:, :], l[:, k, w], x_[:, k, :], start=step == 0,
                              stop=step == 3 * KD - 1)
                        step += 1
                made = pe.mark()
                if ps is g_ps[s]:
                    act.wait(made)
                    if n >= 2:
                        act.wait(silu_read[n - 2])
                    gate_read[n] = act.do(nc.scalar.activation, silu[s][:, :], ps[:, :], ACT.Silu).mark()
            if t == TILES + STILES - 1:
                x_used[g] = made
            if m < TILES:
                pe.wait(spread[g])
                if turn_read:
                    pe.wait(turn_read['last'])
                for i in range(GB):
                    pe.do(nc.tensor.transpose, c_ps[:, i * TOK:(i + 1) * TOK],
                          comb_x[:, i, 2 * m:2 * m + 2, :].rearrange("p e h -> p (e h)"), ident[:, :])
                c_made = comb_read[g] = pe.mark()
            dve.wait(made, gate_read[n])
            if n >= 3:
                dve.wait(hid_used[n - 3])
            h = hid[n % 3]
            up_read[n] = silu_read[n] = hid_ready[n] = dve.do(
                nc.vector.tensor_tensor, h[:, :], silu[s][:, :], u_ps[s][:, :], ALU.mult).mark()
            if m < TILES:
                dve.wait(c_made, hid_ready[n])
                hid_ready[n] = turn_read['last'] = dve.do(
                    nc.vector.tensor_tensor, h[:, :], h[:, :], c_ps[:, :], ALU.mult).mark()

        def down_proj(n):
            g, t = divmod(n, TILES + STILES)
            m = order[t]
            pe.wait(hid_ready[n], w_in)
            if t == 0 and g:
                pe.wait(out_added[g - 1])
            for i in range(GB):
                pe.do(nc.tensor.matmul, out_ps[i // 2][:, (i % 2) * DIM:(i % 2 + 1) * DIM],
                      hid[n % 3][:, i * TOK:(i + 1) * TOK], down_w[:, m, :],
                      start=t == 0 and i % 2 == 0, stop=t == TILES + STILES - 1, skip_group_check=True)
            hid_used[n] = pe.mark()
            if t == TILES + STILES - 1:
                dve.wait(hid_used[n])
                for i in range(2):
                    xs = x_all[:, GB * g + 2 * i:GB * g + 2 * i + 2, :].rearrange("p b d -> p (b d)")
                    dve.do(nc.vector.tensor_tensor, xs, xs, out_ps[i][:, :], ALU.add)
                out_added[g] = dve.mark()

        per = TILES + STILES
        norm(0)
        turn(0)
        route(0)
        spread_weights(0)
        for n in range(NG * per + 1):
            g, t = divmod(n, per)
            if n < NG * per:
                up_gate(n)
            if n:
                down_proj(n - 1)
            if g + 1 < NG:
                if t == 1:
                    norm(g + 1)
                if t == 3:
                    turn(g + 1)
                if t == 5:
                    route(g + 1)
                if t == per - 1:
                    spread_weights(g + 1)


def distances(nc, x_all, ident, half, ctx, ctxT, dist):
    with Stage(nc, "distance") as st:
        pe, act, dve, pool, sp = st.pe, st.act, st.dve, st.pool, st.sp
        ctx_sb = [st.sb(f"ctx{i}", [P, GB, DIM]) for i in range(2)]
        cT = [st.sb(f"ctxT{i}", [P, KD, GB, TOK]) for i in range(2)]
        junk = st.sb("squares", [P, DIM])
        aa = [st.sb(f"ctx_norm{i}", [P, GB]) for i in range(2)]
        xn = st.sb("xn", [P, GB, DIM])
        raw = st.sb("raw_stats", [P, GB, 6])
        mv = st.sb("mean_var", [P, GB, 2])
        var_eps = st.sb("var_eps", [P, GB])
        rstd = st.sb("rstd", [P, GB])
        xT = [st.sb(f"xT{i}", [P, KD, GB * TOK]) for i in range(2)]
        xT2 = [st.sb(f"xT_square{i}", [P, KD, GB * TOK]) for i in range(2)]
        ones = st.sb("ones", [P, P])
        sq = [st.sb(f"squared_dist{i}", [P, GB, TOK]) for i in range(2)]
        dt_ = [st.sb(f"dist{i}", [P, GB, TOK]) for i in range(2)]
        turned = [st.bank(f"turned{i}") for i in range(2)]
        d_ps = [st.bank(f"dist_ps{i}") for i in range(2)]
        load = [st.lane(f"ctx_load{i}") for i in range(2)]
        store = [st.lane(f"dist_store{i}") for i in range(2)]
        const = pool.do(nc.gpsimd.memset, ones[:, :], 1.0).mark()
        landed, normed, turn_copied, x_turned, xs_ready, made = {}, {}, {}, {}, {}, {}
        scaled, aa_done, clamp, rooted, stored, sqd = {}, {}, {}, {}, {}, {}

        def fetch(g):
            s = g % 2
            if g >= 2:
                sp.wait(made[g - 2], aa_done[g - 2])
            sp.dma(nc.sync.dma_start, load[s], ctx_sb[s][:, :, :],
                   ctx[GB * g:GB * g + GB].rearrange("b t d -> t b d"))
            for k in range(KD):
                landed[g] = sp.dma(nc.sync.dma_start, load[s], cT[s][:, k, :, :],
                                   ctxT[GB * g:GB * g + GB, k * P:(k + 1) * P, :].rearrange("b p t -> p b t"))
            xs = [x_all[:, GB * g + i, :] for i in range(GB)]
            got = stats(st, xs, raw, mv)
            r = rsqrt_var(st, mv, var_eps[:, :], rstd[:, :], half, GB, (got,))
            if g:
                dve.wait(x_turned[g - 1])
            normed[g] = normalise(st, [xn[:, i, :] for i in range(GB)], xs, mv, rstd, (r,))

        def turn(g):
            s = g % 2
            for k in range(KD):
                pe.wait(normed[g])
                if g:
                    pe.wait(sqd[g - 1, k])
                for i in range(GB):
                    pe.do(nc.tensor.transpose, turned[k][:, i * P:(i + 1) * P], xn[:, i, k * P:(k + 1) * P],
                          ident[:, :])
                x_turned[g] = pe.mark()
                dve.wait(x_turned[g])
                act.wait(x_turned[g])
                if g >= 2:
                    dve.wait(made[g - 2])
                    act.wait(made[g - 2])
                turn_copied[g, k] = dve.do(nc.vector.tensor_scalar, xT[s][:, k, :], turned[k][:, :], -2.0,
                                           None, ALU.mult).mark()
                act.wait(turn_copied[g, k])
                sqd[g, k] = act.do(nc.scalar.activation, xT2[s][:, k, :], turned[k][:, :], ACT.Square).mark()
            act.wait(landed[g])
            if g >= 2:
                act.wait(clamp[g - 2])
            for i in range(GB):
                act.do(nc.scalar.activation, junk[:, :], ctx_sb[s][:, i, :], ACT.Square,
                       accum_out=aa[s][:, i:i + 1])
                aa_done[g] = act.mark()
                act.wait(aa_done[g])

        def multiply(g):
            s = g % 2
            pe.wait(landed[g], turn_copied[g, 0], turn_copied[g, 1], sqd[g, 0], sqd[g, 1], const)
            if g >= 2:
                pe.wait(clamp[g - 2])
            for i in range(GB):
                cols = slice(i * TOK, (i + 1) * TOK)
                for k in range(KD):
                    pe.do(nc.tensor.matmul, d_ps[s][:, cols], ones[:, :], xT2[s][:, k, cols],
                          start=k == 0, stop=False)
                for k in range(KD):
                    pe.do(nc.tensor.matmul, d_ps[s][:, cols], cT[s][:, k, i, :], xT[s][:, k, cols],
                          start=False, stop=k == KD - 1)
            made[g] = pe.mark()
            dve.wait(made[g], aa_done[g])
            if g >= 2:
                dve.wait(rooted[g - 2])
            for i in range(GB):
                dve.do(nc.vector.tensor_scalar, sq[s][:, i, :], d_ps[s][:, i * TOK:(i + 1) * TOK],
                       aa[s][:, i:i + 1], 0.0, ALU.add, ALU.max)
            clamp[g] = dve.mark()
            act.wait(clamp[g])
            if g >= 2:
                act.wait(stored[g - 2])
            rooted[g] = act.do(nc.scalar.activation, dt_[s][:, :, :], sq[s][:, :, :], ACT.Sqrt).mark()
            sp.wait(rooted[g])
            stored[g] = sp.dma(nc.sync.dma_start, store[s],
                               dist[GB * g:GB * g + GB].rearrange("b i j -> i b j"), dt_[s][:, :, :])

        pipeline(NG, fetch, turn, multiply)
        sp.wait(*stored.values())


def align(nc, dist, path):
    N, CH = TOK, 16
    with Stage(nc, "align") as st:
        dve, pool, sp, act = st.dve, st.pool, st.sp, st.act
        cost = st.sb("cost", [SEQS, N + 1, N + 1])
        best = [st.sb(f"best{i}", [SEQS, N]) for i in range(2)]
        first = st.sb("first", [SEQS, N])
        load = [st.lane(f"dist_load{i}") for i in range(N // CH)]
        store = [st.lane(f"path_store{i}") for i in range(2)]
        landed = []
        for c in range(N // CH):
            landed.append(sp.dma(nc.sync.dma_start, load[c], cost[:, 1 + c * CH:1 + (c + 1) * CH, 1:],
                                 dist[:, c * CH:(c + 1) * CH, :]))
        V = nc.vector
        pool.do(nc.gpsimd.memset, cost[:, :, 0:1], BIG)
        pool.do(nc.gpsimd.memset, cost[:, 0, 1:], BIG)
        pool.do(nc.gpsimd.memset, first[:, :], BIG)
        edges = pool.mark()
        pool.wait(edges)
        edges = pool.do(nc.gpsimd.memset, first[:, 0:1], 0.0).mark()
        dve.wait(edges)
        row = None
        for i in range(N):
            if i % CH == 0:
                dve.wait(landed[i // CH])
            if i:
                dve.wait(row)
                b = best[i % 2]
                up = dve.do(V.tensor_tensor, b[:, :], cost[:, i, 1:], cost[:, i, 0:N], ALU.min).mark()
                dve.wait(up)
            else:
                b = first
            row = dve.do(V.tensor_tensor_scan, cost[:, i + 1, 1:], b[:, :], cost[:, i + 1, 1:], BIG,
                         ALU.min, ALU.add).mark()
        dve.wait(row)

        lesser = st.sb("lesser", [SEQS, CH, N])
        left = [st.sb(f"left{i}", [SEQS, CH, N + 1], BF16) for i in range(2)]
        leave = [st.sb(f"leave{i}", [SEQS, CH, 2, N], BF16) for i in range(2)]
        on_path = [st.sb(f"on_path{i}", [SEQS, CH, N]) for i in range(2)]
        enter = st.sb("enter", [SEQS, N])
        moved = st.sb("moved", [SEQS, 2, N + 1])
        for i in range(2):
            pool.do(nc.gpsimd.memset, left[i][:, :, N:], 0.0)
        pool.do(nc.gpsimd.memset, moved[:, :, :], 0.0)
        zero = pool.do(nc.gpsimd.memset, enter[:, :], 0.0).mark()
        pool.wait(zero)
        start = pool.do(nc.gpsimd.memset, enter[:, N - 1:], 1.0).mark()
        dve.wait(start)
        stored = {}
        for c in reversed(range(N // CH)):
            s = c % 2
            above = cost[:, c * CH:c * CH + CH, :]
            here = cost[:, c * CH + 1:c * CH + CH + 1, :]
            go_left, out = left[s][:, :, 0:N], leave[s]
            done = dve.do(V.tensor_tensor, lesser[:, :, :], above[:, :, 1:], above[:, :, 0:N], ALU.min).mark()
            dve.wait(done)
            if c == 0:
                done = dve.do(V.tensor_copy, lesser[:, 0, :], first[:, :]).mark()
                dve.wait(done)
            dve.do(V.tensor_tensor, go_left, here[:, :, 0:N], lesser[:, :, :], ALU.is_lt)
            done = dve.do(V.tensor_tensor, out[:, :, 1, :], above[:, :, 0:N], above[:, :, 1:], ALU.is_le).mark()
            dve.wait(done)
            done = dve.do(V.tensor_scalar, out[:, :, 0, :], go_left, -1.0, 1.0, ALU.mult, ALU.add).mark()
            dve.wait(done)
            done = dve.do(V.tensor_tensor, out[:, :, 1, :], out[:, :, 1, :], out[:, :, 0, :], ALU.mult).mark()
            dve.wait(done)
            done = dve.do(V.tensor_tensor, out[:, :, 0, :], out[:, :, 0, :], out[:, :, 1, :],
                          ALU.subtract).mark()
            dve.wait(done)
            if c + 2 in stored:
                dve.wait(stored[c + 2])
            for r in reversed(range(CH)):
                cells = on_path[s][:, r, :]
                done = dve.do(V.tensor_tensor_scan, cells[:, ::-1], left[s][:, r, 1:][:, ::-1],
                              enter[:, ::-1], 0.0, ALU.mult, ALU.add).mark()
                dve.wait(done)
                if c == 0 and r == 0:
                    break
                done = dve.do(V.tensor_tensor, moved[:, :, 0:N], cells.unsqueeze(1).broadcast_to([SEQS, 2, N]),
                              out[:, r, :, :], ALU.mult).mark()
                dve.wait(done)
                done = dve.do(V.tensor_tensor, enter[:, :], moved[:, 0, 0:N], moved[:, 1, 1:], ALU.add).mark()
                dve.wait(done)
            sp.wait(done)
            stored[c] = sp.dma(nc.sync.dma_start, store[s], path[:, c * CH:(c + 1) * CH, :], on_path[s][:, :, :])
        sp.wait(*stored.values())


def conv_ffn(nc, x_all, ident, half, ctx, path, w1T, w2T, conv_w, conv_b, out):
    TILES = CONV_HID // P
    with Stage(nc, "conv") as st:
        pe, act, dve, pool, sp = st.pe, st.act, st.dve, st.pool, st.sp
        w1q = st.sb("w1_ternary", [P, KD, CONV_HID], BF16)
        w2q = st.sb("w2_ternary", [P, TILES, DIM], BF16)
        w_sb = st.sb("w_stage", [P, 2, KD * CONV_HID])
        absum = st.sb("abs_sum", [P, 2])
        w_mean = st.sb("w_mean", [P, 2])
        w_inv = st.sb("w_inv", [P, 2])
        ones = st.sb("ones", [P, P])
        ident_b = st.sb("ident_bf16", [P, P], BF16)
        cw = st.sb("conv_w", [P, TILES, 3])
        cb = st.sb("conv_b", [P, TILES])
        ctx_sb = [st.sb(f"ctx{i}", [P, GB, DIM]) for i in range(2)]
        path_sb = [st.sb(f"path{i}", [P, GB, TOK]) for i in range(2)]
        raw = st.sb("raw_stats", [P, GB, 6])
        mv = st.sb("mean_var", [P, GB, 2])
        var_eps = st.sb("var_eps", [P, GB])
        rstd = st.sb("rstd", [P, GB])
        xn = st.sb("xn", [P, GB, DIM])
        xq = st.sb("xq", [P, GB, DIM], BF16)
        amax = st.sb("x_absmax", [P, GB])
        inv1 = st.sb("x_inv", [P, GB])
        q1 = st.sb("x_scale", [P, GB])
        xqT = [st.sb(f"xqT{i}", [P, KD, GB * TOK], BF16) for i in range(2)]
        inv1_b = [st.sb(f"x_inv_b{i}", [P, GB * TOK]) for i in range(2)]
        h = [st.sb(f"h{i}", [P, GB, TOK]) for i in range(2)]
        acc = [st.sb(f"acc{i}", [P, GB, TOK]) for i in range(2)]
        act_h = [st.sb(f"act_h{i}", [P, TILES, GB * TOK]) for i in range(2)]
        hmax = st.sb("h_absmax_part", [P, GB * TOK])
        amax2 = st.sb("h_absmax", [P, GB])
        inv2 = [st.sb(f"h_inv{i}", [P, GB]) for i in range(2)]
        q2 = st.sb("h_scale", [P, GB])
        q2_b = st.sb("h_scale_b", [P, GB * TOK])
        hq = st.sb("hq", [P, TILES, GB * TOK], BF16)
        x_out = [st.sb(f"x_out{i}", [P, GB, DIM]) for i in range(2)]
        ex_ps = st.bank("expand")
        t_ps = st.bank("turned", BF16)
        b_ps = st.bank("broadcast")
        h_ps = [st.bank(f"h_ps{i}") for i in range(3)]
        o_ps = [st.bank(f"out_ps{i}") for i in range(2)]

        w_lane = st.lane("weight_load")
        sp.dma(nc.sync.dma_start, w_lane, w_sb[:, 0, :].rearrange("p (k n) -> p k n", k=KD),
               w1T.rearrange("(k p) n -> p k n", p=P))
        sp.dma(nc.sync.dma_start, w_lane, w_sb[:, 1, :].rearrange("p (m n) -> p m n", m=TILES),
               w2T.rearrange("(m p) n -> p m n", p=P))
        sp.dma(nc.sync.dma_start, w_lane, cw[:, :, :], conv_w)
        w_in = sp.dma(nc.sync.dma_start, w_lane, cb[:, :], conv_b)
        pool.do(nc.gpsimd.memset, ones[:, :], 1.0)
        const = pool.do(nc.gpsimd.tensor_copy, ident_b[:, :], ident[:, :]).mark()
        dve.wait(w_in)
        for n in range(2):
            dve.do(nc.vector.tensor_reduce, absum[:, n:n + 1], w_sb[:, n, :], AX.X, ALU.add,
                   apply_absolute_value=True)
        summed = dve.mark()
        pe.wait(summed, const)
        total = pe.do(nc.tensor.matmul, b_ps[:, 0:2], ones[:, :], absum[:, :], start=True, stop=True).mark()
        dve.wait(total)
        mean = dve.do(nc.vector.tensor_scalar, w_mean[:, :], b_ps[:, 0:2], 1.0 / (DIM * CONV_HID), 1e-5,
                      ALU.mult, ALU.max).mark()
        b_free = [mean]
        dve.wait(mean)
        r = dve.do(nc.vector.reciprocal, w_inv[:, :], w_mean[:, :]).mark()
        dve.wait(r)
        for n, dst in enumerate((w1q[:, :, :].rearrange("p k n -> p (k n)"),
                                 w2q[:, :, :].rearrange("p m n -> p (m n)"))):
            w = w_sb[:, n, :]
            r = dve.do(nc.vector.tensor_scalar, w, w, w_inv[:, n:n + 1], ROUND, ALU.mult, ALU.add).mark()
            dve.wait(r)
            r = dve.do(nc.vector.tensor_scalar, w, w, ROUND, 1.0, ALU.subtract, ALU.min).mark()
            dve.wait(r)
            w_quant = dve.do(nc.vector.tensor_scalar, dst, w, -1.0, None, ALU.max).mark()

        load = [st.lane(f"load{i}") for i in range(2)]
        store = [st.lane(f"store{i}") for i in range(2)]
        landed, expanded, x_added, quantised, xq_turned, xq_ready, bc1 = {}, {}, {}, {}, {}, {}, {}
        xn_norm, inv1_ready = {}, {}
        t_free = [None]
        made, h_read, conv_done, silu_done, x_used = {}, {}, {}, {}, {}
        maxed, max_turned, q2_ready, hq_ready, out_made, finished, stored = {}, {}, {}, {}, {}, {}, {}
        hmax_read, q2b_ready, inv2_ready = {}, {}, {}

        def expand(g):
            s = g % 2
            if g >= 2:
                sp.wait(expanded[g - 2])
            sp.dma(nc.sync.dma_start, load[s], ctx_sb[s][:, :, :],
                   ctx[GB * g:GB * g + GB].rearrange("b t d -> t b d"))
            landed[g] = sp.dma(nc.sync.dma_start, load[s], path_sb[s][:, :, :],
                               path[GB * g:GB * g + GB].rearrange("b i j -> i b j"))
            pe.wait(landed[g])
            for p2 in range(2):
                if (g, p2) != (0, 0):
                    pe.wait(x_added['last'])
                for i in range(2):
                    pe.do(nc.tensor.matmul, ex_ps[:, i * DIM:(i + 1) * DIM], path_sb[s][:, 2 * p2 + i, :],
                          ctx_sb[s][:, 2 * p2 + i, :], start=True, stop=True)
                expanded[g] = pe.mark()
                dve.wait(expanded[g])
                xs = x_all[:, GB * g + 2 * p2:GB * g + 2 * p2 + 2, :].rearrange("p b d -> p (b d)")
                x_added['last'] = dve.do(nc.vector.tensor_tensor, xs, xs, ex_ps[:, :], ALU.add).mark()
            x_added[g] = x_added['last']

        def quantise(g):
            xs = [x_all[:, GB * g + i, :] for i in range(GB)]
            V = nc.vector
            dve.wait(x_added[g])
            got = stats(st, xs, raw, mv)
            r = rsqrt_var(st, mv, var_eps[:, :], rstd[:, :], half, GB, (got,))
            one = normalise(st, [xn[:, i, :] for i in range(GB)], xs, mv, rstd, (r,))
            dve.wait(one)
            if g:
                dve.wait(inv1_ready[g - 1])
            r = dve.do(V.tensor_reduce, amax[:, :], xn[:, :, :], AX.X, ALU.max, apply_absolute_value=True).mark()
            dve.wait(r)
            r = dve.do(V.tensor_scalar, inv1[:, :], amax[:, :], 1e-5, 1.0 / 127.0, ALU.max, ALU.mult).mark()
            xn_norm[g] = r
            dve.wait(r)
            r = dve.do(V.reciprocal, q1[:, :], inv1[:, :]).mark()
            dve.wait(r)
            for i in range(GB):
                dve.do(V.tensor_scalar, xn[:, i, :], xn[:, i, :], q1[:, i:i + 1], ROUND, ALU.mult, ALU.add)
            r = dve.mark()
            dve.wait(r)
            if g:
                dve.wait(xq_turned[g - 1])
            quantised[g] = dve.do(V.tensor_scalar, xq[:, :, :], xn[:, :, :], ROUND, 127.0,
                                  ALU.subtract, ALU.min).mark()

        def turn(g):
            s = g % 2
            pe.wait(quantised[g], const)
            if t_free[0]:
                pe.wait(t_free[0])
            for k in range(KD):
                for i in range(GB):
                    pe.do(nc.tensor.transpose, t_ps[:, (k * GB + i) * P:(k * GB + i + 1) * P],
                          xq[:, i, k * P:(k + 1) * P], ident_b[:, :])
            xq_turned[g] = pe.mark()
            act.wait(xq_turned[g])
            if g >= 2:
                act.wait(x_used[g - 2])
            t_free[0] = xq_ready[g] = act.do(nc.scalar.copy, xqT[s][:, :, :],
                                             t_ps[:, :].rearrange("p (k t) -> p k t", k=KD)).mark()
            pe.wait(xn_norm[g], b_free[0])
            for i in range(GB):
                pe.do(nc.tensor.transpose, b_ps[:, i * TOK:(i + 1) * TOK],
                      inv1[:, i:i + 1].broadcast_to([P, P]), ident[:, :])
            inv1_ready[g] = pe.mark()
            act.wait(inv1_ready[g], mean)
            if g >= 2:
                act.wait(h_read[(g - 2) * TILES + TILES - 1])
            b_free[0] = bc1[g] = act.do(nc.scalar.activation, inv1_b[s][:, :], b_ps[:, :], ACT.Copy,
                                        scale=w_mean[:, 0:1]).mark()

        def hidden(n):
            g, m = divmod(n, TILES)
            s, r = g % 2, n % 2
            ps = h_ps[n % 3]
            pe.wait(xq_ready[g], w_quant)
            if n >= 3:
                pe.wait(h_read[n - 3])
            for k in range(KD):
                pe.do(nc.tensor.matmul, ps[:, :], w1q[:, k, m * P:(m + 1) * P], xqT[s][:, k, :],
                      start=k == 0, stop=k == KD - 1)
            made[n] = pe.mark()
            if m == TILES - 1:
                x_used[g] = made[n]
            dve.wait(made[n], bc1[g])
            if n >= 2:
                dve.wait(conv_done[n - 2])
            h_read[n] = dve.do(nc.vector.tensor_tensor, h[r][:, :, :],
                               ps[:, :].rearrange("p (b t) -> p b t", b=GB),
                               inv1_b[s][:, :].rearrange("p (b t) -> p b t", b=GB), ALU.mult).mark()
            act.wait(h_read[n])
            if n >= 2:
                act.wait(silu_done[n - 2])
            mid = act.do(nc.scalar.activation, acc[r][:, :, :], h[r][:, :, :], ACT.Identity,
                         scale=cw[:, m, 1:2], bias=cb[:, m:m + 1]).mark()
            dve.wait(mid)
            one = dve.do(nc.vector.scalar_tensor_tensor, acc[r][:, :, 1:], h[r][:, :, 0:TOK - 1],
                         cw[:, m, 0:1], acc[r][:, :, 1:], ALU.mult, ALU.add).mark()
            dve.wait(one)
            conv_done[n] = dve.do(nc.vector.scalar_tensor_tensor, acc[r][:, :, 0:TOK - 1], h[r][:, :, 1:],
                                  cw[:, m, 2:3], acc[r][:, :, 0:TOK - 1], ALU.mult, ALU.add).mark()
            act.wait(conv_done[n])
            if g >= 2:
                act.wait(hq_ready[g - 2, TILES - 1])
            silu_done[n] = act.do(nc.scalar.activation,
                                  act_h[s][:, m, :].rearrange("p (b t) -> p b t", b=GB),
                                  acc[r][:, :, :], ACT.Silu).mark()

        def hidden_scale(g):
            s = g % 2
            V = nc.vector
            dve.wait(silu_done[g * TILES + TILES - 1])
            if g:
                dve.wait(max_turned[g - 1])
            maxed[g] = dve.do(V.tensor_reduce, hmax[:, :], act_h[s][:, :, :].rearrange("p m t -> p t m"), AX.X,
                              ALU.max, apply_absolute_value=True).mark()
            pe.wait(maxed[g], b_free[0])
            for i in range(GB):
                pe.do(nc.tensor.transpose, b_ps[:, i * TOK:(i + 1) * TOK], hmax[:, i * TOK:(i + 1) * TOK],
                      ident[:, :])
            max_turned[g] = pe.mark()
            dve.wait(max_turned[g])
            r = dve.do(V.tensor_reduce, amax2[:, :], b_ps[:, :].rearrange("p (b t) -> p b t", b=GB), AX.X,
                       ALU.max).mark()
            dve.wait(r)
            if g:
                dve.wait(q2_ready[g - 1, 'turned'])
            r2 = dve.do(V.tensor_scalar, amax2[:, :], amax2[:, :], 1e-5, 1.0 / 127.0, ALU.max, ALU.mult).mark()
            dve.wait(r2)
            if g >= 2:
                dve.wait(finished[g - 2])
            q2_ready[g] = dve.do(V.reciprocal, q2[:, :], amax2[:, :]).mark()
            inv2_ready[g] = dve.do(V.tensor_scalar, inv2[s][:, :], amax2[:, :], w_mean[:, 1:2], None,
                                   ALU.mult).mark()
            pe.wait(q2_ready[g], r)
            for i in range(GB):
                pe.do(nc.tensor.transpose, b_ps[:, i * TOK:(i + 1) * TOK], q2[:, i:i + 1].broadcast_to([P, P]),
                      ident[:, :])
            q2_ready[g, 'turned'] = pe.mark()
            act.wait(q2_ready[g, 'turned'])
            if g:
                act.wait(q2b_ready[g - 1, 'used'])
            b_free[0] = q2b_ready[g] = act.do(nc.scalar.copy, q2_b[:, :], b_ps[:, :]).mark()

        def hidden_quant(g):
            s = g % 2
            pool.wait(q2b_ready[g])
            dve.wait(q2b_ready[g])
            for m in range(TILES):
                t = act_h[s][:, m, :]
                q, mul = (pool, nc.gpsimd.tensor_tensor) if m % 2 else (dve, nc.vector.tensor_tensor)
                scaled = q.do(mul, t, t, q2_b[:, :], ALU.mult).mark()
                q2b_ready[g, 'used'] = scaled
                act.wait(scaled)
                r = act.do(nc.scalar.activation, t, t, ACT.Copy, bias=ROUND).mark()
                dve.wait(r)
                if g:
                    dve.wait(out_made[g - 1])
                hq_ready[g, m] = dve.do(nc.vector.tensor_scalar, hq[:, m, :], t, ROUND, 127.0,
                                        ALU.subtract, ALU.min).mark()

        def output(g):
            s = g % 2
            pe.wait(*[hq_ready[g, m] for m in range(TILES)])
            if g:
                pe.wait(finished[g - 1])
            for i in range(GB):
                for m in range(TILES):
                    pe.do(nc.tensor.matmul, o_ps[i // 2][:, (i % 2) * DIM:(i % 2 + 1) * DIM],
                          hq[:, m, i * TOK:(i + 1) * TOK], w2q[:, m, :], start=m == 0, stop=m == TILES - 1)
            out_made[g] = pe.mark()
            dve.wait(out_made[g], inv2_ready[g])
            if g >= 2:
                dve.wait(stored[g - 2])
            for i in range(GB):
                dve.do(nc.vector.scalar_tensor_tensor, x_out[s][:, i, :],
                       o_ps[i // 2][:, (i % 2) * DIM:(i % 2 + 1) * DIM], inv2[s][:, i:i + 1],
                       x_all[:, GB * g + i, :], ALU.mult, ALU.add)
            finished[g] = dve.mark()
            sp.wait(finished[g])
            stored[g] = sp.dma(nc.sync.dma_start, store[s], out[GB * g:GB * g + GB].rearrange("b t d -> t b d"),
                               x_out[s][:, :, :])

        def hiddens(g):
            for m in range(TILES):
                hidden(g * TILES + m)

        def prepare(g):
            quantise(g)
            turn(g)

        def finish(g):
            hidden_scale(g)
            hidden_quant(g)

        pipeline(NG, expand, prepare, hiddens, finish, output)
        sp.wait(*stored.values())


def build(nc, x, ctx, ctxT, wq, wkv, wo, ln_cols, router, bias, gate, up, down, s_gate, s_up, s_down,
          w1T, w2T, conv_w, conv_b, out):
    dist = nc.dram_tensor("dist", (SEQS, TOK, TOK), F32, kind="Internal").ap()
    path = nc.dram_tensor("path", (SEQS, TOK, TOK), F32, kind="Internal").ap()
    with nc.sbuf_tensor("x_all", [P, SEQS, DIM], F32) as x_all, \
            nc.sbuf_tensor("ident", [P, P], F32) as ident, nc.sbuf_tensor("minus_half", [P, 4], F32) as half:
        attention(nc, x_all, ident, half, x, ctx, wq, wkv, wo, ln_cols)
        experts(nc, x_all, ident, half, router, bias, gate, up, down, s_gate, s_up, s_down)
        distances(nc, x_all, ident, half, ctx, ctxT, dist)
        align(nc, dist, path)
        conv_ffn(nc, x_all, ident, half, ctx, path, w1T, w2T, conv_w, conv_b, out)


def kernel(**inputs):
    import concourse.bacc as bacc
    from concourse.bass_utils import run_bass_kernel_spmd

    a = {n: np.asarray(v) for n, v in inputs.items()}
    tiles = CONV_HID // P
    arrays = {
        "x": a["x"],
        "ctx": a["ctx_1024"],
        "ctxT": a["ctx_1024"].transpose(0, 2, 1),
        "wq": a["L0_xattn_Wq"],
        "wkv": a["L0_xattn_Wkv"],
        "wo": a["L0_xattn_Wo"],
        "ln_cols": np.stack([a["L0_xattn_ln1_w"], a["L0_xattn_ln1_b"], a["L0_xattn_ln2_w"],
                             a["L0_xattn_ln2_b"]]).reshape(4, KD, P).transpose(2, 0, 1),
        "router": a["L0_ffn_router_w"].T,
        "bias": np.broadcast_to(a["L0_ffn_correction_bias"], (P, EXPERTS)),
        "gate": a["L0_ffn_gate_w"].transpose(1, 0, 2).reshape(DIM, ROUTED),
        "up": a["L0_ffn_up_w"].transpose(1, 0, 2).reshape(DIM, ROUTED),
        "down": a["L0_ffn_down_w"].reshape(ROUTED, DIM),
        "s_gate": a["L0_ffn_shared_gate_w"].T,
        "s_up": a["L0_ffn_shared_up_w"].T,
        "s_down": a["L0_ffn_shared_down_w"].T,
        "w1T": a["L1_ffn_w1"].T,
        "w2T": a["L1_ffn_w2"].T,
        "conv_w": a["L1_ffn_conv_w"].reshape(tiles, P, 3).transpose(1, 0, 2),
        "conv_b": a["L1_ffn_conv_b"].reshape(tiles, P).T,
    }
    arrays = {f"in_{n}": np.ascontiguousarray(v) for n, v in arrays.items()}
    nc = bacc.Bacc("TRN2", target_bir_lowering=False, num_devices=1)
    args = [nc.dram_tensor(n, v.shape, mybir.dt.from_np(v.dtype), kind="ExternalInput").ap()
            for n, v in arrays.items()]
    out = nc.dram_tensor("out", (SEQS, TOK, DIM), F32, kind="ExternalOutput").ap()
    build(nc, *args, out)
    r = run_bass_kernel_spmd(nc, [arrays], core_ids=[0])
    return r.results[0]["out"]
```

```python
from contextlib import ExitStack

import numpy as np

import concourse.bass as bass
from concourse import mybir

F32 = mybir.dt.float32
F32R = mybir.dt.float32r
BF16 = mybir.dt.bfloat16
ALU = mybir.AluOpType
ACT = mybir.ActivationFunctionType
AX = mybir.AxisListType

P = 128
SEQS, TOK, DIM = 64, 128, 256
KD = DIM // P
HEADS, HEAD = 16, 64
INNER = HEADS * HEAD
EXPERTS, HID, SHARED = 16, 64, 512
ROUTED = EXPERTS * HID
GROUPS, PICK_GROUPS, PICK = 4, 2, 4
CONV_HID = 1024
EPS = 1e-5
BIG = 1e30
ROUND = 1.5 * 2.0 ** 23
GB = 4
NG = SEQS // GB


class Queue:

    def __init__(self, sem):
        self.sem, self.count, self.items, self.known = sem, 0, [], {}

    def do(self, build, *args, **kwargs):
        self.items.append([build, args, kwargs, None])
        return self

    def mark(self):
        self.count += 1
        self.items[-1][3] = (self.sem, 1)
        return (self.sem, self.count)

    def wait(self, *counts):
        for sem, value in counts:
            if self.known.get(sem.name, 0) < value:
                self.known[sem.name] = value
                self.items.append([None, (sem, value), None, None])
        return self

    def dma(self, build, lane, out, in_):
        lane[1] += 16
        self.items.append([build, (out, in_), {}, (lane[0], 16)])
        return (lane[0], lane[1])

    def replay(self, engine):
        for build, args, kwargs, inc in self.items:
            if build is None:
                engine.wait_ge(*args)
            else:
                made = build(*args, **kwargs)
                if inc:
                    made.then_inc(*inc)


class Stage:

    def __init__(self, nc, name):
        self.nc, self.name, self.ctx = nc, name, ExitStack()

    def __enter__(self):
        self.pe, self.act, self.dve, self.pool, self.sp = (
            Queue(self.sem(n)) for n in ("pe", "act", "dve", "pool", "sp"))
        return self

    def sem(self, n):
        return self.ctx.enter_context(self.nc.semaphore(f"{self.name}_{n}_done"))

    def lane(self, n):
        return [self.sem(n), 0]

    def sb(self, n, shape, dt=F32):
        return self.ctx.enter_context(self.nc.sbuf_tensor(f"{self.name}_{n}", shape, dt))

    def bank(self, n, dt=F32):
        return self.ctx.enter_context(
            self.nc.psum_tensor(f"{self.name}_{n}", [P, 2048 // mybir.dt.size(dt)], dt))

    def __exit__(self, kind, *rest):
        if kind is None:
            with self.nc.Block() as block:
                block.sync(self.sp.replay)
                block.tensor(self.pe.replay)
                block.scalar(self.act.replay)
                block.vector(self.dve.replay)
                block.gpsimd(self.pool.replay)
        return self.ctx.__exit__(kind, *rest)


def pipeline(count, *steps):
    for t in range(count + len(steps) - 1):
        for s in reversed(range(len(steps))):
            if 0 <= t - s < count:
                steps[s](t - s)


def split_weight(st, lane, stage, stage_free, src, hi, lo):
    nc = st.nc
    st.sp.wait(*stage_free)
    landed = st.sp.dma(nc.sync.dma_start, lane, stage, src)
    st.dve.wait(landed)
    high = st.dve.do(nc.vector.tensor_copy, hi, stage).mark()
    st.dve.wait(high)
    return st.dve.do(nc.vector.tensor_tensor, lo, stage, hi.bitcast(F32), ALU.subtract).mark()


def rsqrt_var(st, mv, var_eps, rstd, half, n, ready, free=()):
    nc = st.nc
    st.pool.wait(*ready, *free)
    a = st.pool.do(nc.gpsimd.tensor_scalar, var_eps, mv[:, 0:n, 1], EPS, None, ALU.add).mark()
    st.pool.wait(a)
    return st.pool.do(nc.gpsimd.tensor_tensor, rstd, var_eps, half[:, 0:n], ALU.pow).mark()


def stats(st, tiles, raw, mv):
    nc = st.nc
    for n, t in enumerate(tiles):
        st.dve.do(nc.vector.bn_stats, raw[:, n, :], t)
    done = st.dve.mark()
    st.dve.wait(done)
    for n in range(len(tiles)):
        st.dve.do(nc.vector.bn_aggr, mv[:, n, :], raw[:, n, :])
    return st.dve.mark()


def normalise(st, outs, tiles, mv, rstd, ready):
    nc = st.nc
    st.dve.wait(*ready)
    for n, t in enumerate(tiles):
        st.dve.do(nc.vector.tensor_scalar, outs[n], t, mv[:, n, 0:1], rstd[:, n:n + 1],
                  ALU.subtract, ALU.mult)
    return st.dve.mark()


def attention(nc, x_all, ident, half, x, ctx, wq, wkv, wo, ln_cols):
    QUADS, QH = 4, HEADS // 4
    QT = QH * HEAD // P
    QW = QH * HEAD
    LAST = SEQS * QUADS
    with Stage(nc, "attention") as st:
        pe, act, dve, pool, sp = st.pe, st.act, st.dve, st.pool, st.sp
        wq_p = [st.sb(f"wq_{n}", [P, KD, INNER], F32R) for n in ("hi", "lo")]
        wkv_p = [st.sb(f"wkv_{n}", [P, KD, 2 * INNER], F32R) for n in ("hi", "lo")]
        wo_p = [st.sb(f"wo_{n}", [P, INNER // P, DIM], F32R) for n in ("hi", "lo")]
        cols = st.sb("ln_cols", [P, 4, KD])
        ctx_sb = [st.sb(f"ctx{i}", [P, 2, DIM]) for i in range(2)]
        lat = st.sb("latents", [P, 2, DIM])
        raw = st.sb("raw_stats", [P, 4, 6])
        mv = [st.sb(f"mean_var{i}", [P, 4, 2]) for i in range(2)]
        var_eps = [st.sb(f"var_eps{i}", [P, 4]) for i in range(2)]
        rstd = [st.sb(f"rstd{i}", [P, 4]) for i in range(2)]
        kv_full = st.sb("kv_full", [P, KD, 2 * TOK])
        kv_hi = [st.sb(f"kv_hi{i}", [P, KD, 2 * TOK], F32R) for i in range(2)]
        kv_lo = [st.sb(f"kv_lo{i}", [P, KD, 2 * TOK], F32R) for i in range(2)]
        q_hi, q_lo = ([st.sb(f"q_{n}{i}", [P, QT, TOK], F32R) for i in range(2)] for n in ("hi", "lo"))
        k_hi, k_lo = ([st.sb(f"k_{n}{i}", [P, QT, 2 * TOK], F32R) for i in range(2)] for n in ("hi", "lo"))
        v = [st.sb(f"v{i}", [P, 2, QH, 2, HEAD], F32R) for i in range(3)]
        prob = [st.sb(f"prob{i}", [P, QH, 2 * TOK]) for i in range(2)]
        probT_hi, probT_lo = ([st.sb(f"probT_{n}{i}", [P, QH, 2, TOK], F32R) for i in range(2)]
                              for n in ("hi", "lo"))
        neg_max = st.sb("neg_max", [P, 2, QH])
        sums = st.sb("row_sums", [P, 3, QH])
        inv = st.sb("inv_sums", [P, QH])
        low = st.sb("low_part", [P, QH, HEAD])
        att = st.sb("att", [P, INNER])
        attT_hi, attT_lo = (st.sb(f"attT_{n}", [P, INNER // P, TOK], F32R) for n in ("hi", "lo"))
        proj = [st.bank(f"proj{i}") for i in range(3)]
        scores = [st.bank(f"scores{i}") for i in range(2)]
        turned = [st.bank(f"turned{i}") for i in range(2)]
        heads_out = st.bank("heads_out")

        XC = 8
        ctx_lane = [st.lane(f"ctx_load{i}") for i in range(2)]
        x_in, ctx_in = {}, {}

        def load_x(c):
            x_in[c] = sp.dma(nc.sync.dma_start, st.lane(f"x_load{c}"), x_all[:, XC * c:XC * c + XC, :],
                             x[XC * c:XC * c + XC].rearrange("b t d -> t b d"))

        w_lane = st.lane("column_load")
        load_x(0)
        w_in = sp.dma(nc.sync.dma_start, w_lane, cols[:, :, :], ln_cols)
        pool.do(nc.gpsimd.memset, half[:, :], -0.5)
        zero = pool.do(nc.gpsimd.memset, ident[:, :], 0.0).mark()
        pool.wait(zero)
        const = pool.do(nc.gpsimd.affine_select, out=ident[:, :], in_=ident[:, :],
                        compare_op=ALU.not_equal, fill=1.0, base=0, pattern=[[-1, P]],
                        channel_multiplier=1).mark()
        stage_lane = [st.lane(f"stage_load{i}") for i in range(2)]
        staged = []

        def load_weight(src, hi, lo):
            n = len(staged)
            buf = prob[n % 2][:, :, :].rearrange("p a b -> p (a b)")
            staged.append(split_weight(st, stage_lane[n % 2], buf[:, 0:src.shape[1]], staged[n - 2:n - 1] if n >= 2 else (),
                                       src, hi, lo))

        got_stats, r_one, turned_in, normed, kv_ready, kv_used = {}, {}, {}, {}, {}, {}
        q_ready, k_ready, v_ready = {}, {}, {}
        score_done, max_done, exp_done, t_done, t_split, pv_done = {}, {}, {}, {}, {}, {}
        low_read, att_done, att_turned, attT_done, out_made = {}, {}, {}, {}, {}
        proj_free, n_proj = {}, [0]

        def take_proj():
            i = n_proj[0] % len(proj)
            n_proj[0] += 1
            if i in proj_free:
                pe.wait(proj_free[i])
            return i, proj[i]

        def load_ctx(b):
            s = (b // 2) % 2
            if b >= 4:
                sp.wait(turned_in[b - 4], turned_in[b - 3])
            ctx_in[b] = sp.dma(nc.sync.dma_start, ctx_lane[s], ctx_sb[s][:, :, :],
                               ctx[b:b + 2].rearrange("b t d -> t b d"))

        def pair(b):
            s = (b // 2) % 2
            return ([x_all[:, b + i, :] for i in range(2)], [ctx_sb[s][:, i, :] for i in range(2)],
                    [lat[:, i, :] for i in range(2)])

        def norm_a(b):
            xs, cs, ls = pair(b)
            dve.wait(x_in[b // XC], ctx_in[b])
            got = stats(st, xs + cs, raw, mv[0])
            r_one[b] = rsqrt_var(st, mv[0], var_eps[0][:, :], rstd[0][:, :], half, 4, (got, const))

        def norm_b(b):
            xs, cs, ls = pair(b)
            if b:
                dve.wait(turned_in[b - 1])
            one = normalise(st, ls + cs, xs + cs, mv[0], rstd[0], (r_one[b],))
            dve.wait(one)
            got = stats(st, ls, raw, mv[1])
            r_one[b] = rsqrt_var(st, mv[1], var_eps[1][:, 0:2], rstd[1][:, 0:2], half, 2, (got,))

        def norm_c(b):
            xs, cs, ls = pair(b)
            normed[b] = normed[b + 1] = normalise(st, ls, ls, mv[1], rstd[1], (r_one[b],))

        def turn_inputs(b):
            s, i = (b // 2) % 2, b % 2
            at, bank = take_proj()
            pe.wait(normed[b], const)
            view = bank[:, :].rearrange("p (k c t) -> p k c t", k=KD, c=2)
            for k in range(KD):
                for c, src in enumerate((ctx_sb[s], lat)):
                    pe.do(nc.tensor.transpose, view[:, k, c, :], src[:, i, k * P:(k + 1) * P], ident[:, :])
            turned_in[b] = pe.mark()
            dve.wait(turned_in[b], w_in)
            if b:
                dve.wait(kv_ready[b - 1])
            for k in range(KD):
                for c in range(2):
                    dve.do(nc.vector.tensor_scalar, kv_full[:, k, c * TOK:(c + 1) * TOK], view[:, k, c, :],
                           cols[:, 2 * c, k:k + 1], cols[:, 2 * c + 1, k:k + 1], ALU.mult, ALU.add)
            full = proj_free[at] = dve.mark()
            act.wait(full)
            pool.wait(full)
            if b >= 2:
                act.wait(kv_used[b - 2])
                pool.wait(kv_used[b - 2])
            high = act.do(nc.scalar.activation, kv_hi[b % 2][:, :, :], kv_full[:, :, :], ACT.Copy).mark()
            pool.wait(high)
            kv_ready[b] = pool.do(nc.gpsimd.tensor_tensor, kv_lo[b % 2][:, :, :], kv_full[:, :, :],
                                  kv_hi[b % 2][:, :, :].bitcast(F32), ALU.subtract).mark()

        def three_pass(out, left, right):
            n = 0
            for k in range(KD):
                for l, r in ((0, 0), (0, 1), (1, 0)):
                    pe.do(nc.tensor.matmul, out, left[l](k), right[r](k), start=n == 0, stop=n == 3 * KD - 1)
                    n += 1

        def split_out(made, view, hi, lo, used, scale):
            act.wait(made, *used)
            high = act.do(nc.scalar.activation, hi, view, ACT.Copy, scale=scale).mark()
            dve.wait(high)
            return dve.do(nc.vector.scalar_tensor_tensor, lo, view, scale, hi.bitcast(F32), ALU.mult,
                          ALU.subtract).mark()

        def columns(w, lo, hi):
            return [lambda k, t=t: t[:, k, lo:hi] for t in w]

        def project_q(n):
            b, i = divmod(n, QUADS)
            at, bank = take_proj()
            pe.wait(kv_ready[b], wq_split[i])
            kv = (kv_hi[b % 2], kv_lo[b % 2])
            for m in range(QT):
                w = i * QW + m * P
                three_pass(bank[:, m * TOK:(m + 1) * TOK], columns(wq_p, w, w + P), columns(kv, TOK, 2 * TOK))
            proj_free[at] = q_ready[n] = split_out(
                pe.mark(), bank[:, 0:QT * TOK].rearrange("p (m t) -> p m t", m=QT), q_hi[n % 2][:, :, :],
                q_lo[n % 2][:, :, :], [score_done[n - 2]] if n >= 2 else [], HEAD ** -0.5)

        def project_k(n):
            b, i = divmod(n, QUADS)
            at, bank = take_proj()
            pe.wait(wk_split[i])
            kv = (kv_hi[b % 2], kv_lo[b % 2])
            for m in range(QT):
                w = i * QW + m * P
                three_pass(bank[:, m * 2 * TOK:(m + 1) * 2 * TOK], columns(wkv_p, w, w + P),
                           columns(kv, 0, 2 * TOK))
            proj_free[at] = k_ready[n] = split_out(
                pe.mark(), bank[:, :].rearrange("p (m t) -> p m t", m=QT), k_hi[n % 2][:, :, :],
                k_lo[n % 2][:, :, :], [score_done[n - 2]] if n >= 2 else [], 1.0)

        def project_v(n):
            b, i = divmod(n, QUADS)
            at, bank = take_proj()
            pe.wait(wv_split[i])
            kv = (kv_hi[b % 2], kv_lo[b % 2])
            w = INNER + i * QW
            for t in range(2):
                three_pass(bank[:, t * QW:(t + 1) * QW], columns(kv, t * TOK, (t + 1) * TOK),
                           columns(wkv_p, w, w + QW))
            made = pe.mark()
            if i == QUADS - 1:
                kv_used[b] = made
            act.wait(made)
            if n >= 3:
                act.wait(pv_done[n - 3])
            view = bank[:, :].rearrange("p (t h c) -> p t h c", t=2, h=QH)
            high = act.do(nc.scalar.activation, v[n % 3][:, :, :, 0, :], view, ACT.Copy).mark()
            dve.wait(high)
            dve.do(nc.vector.tensor_tensor, v[n % 3][:, :, :, 1, :], view,
                   v[n % 3][:, :, :, 0, :].bitcast(F32), ALU.subtract)
            proj_free[at] = v_ready[n] = dve.mark()

        def score(n):
            pe.wait(q_ready[n], k_ready[n])
            if n:
                pe.wait(exp_done[n - 1])
            s = n % 2
            for h in range(QH):
                m, e = divmod(h, 2)
                r = slice(e * HEAD, (e + 1) * HEAD)
                for j, (q_, k_) in enumerate(((q_hi, k_hi), (q_hi, k_lo), (q_lo, k_hi))):
                    pe.do(nc.tensor.matmul, scores[e][:, m * 256:(m + 1) * 256], q_[s][r, m, :],
                          k_[s][r, m, :], start=j == 0, stop=j == 2)
            score_done[n] = pe.mark()

        def row_max(n):
            dve.wait(score_done[n])
            if n >= 2:
                dve.wait(exp_done[n - 2])
            for e in range(2):
                dve.do(nc.vector.tensor_reduce, neg_max[:, n % 2, 2 * e:2 * e + 2],
                       scores[e][:, :].rearrange("p (h c) -> p h c", h=2), AX.X, ALU.max, negate=True)
            max_done[n] = dve.mark()

        def exponentials(n):
            act.wait(max_done[n], *staged[-2:])
            if n >= 2:
                act.wait(t_done[n - 2])
            if n >= 3:
                act.wait(att_done[n - 3])
            for h in range(QH):
                m, e = divmod(h, 2)
                act.do(nc.scalar.activation, prob[n % 2][:, h, :], scores[e][:, m * 256:(m + 1) * 256], ACT.Exp,
                       bias=neg_max[:, n % 2, 2 * e + m:2 * e + m + 1], accum_out=sums[:, n % 3, h:h + 1])
            exp_done[n] = act.mark()

        def turn_probs(n):
            pe.wait(exp_done[n])
            for g in range(2):
                if n:
                    pe.wait(t_split[n - 1, g])
                for h in range(2):
                    for t in range(2):
                        pe.do(nc.tensor.transpose, turned[g][:, (2 * h + t) * P:(2 * h + t + 1) * P],
                              prob[n % 2][:, 2 * g + h, t * P:(t + 1) * P], ident[:, :])
                t_done[n] = pe.mark()
                t_split[n, g] = split_out(
                    t_done[n], turned[g][:, :], probT_hi[n % 2][:, 2 * g:2 * g + 2].rearrange("p h t c -> p (h t c)"),
                    probT_lo[n % 2][:, 2 * g:2 * g + 2].rearrange("p h t c -> p (h t c)"),
                    [pv_done[n - 2]] if n >= 2 else [], 1.0)

        def weigh_values(n):
            b, i = divmod(n, QUADS)
            pe.wait(t_split[n, 0], t_split[n, 1], v_ready[n])
            if n:
                pe.wait(low_read[n - 1])
            for h in range(QH):
                j = 0
                for t in range(2):
                    for part in (probT_hi, probT_lo):
                        pe.do(nc.tensor.matmul, heads_out[:, h * P:(h + 1) * P], part[n % 2][:, h, t, :],
                              v[n % 3][:, t, h].rearrange("p a c -> p (a c)"), start=j == 0, stop=j == 3)
                        j += 1
            pv_done[n] = pe.mark()
            view = heads_out[:, :].rearrange("p (h a c) -> p h a c", h=QH, a=2)
            act.wait(pv_done[n])
            if n:
                act.wait(low_read[n - 1])
            copied = act.do(nc.scalar.copy, low[:, :, :], view[:, :, 1, :]).mark()
            dve.wait(exp_done[n])
            r = dve.do(nc.vector.reciprocal, inv[:, :], sums[:, n % 3, :]).mark()
            dve.wait(copied)
            if b:
                dve.wait(att_turned[b - 1])
            here = att[:, i * QW:(i + 1) * QW].rearrange("p (h c) -> p h c", h=QH)
            low_read[n] = dve.do(nc.vector.tensor_tensor, here, view[:, :, 0, :], low[:, :, :], ALU.add).mark()
            dve.wait(low_read[n], r)
            att_done[n] = dve.do(nc.vector.tensor_tensor, here, here,
                                 inv[:, :].unsqueeze(2).broadcast_to([P, QH, HEAD]), ALU.mult).mark()
            dve.wait(att_done[n])

        def turn_heads(b):
            pe.wait(att_done[b * QUADS + QUADS - 1])
            for o in range(2):
                at, bank = take_proj()
                for m in range(4):
                    pe.do(nc.tensor.transpose, bank[:, m * P:(m + 1) * P],
                          att[:, (4 * o + m) * P:(4 * o + m + 1) * P], ident[:, :])
                att_turned[b] = pe.mark()
                proj_free[at] = attT_done[b, o] = split_out(
                    att_turned[b], bank[:, :].rearrange("p (m t) -> p m t", m=4), attT_hi[:, 4 * o:4 * o + 4, :],
                    attT_lo[:, 4 * o:4 * o + 4, :], [out_made[b - 1]] if b else [], 1.0)

        def output(b):
            pe.wait(attT_done[b, 0], attT_done[b, 1], wo_split)
            at, bank = take_proj()
            n = 0
            for m in range(INNER // P):
                for l, r in ((attT_hi, 0), (attT_hi, 1), (attT_lo, 0)):
                    pe.do(nc.tensor.matmul, bank[:, 0:DIM], l[:, m, :], wo_p[r][:, m, :],
                          start=n == 0, stop=n == 3 * INNER // P - 1)
                    n += 1
            out_made[b] = pe.mark()
            dve.wait(out_made[b])
            proj_free[at] = dve.do(nc.vector.tensor_tensor, x_all[:, b, :], x_all[:, b, :],
                                   bank[:, 0:DIM], ALU.add).mark()

        load_ctx(0)
        norm_a(0)
        norm_b(0)
        norm_c(0)

        def load_block(src, dst, c, width):
            for k in range(KD):
                w = slice(c, c + width)
                load_weight(src[k * P:(k + 1) * P, w], dst[0][:, k, w], dst[1][:, k, w])
            return staged[-1]

        wq_split = [load_block(wq, wq_p, 0, INNER)] * QUADS
        wk_split = [load_block(wkv, wkv_p, 0, INNER)] * QUADS
        wv_split = [load_block(wkv, wkv_p, INNER, INNER)] * QUADS
        wo_v = wo.rearrange("(m p) n -> p m n", p=P)
        for m in range(0, INNER // P, 4):
            n = len(staged)
            buf = prob[n % 2][:, :, :]
            staged.append(split_weight(st, stage_lane[n % 2], buf, [staged[n - 2]], wo_v[:, m:m + 4, :],
                                       wo_p[0][:, m:m + 4, :], wo_p[1][:, m:m + 4, :]))
        wo_split = staged[-1]
        load_ctx(2)
        for c in range(1, SEQS // XC):
            load_x(c)
        turn_inputs(0)
        project_q(0)
        project_k(0)
        project_v(0)
        for n in range(LAST + 4):
            b, i = divmod(n, QUADS)
            if n < LAST:
                score(n)
                row_max(n)
            if n + 1 < LAST:
                project_q(n + 1)
            if n < LAST:
                exponentials(n)
            if n + 1 < LAST:
                project_k(n + 1)
            if i == 2 and 1 <= b <= SEQS:
                turn_heads(b - 1)
            if i == 3 and 1 <= b <= SEQS:
                output(b - 1)
            if 1 <= n <= LAST:
                turn_probs(n - 1)
            if i == 1 and b + 1 < SEQS:
                turn_inputs(b + 1)
            if 2 <= n <= LAST + 1:
                weigh_values(n - 2)
            if n + 1 < LAST:
                project_v(n + 1)
            if b % 2 == 0 and b + 2 < SEQS:
                if i == 1:
                    norm_a(b + 2)
                if i == 2:
                    norm_b(b + 2)
                if i == 3:
                    norm_c(b + 2)
            if b % 2 == 1 and i == 2 and b + 3 < SEQS:
                load_ctx(b + 3)


def experts(nc, x_all, ident, half, router, bias, gate, up, down, s_gate, s_up, s_down):
    TILES = ROUTED // P
    STILES = SHARED // P
    with Stage(nc, "experts") as st:
        pe, act, dve, pool, sp = st.pe, st.act, st.dve, st.pool, st.sp
        gate_w = [st.sb(f"gate_{n}", [P, KD, ROUTED + SHARED], F32R) for n in ("hi", "lo")]
        up_w = [st.sb(f"up_{n}", [P, KD, ROUTED + SHARED], F32R) for n in ("hi", "lo")]
        down_w = [st.sb(f"down_{n}", [P, TILES + STILES, DIM], F32R) for n in ("hi", "lo")]
        router_w = st.sb("router", [P, KD, EXPERTS])
        bias_w = st.sb("bias", [P, EXPERTS])
        below = st.sb("below", [P, EXPERTS, EXPERTS])
        xn = st.sb("xn", [P, GB, DIM])
        raw = st.sb("raw_stats", [P, GB, 6])
        mv = st.sb("mean_var", [P, GB, 2])
        var_eps = st.sb("var_eps", [P, GB])
        rstd = st.sb("rstd", [P, GB])
        xT = st.sb("xT", [P, KD, GB * TOK])
        xT_hi = [st.sb(f"xT_hi{i}", [P, KD, GB * TOK], F32R) for i in range(2)]
        xT_lo = [st.sb(f"xT_lo{i}", [P, KD, GB * TOK], F32R) for i in range(2)]
        comb_x = st.sb("comb_spread", [P, GB, EXPERTS, HID])
        silu = [st.sb(f"silu{i}", [P, GB * TOK]) for i in range(2)]
        weighed = [st.sb(f"weighed{i}", [P, GB * TOK]) for i in range(2)]
        hid_hi = [st.sb(f"hidden_hi{i}", [P, GB * TOK], F32R) for i in range(3)]
        hid_lo = [st.sb(f"hidden_lo{i}", [P, GB * TOK], F32R) for i in range(3)]
        sc, sb_, tmp = (st.sb(n, [P, GB, EXPERTS]) for n in ("score", "biased", "small"))
        pq = st.sb("pair", [P, 2, GB * GROUPS, 2])
        tops = st.sb("tops", [P, 4, GB * GROUPS])
        gs = st.sb("group_score", [P, GB, GROUPS])
        gcmp = st.sb("group_compare", [P, 2, GB, GROUPS, GROUPS])
        gmask = st.sb("group_mask", [P, GB, GROUPS])
        gneg = st.sb("group_neg", [P, GB, GROUPS])
        masked = st.sb("masked", [P, GB, EXPERTS])
        cmp_ge = st.sb("compare_ge", [P, GB, EXPERTS, EXPERTS], BF16)
        cmp_gt = st.sb("compare_gt", [P, GB, EXPERTS, EXPERTS], BF16)
        rank = st.sb("rank", [P, GB, EXPERTS])
        comb = st.sb("combine", [P, GB, EXPERTS])
        wsum = st.sb("weight_sum", [P, 2, GB])
        misc = st.bank("misc")
        g_ps = [st.bank(f"gate{i}") for i in range(2)]
        u_ps = [st.bank(f"up{i}") for i in range(2)]
        c_ps = st.bank("combine_turned")
        out_ps = [st.bank(f"out{i}") for i in range(2)]

        w_lane = st.lane("weight_load")
        for src, dst in ((router.rearrange("(k p) n -> p k n", p=P), router_w[:, :, :]), (bias, bias_w[:, :])):
            w_in = sp.dma(nc.sync.dma_start, w_lane, dst, src)
        ones = pool.do(nc.gpsimd.memset, below[:, :, :], 1.0).mark()
        pool.wait(ones)
        const = pool.do(nc.gpsimd.affine_select, out=below[:, :, :], in_=below[:, :, :],
                        compare_op=ALU.is_gt, fill=0.0, base=0, pattern=[[1, EXPERTS], [-1, EXPERTS]],
                        channel_multiplier=0).mark()
        stage_lane = [st.lane(f"stage_load{i}") for i in range(4)]
        stage = comb_x[:, :, :, :].rearrange("p b e h -> p (b e h)")
        staged = []
        for src, (hi, lo), at, width in ((gate, gate_w, 0, ROUTED), (up, up_w, 0, ROUTED),
                                         (s_gate, gate_w, ROUTED, SHARED), (s_up, up_w, ROUTED, SHARED)):
            for k in range(KD):
                n = len(staged)
                s = (n % 4) * 1024
                w = slice(at, at + width)
                staged.append(split_weight(st, stage_lane[n % 4], stage[:, s:s + width],
                                           staged[n - 4:n - 3] if n >= 4 else (),
                                           src[k * P:(k + 1) * P, :], hi[:, k, w], lo[:, k, w]))
        gate_up_split = staged[-1]
        for src, at, tiles in ((down, 0, TILES), (s_down, TILES, STILES)):
            view = src.rearrange("(m p) n -> p m n", p=P)
            for m in range(0, tiles, 4):
                n = len(staged)
                s, w = (n % 4) * 1024, slice(at + m, at + m + 4)
                buf = stage[:, s:s + 4 * DIM].rearrange("p (m n) -> p m n", m=4)
                staged.append(split_weight(st, stage_lane[n % 4], buf, staged[n - 4:n - 3],
                                           view[:, m:m + 4, :], down_w[0][:, w, :], down_w[1][:, w, :]))
        w_split = staged[-1]
        stage_free = w_split

        normed, turned, x_ready, routed, spread = {}, {}, {}, {}, {}
        misc_free = [None]
        full_read = {}
        x_used, xn_used, comb_read, out_added = {}, {}, {}, {}

        def norm(g):
            xs = [x_all[:, GB * g + i, :] for i in range(GB)]
            got = stats(st, xs, raw, mv)
            r = rsqrt_var(st, mv, var_eps[:, :], rstd[:, :], half, GB, (got,))
            if g:
                dve.wait(xn_used[g - 1])
            normed[g] = normalise(st, [xn[:, i, :] for i in range(GB)], xs, mv, rstd, (r,))

        def turn(g):
            s = g % 2
            pe.wait(normed[g])
            for k in range(KD):
                if misc_free[0]:
                    pe.wait(misc_free[0])
                for i in range(GB):
                    pe.do(nc.tensor.transpose, misc[:, i * P:(i + 1) * P], xn[:, i, k * P:(k + 1) * P], ident[:, :])
                xn_used[g] = pe.mark()
                act.wait(xn_used[g])
                if g:
                    act.wait(full_read[g - 1], x_ready[g - 1])
                misc_free[0] = full = act.do(nc.scalar.copy, xT[:, k, :], misc[:, :]).mark()
            act.wait(full)
            if g >= 2:
                act.wait(x_used[g - 2])
            high = act.do(nc.scalar.activation, xT_hi[s][:, :, :], xT[:, :, :], ACT.Copy).mark()
            pool.wait(high)
            x_ready[g] = pool.do(nc.gpsimd.tensor_tensor, xT_lo[s][:, :, :], xT[:, :, :],
                                 xT_hi[s][:, :, :].bitcast(F32), ALU.subtract).mark()
            pe.wait(full, w_in)
            for i in range(GB):
                for k in range(KD):
                    pe.do(nc.tensor.matmul, misc[:, i * EXPERTS:(i + 1) * EXPERTS],
                          xT[:, k, i * TOK:(i + 1) * TOK], router_w[:, k, :], start=k == 0, stop=k == KD - 1)
            full_read[g] = pe.mark()
            act.wait(full_read[g])
            if g:
                act.wait(routed[g - 1])
            misc_free[0] = act.do(nc.scalar.activation, tmp[:, :, :],
                                  misc[:, 0:GB * EXPERTS].rearrange("p (b e) -> p b e", b=GB),
                                  ACT.Tanh, scale=0.5).mark()

        def chain(build, *a, **k):
            done = dve.do(build, *a, **k).mark()
            dve.wait(done)
            return done

        def route(g):
            V = nc.vector
            tt, ts = V.tensor_tensor, V.tensor_scalar
            dve.wait(misc_free[0], w_in, const)
            if g:
                dve.wait(spread[g - 1])
            chain(ts, sc[:, :, :], tmp[:, :, :], 0.5, 0.5, ALU.mult, ALU.add)
            chain(tt, sb_[:, :, :], sc[:, :, :], bias_w[:, :].unsqueeze(1).broadcast_to([P, GB, EXPERTS]), ALU.add)
            quad = sb_[:, :, :].rearrange("p b (g a c) -> p (b g) a c", g=GROUPS, a=2)
            dve.do(tt, pq[:, 0, :, :], quad[:, :, :, 0], quad[:, :, :, 1], ALU.max)
            chain(tt, pq[:, 1, :, :], quad[:, :, :, 0], quad[:, :, :, 1], ALU.min)
            dve.do(tt, tops[:, 0, :], pq[:, 0, :, 0], pq[:, 0, :, 1], ALU.max)
            dve.do(tt, tops[:, 1, :], pq[:, 0, :, 0], pq[:, 0, :, 1], ALU.min)
            chain(tt, tops[:, 2, :], pq[:, 1, :, 0], pq[:, 1, :, 1], ALU.max)
            chain(tt, tops[:, 3, :], tops[:, 1, :], tops[:, 2, :], ALU.max)
            chain(tt, gs[:, :, :].rearrange("p b g -> p (b g)"), tops[:, 0, :], tops[:, 3, :], ALU.add)

            def ranks(value, n, ge, gt, out):
                for i in range(GB):
                    e = value[:, i, :].unsqueeze(2).broadcast_to([P, n, n])
                    j = value[:, i, :].unsqueeze(1).broadcast_to([P, n, n])
                    dve.do(tt, ge[:, i], j, e, ALU.is_ge)
                    last = dve.do(tt, gt[:, i], j, e, ALU.is_gt)
                last = dve.mark()
                dve.wait(last)
                for i in range(GB):
                    dve.do(tt, ge[:, i], ge[:, i], below[:, 0:n, 0:n], ALU.mult)
                last = dve.mark()
                dve.wait(last)
                chain(tt, ge, ge, gt, ALU.max)
                chain(V.tensor_reduce, out, ge, AX.X, ALU.add)

            ranks(gs[:, :, :], GROUPS, gcmp[:, 0], gcmp[:, 1], gmask[:, :, :])
            chain(ts, gmask[:, :, :], gmask[:, :, :], PICK_GROUPS - 0.5, None, ALU.is_lt)
            chain(ts, gneg[:, :, :], gmask[:, :, :], 1.0, BIG, ALU.subtract, ALU.mult)
            g4 = lambda t: t[:, :, :].rearrange("p b g -> p (b g)").unsqueeze(2).broadcast_to(
                [P, GB * GROUPS, EXPERTS // GROUPS])
            flat = lambda t: t[:, :, :].rearrange("p b (g c) -> p (b g) c", g=GROUPS)
            chain(tt, flat(masked), flat(sb_), g4(gmask), ALU.mult)
            chain(tt, flat(masked), flat(masked), g4(gneg), ALU.add)
            ranks(masked[:, :, :], EXPERTS, cmp_ge[:, :], cmp_gt[:, :], rank[:, :, :])
            chain(ts, rank[:, :, :], rank[:, :, :], PICK - 0.5, None, ALU.is_lt)
            chain(tt, comb[:, :, :], sc[:, :, :], rank[:, :, :], ALU.mult)
            chain(V.tensor_reduce, wsum[:, 0, :], comb[:, :, :], AX.X, ALU.add)
            chain(ts, wsum[:, 0, :], wsum[:, 0, :], 1e-20, None, ALU.add)
            chain(V.reciprocal, wsum[:, 1, :], wsum[:, 0, :])
            routed[g] = chain(tt, comb[:, :, :], comb[:, :, :],
                              wsum[:, 1, :].unsqueeze(2).broadcast_to([P, GB, EXPERTS]), ALU.mult)

        def spread_weights(g):
            pool.wait(routed[g], stage_free)
            if g:
                pool.wait(comb_read[g - 1])
            for i in range(GB):
                pool.do(nc.gpsimd.tensor_copy, comb_x[:, i, :, :],
                        comb[:, i, :].unsqueeze(2).broadcast_to([P, EXPERTS, HID]))
            spread[g] = pool.mark()

        hid_ready, hid_used, gate_read, up_read, turn_read, weigh_read = {}, {}, {}, {}, {}, {}
        order = list(range(TILES, TILES + STILES)) + list(range(TILES))
        per = TILES + STILES

        def three_pass(ps, parts, w, r):
            n = 0
            for k in range(KD):
                for l, x_ in ((parts[0], xT_hi[r]), (parts[0], xT_lo[r]), (parts[1], xT_hi[r])):
                    pe.do(nc.tensor.matmul, ps, l[:, k, w], x_[:, k, :], start=n == 0, stop=n == 3 * KD - 1)
                    n += 1
            return pe.mark()

        def up_gate(n):
            g, t = divmod(n, per)
            m = order[t]
            s, r = n % 2, g % 2
            w = slice(m * P, (m + 1) * P)
            pe.wait(x_ready[g], gate_up_split)
            if n >= 2:
                pe.wait(gate_read[n - 2])
            made = three_pass(g_ps[s][:, :], gate_w, w, r)
            act.wait(made)
            if n >= 2:
                act.wait(weigh_read[n - 2])
            gate_read[n] = act.do(nc.scalar.activation, silu[s][:, :], g_ps[s][:, :], ACT.Silu).mark()
            if m < TILES:
                pe.wait(spread[g])
                if turn_read:
                    pe.wait(turn_read['last'])
                for i in range(GB):
                    pe.do(nc.tensor.transpose, c_ps[:, i * TOK:(i + 1) * TOK],
                          comb_x[:, i, 2 * m:2 * m + 2, :].rearrange("p e h -> p (e h)"), ident[:, :])
                c_made = comb_read[g] = pe.mark()
            if n >= 2:
                pe.wait(up_read[n - 2])
            made = three_pass(u_ps[s][:, :], up_w, w, r)
            if t == per - 1:
                x_used[g] = made
            dve.wait(gate_read[n])
            if m < TILES:
                dve.wait(c_made)
                turn_read['last'] = dve.do(nc.vector.tensor_tensor, silu[s][:, :], silu[s][:, :], c_ps[:, :],
                                           ALU.mult).mark()
                dve.wait(turn_read['last'])
            dve.wait(made)
            if n >= 2:
                dve.wait(hid_ready[n - 2])
            up_read[n] = weigh_read[n] = dve.do(nc.vector.tensor_tensor, weighed[s][:, :], silu[s][:, :],
                                                u_ps[s][:, :], ALU.mult).mark()
            act.wait(up_read[n])
            if n >= 3:
                act.wait(hid_used[n - 3])
            high = act.do(nc.scalar.activation, hid_hi[n % 3][:, :], weighed[s][:, :], ACT.Copy).mark()
            pool.wait(high)
            hid_ready[n] = pool.do(nc.gpsimd.tensor_tensor, hid_lo[n % 3][:, :], weighed[s][:, :],
                                   hid_hi[n % 3][:, :].bitcast(F32), ALU.subtract).mark()

        def down_proj(n):
            g, t = divmod(n, per)
            m = order[t]
            pe.wait(hid_ready[n], w_split)
            if t == 0 and g:
                pe.wait(out_added[g - 1])
            for i in range(GB):
                for j, (l, r) in enumerate(((hid_hi, 0), (hid_hi, 1), (hid_lo, 0))):
                    pe.do(nc.tensor.matmul, out_ps[i // 2][:, (i % 2) * DIM:(i % 2 + 1) * DIM],
                          l[n % 3][:, i * TOK:(i + 1) * TOK], down_w[r][:, m, :],
                          start=t == 0 and i % 2 == 0 and j == 0, stop=t == per - 1 and j == 2,
                          skip_group_check=True)
            hid_used[n] = pe.mark()
            if t == per - 1:
                dve.wait(hid_used[n])
                for i in range(2):
                    xs = x_all[:, GB * g + 2 * i:GB * g + 2 * i + 2, :].rearrange("p b d -> p (b d)")
                    dve.do(nc.vector.tensor_tensor, xs, xs, out_ps[i][:, :], ALU.add)
                out_added[g] = dve.mark()

        norm(0)
        turn(0)
        route(0)
        spread_weights(0)
        for n in range(NG * per + 2):
            g, t = divmod(n, per)
            if n < NG * per:
                up_gate(n)
            if n >= 2:
                down_proj(n - 2)
            if g + 1 < NG:
                if t == 1:
                    norm(g + 1)
                if t == 3:
                    turn(g + 1)
                if t == 5:
                    route(g + 1)
                if t == per - 1:
                    spread_weights(g + 1)


def distances(nc, x_all, ident, half, ctx, ctxT, dist):
    with Stage(nc, "distance") as st:
        pe, act, dve, pool, sp = st.pe, st.act, st.dve, st.pool, st.sp
        ctx_sb = [st.sb(f"ctx{i}", [P, GB, DIM]) for i in range(2)]
        cT = [st.sb(f"ctxT{i}", [P, KD, GB, TOK]) for i in range(2)]
        junk = st.sb("squares", [P, DIM])
        aa = [st.sb(f"ctx_norm{i}", [P, GB]) for i in range(2)]
        xn = st.sb("xn", [P, GB, DIM])
        raw = st.sb("raw_stats", [P, GB, 6])
        mv = st.sb("mean_var", [P, GB, 2])
        var_eps = st.sb("var_eps", [P, GB])
        rstd = st.sb("rstd", [P, GB])
        xT = [st.sb(f"xT{i}", [P, KD, GB * TOK]) for i in range(2)]
        xT2 = [st.sb(f"xT_square{i}", [P, KD, GB * TOK]) for i in range(2)]
        ones = st.sb("ones", [P, P])
        sq = [st.sb(f"squared_dist{i}", [P, GB, TOK]) for i in range(2)]
        dt_ = [st.sb(f"dist{i}", [P, GB, TOK]) for i in range(2)]
        turned = [st.bank(f"turned{i}") for i in range(2)]
        d_ps = [st.bank(f"dist_ps{i}") for i in range(2)]
        load = [st.lane(f"ctx_load{i}") for i in range(2)]
        store = [st.lane(f"dist_store{i}") for i in range(2)]
        const = pool.do(nc.gpsimd.memset, ones[:, :], 1.0).mark()
        landed, normed, turn_copied, x_turned, xs_ready, made = {}, {}, {}, {}, {}, {}
        scaled, aa_done, clamp, rooted, stored, sqd = {}, {}, {}, {}, {}, {}

        def fetch(g):
            s = g % 2
            if g >= 2:
                sp.wait(made[g - 2], aa_done[g - 2])
            sp.dma(nc.sync.dma_start, load[s], ctx_sb[s][:, :, :],
                   ctx[GB * g:GB * g + GB].rearrange("b t d -> t b d"))
            for k in range(KD):
                landed[g] = sp.dma(nc.sync.dma_start, load[s], cT[s][:, k, :, :],
                                   ctxT[GB * g:GB * g + GB, k * P:(k + 1) * P, :].rearrange("b p t -> p b t"))
            xs = [x_all[:, GB * g + i, :] for i in range(GB)]
            got = stats(st, xs, raw, mv)
            r = rsqrt_var(st, mv, var_eps[:, :], rstd[:, :], half, GB, (got,))
            if g:
                dve.wait(x_turned[g - 1])
            normed[g] = normalise(st, [xn[:, i, :] for i in range(GB)], xs, mv, rstd, (r,))

        def turn(g):
            s = g % 2
            for k in range(KD):
                pe.wait(normed[g])
                if g:
                    pe.wait(sqd[g - 1, k])
                for i in range(GB):
                    pe.do(nc.tensor.transpose, turned[k][:, i * P:(i + 1) * P], xn[:, i, k * P:(k + 1) * P],
                          ident[:, :])
                x_turned[g] = pe.mark()
                dve.wait(x_turned[g])
                act.wait(x_turned[g])
                if g >= 2:
                    dve.wait(made[g - 2])
                    act.wait(made[g - 2])
                turn_copied[g, k] = dve.do(nc.vector.tensor_scalar, xT[s][:, k, :], turned[k][:, :], -2.0,
                                           None, ALU.mult).mark()
                act.wait(turn_copied[g, k])
                sqd[g, k] = act.do(nc.scalar.activation, xT2[s][:, k, :], turned[k][:, :], ACT.Square).mark()
            act.wait(landed[g])
            if g >= 2:
                act.wait(clamp[g - 2])
            for i in range(GB):
                act.do(nc.scalar.activation, junk[:, :], ctx_sb[s][:, i, :], ACT.Square,
                       accum_out=aa[s][:, i:i + 1])
                aa_done[g] = act.mark()
                act.wait(aa_done[g])

        def multiply(g):
            s = g % 2
            pe.wait(landed[g], turn_copied[g, 0], turn_copied[g, 1], sqd[g, 0], sqd[g, 1], const)
            if g >= 2:
                pe.wait(clamp[g - 2])
            for i in range(GB):
                cols = slice(i * TOK, (i + 1) * TOK)
                for k in range(KD):
                    pe.do(nc.tensor.matmul, d_ps[s][:, cols], ones[:, :], xT2[s][:, k, cols],
                          start=k == 0, stop=False)
                for k in range(KD):
                    pe.do(nc.tensor.matmul, d_ps[s][:, cols], cT[s][:, k, i, :], xT[s][:, k, cols],
                          start=False, stop=k == KD - 1)
            made[g] = pe.mark()
            dve.wait(made[g], aa_done[g])
            if g >= 2:
                dve.wait(rooted[g - 2])
            for i in range(GB):
                dve.do(nc.vector.tensor_scalar, sq[s][:, i, :], d_ps[s][:, i * TOK:(i + 1) * TOK],
                       aa[s][:, i:i + 1], 0.0, ALU.add, ALU.max)
            clamp[g] = dve.mark()
            act.wait(clamp[g])
            if g >= 2:
                act.wait(stored[g - 2])
            rooted[g] = act.do(nc.scalar.activation, dt_[s][:, :, :], sq[s][:, :, :], ACT.Sqrt).mark()
            sp.wait(rooted[g])
            stored[g] = sp.dma(nc.sync.dma_start, store[s],
                               dist[GB * g:GB * g + GB].rearrange("b i j -> i b j"), dt_[s][:, :, :])

        pipeline(NG, fetch, turn, multiply)
        sp.wait(*stored.values())


def align(nc, dist, entries):
    N, CH = TOK, 8
    with Stage(nc, "align") as st:
        dve, pool, sp = st.dve, st.pool, st.sp
        V = nc.vector
        cost = st.sb("cost", [SEQS, N + 1, N + 1])
        best = [st.sb(f"best{i}", [SEQS, CH, N]) for i in range(2)]
        stay = [st.sb(f"not_left{i}", [SEQS, CH, N], BF16) for i in range(2)]
        code = [st.sb(f"code{i}", [SEQS, CH, N]) for i in range(2)]
        rise = st.sb("rise", [SEQS, N, N], mybir.dt.float16)
        columns = st.sb("columns", [SEQS, CH, N])
        junk = st.sb("products", [SEQS, N])
        load = [st.lane(f"dist_load{i}") for i in range(N // CH)]
        landed = [sp.dma(nc.sync.dma_start, load[c], cost[:, 1 + c * CH:1 + (c + 1) * CH, 1:],
                         dist[:, c * CH:(c + 1) * CH, :]) for c in range(N // CH)]
        pool.do(nc.gpsimd.iota, columns[:, :, :], pattern=[[256, CH], [1, N]], base=0, channel_multiplier=0,
                allow_small_or_imprecise_dtypes=True)
        pool.do(nc.gpsimd.memset, cost[:, :, 0:1], BIG)
        pool.do(nc.gpsimd.memset, cost[:, 0, 1:], BIG)
        pool.do(nc.gpsimd.memset, entries[:, N:N + 1], N - 1.0)
        pool.do(nc.gpsimd.memset, best[0][:, 0, :], BIG)
        edges = pool.mark()
        pool.wait(edges)
        edges = pool.do(nc.gpsimd.memset, best[0][:, 0, 0:1], 0.0).mark()
        dve.wait(edges)

        coded, maxed, risen, read = {}, {}, {}, {}

        def coding(c):
            s = c % 2
            above = cost[:, c * CH:c * CH + CH, :]
            here = cost[:, c * CH + 1:c * CH + CH + 1, :]

            def not_left():
                if c >= 2:
                    dve.wait(coded[c - 2])
                read[c] = dve.do(V.tensor_tensor, stay[s][:, :, :], here[:, :, 0:N], best[s][:, :, :],
                                 ALU.is_ge).mark()

            def diagonal():
                if c >= 2:
                    dve.wait(risen[c - 2])
                done = dve.do(V.tensor_tensor, code[s][:, :, :], above[:, :, 0:N], above[:, :, 1:],
                              ALU.is_le).mark()
                dve.wait(done)

            def column():
                done = dve.do(V.scalar_tensor_tensor, code[s][:, :, :], code[s][:, :, :], -0.75,
                              columns[:, :, :], ALU.mult, ALU.add).mark()
                pool.wait(done)
                coded[c] = pool.do(nc.gpsimd.tensor_tensor, code[s][:, :, :], code[s][:, :, :],
                                   stay[s][:, :, :], ALU.mult).mark()

            def running_max():
                dve.wait(coded[c])
                flat = code[s][:, :, :].rearrange("p r j -> p (r j)")
                maxed[c] = dve.do(V.tensor_tensor_scan, flat, flat, flat, 0.0, ALU.max, ALU.max).mark()
                pool.wait(maxed[c])
                risen[c] = pool.do(nc.gpsimd.tensor_tensor, rise[:, c * CH:(c + 1) * CH, 1:],
                                   code[s][:, :, 1:], code[s][:, :, 0:N - 1], ALU.subtract).mark()

            return [not_left, diagonal, column, None, None, running_max]

        row, between = None, []
        for i in range(N):
            c, r = divmod(i, CH)
            s = c % 2
            if r == 0:
                dve.wait(landed[c])
            if i:
                dve.wait(row)
                if r == 0 and c >= 2:
                    dve.wait(read[c - 2])
                least = dve.do(V.tensor_tensor, best[s][:, r, :], cost[:, i, 1:], cost[:, i, 0:N], ALU.min).mark()
                dve.wait(least)
            row = dve.do(V.tensor_tensor_scan, cost[:, i + 1, 1:], best[s][:, r, :], cost[:, i + 1, 1:], BIG,
                         ALU.min, ALU.add).mark()
            step = between.pop(0) if between else None
            if step:
                step()
            if r == CH - 1:
                between = coding(c)
        dve.wait(row)
        for step in between:
            if step:
                step()
        dve.wait(risen[N // CH - 1])
        for i in reversed(range(N)):
            done = dve.do(V.scalar_tensor_tensor, junk[:, 1:], columns[:, 0, 1:], entries[:, i + 1:i + 2],
                          rise[:, i, 1:], ALU.is_le, ALU.mult, accum_out=entries[:, i:i + 1]).mark()
            dve.wait(done)


def conv_ffn(nc, x_all, ident, half, ctx, entries, w1T, w2T, conv_w, conv_b, out):
    TILES = CONV_HID // P
    ON_VECTOR = (3, 7)
    with Stage(nc, "conv") as st:
        pe, act, dve, pool, sp = st.pe, st.act, st.dve, st.pool, st.sp
        w1q = st.sb("w1_ternary", [P, KD, CONV_HID], BF16)
        w2q = st.sb("w2_ternary", [P, TILES, DIM], BF16)
        w_sb = st.sb("w_stage", [P, 2, KD * CONV_HID])
        absum = st.sb("abs_sum", [P, 2])
        w_mean = st.sb("w_mean", [P, 2])
        w_inv = st.sb("w_inv", [P, 2])
        ones = st.sb("ones", [P, P])
        ident_b = st.sb("ident_bf16", [P, P], BF16)
        cw = st.sb("conv_w", [P, TILES, 3])
        cb = st.sb("conv_b", [P, TILES])
        ctx_sb = [st.sb(f"ctx{i}", [P, GB, DIM]) for i in range(2)]
        column = st.sb("column", [P, TOK])
        bounds = st.sb("path_bounds", [P, 2, SEQS])
        not_before = [st.sb(f"not_before{i}", [P, GB, TOK]) for i in range(2)]
        path_sb = [st.sb(f"path{i}", [P, GB, TOK]) for i in range(2)]
        raw = st.sb("raw_stats", [P, GB, 6])
        mv = st.sb("mean_var", [P, GB, 2])
        var_eps = st.sb("var_eps", [P, GB])
        rstd = st.sb("rstd", [P, GB])
        xn = st.sb("xn", [P, GB, DIM])
        xq = st.sb("xq", [P, GB, DIM], BF16)
        amax = st.sb("x_absmax", [P, GB])
        inv1 = st.sb("x_inv", [P, GB])
        q1 = st.sb("x_scale", [P, GB])
        xqT = [st.sb(f"xqT{i}", [P, KD, GB * TOK], BF16) for i in range(2)]
        inv1_b = [st.sb(f"x_inv_b{i}", [P, GB * TOK]) for i in range(2)]
        h = [st.sb(f"h{i}", [P, GB, TOK]) for i in range(3)]
        acc = [st.sb(f"acc{i}", [P, GB, TOK]) for i in range(3)]
        act_h = [st.sb(f"act_h{i}", [P, TILES, GB * TOK]) for i in range(2)]
        hmax = st.sb("h_absmax_part", [P, GB * TOK])
        amax2 = st.sb("h_absmax", [P, GB])
        inv2 = [st.sb(f"h_inv{i}", [P, GB]) for i in range(2)]
        q2 = st.sb("h_scale", [P, GB])
        q2_b = st.sb("h_scale_b", [P, GB * TOK])
        hq = st.sb("hq", [P, TILES, GB * TOK], BF16)
        x_out = [st.sb(f"x_out{i}", [P, GB, DIM]) for i in range(2)]
        ex_ps = st.bank("expand")
        t_ps = st.bank("turned", BF16)
        b_ps = st.bank("broadcast")
        h_ps = [st.bank(f"h_ps{i}") for i in range(3)]
        o_ps = [st.bank(f"out_ps{i}") for i in range(2)]

        w_lane = st.lane("weight_load")
        sp.dma(nc.sync.dma_start, w_lane, w_sb[:, 0, :].rearrange("p (k n) -> p k n", k=KD),
               w1T.rearrange("(k p) n -> p k n", p=P))
        sp.dma(nc.sync.dma_start, w_lane, w_sb[:, 1, :].rearrange("p (m n) -> p m n", m=TILES),
               w2T.rearrange("(m p) n -> p m n", p=P))
        sp.dma(nc.sync.dma_start, w_lane, cw[:, :, :], conv_w)
        w_in = sp.dma(nc.sync.dma_start, w_lane, cb[:, :], conv_b)
        pool.do(nc.gpsimd.memset, ones[:, :], 1.0)
        const = pool.do(nc.gpsimd.tensor_copy, ident_b[:, :], ident[:, :]).mark()
        dve.wait(w_in)
        for n in range(2):
            dve.do(nc.vector.tensor_reduce, absum[:, n:n + 1], w_sb[:, n, :], AX.X, ALU.add,
                   apply_absolute_value=True)
        summed = dve.mark()
        pe.wait(summed, const)
        total = pe.do(nc.tensor.matmul, b_ps[:, 0:2], ones[:, :], absum[:, :], start=True, stop=True).mark()
        dve.wait(total)
        mean = dve.do(nc.vector.tensor_scalar, w_mean[:, :], b_ps[:, 0:2], 1.0 / (DIM * CONV_HID), 1e-5,
                      ALU.mult, ALU.max).mark()
        b_free = [mean]
        dve.wait(mean)
        r = dve.do(nc.vector.reciprocal, w_inv[:, :], w_mean[:, :]).mark()
        dve.wait(r)
        for n, dst in enumerate((w1q[:, :, :].rearrange("p k n -> p (k n)"),
                                 w2q[:, :, :].rearrange("p m n -> p (m n)"))):
            w = w_sb[:, n, :]
            r = dve.do(nc.vector.tensor_scalar, w, w, w_inv[:, n:n + 1], ROUND, ALU.mult, ALU.add).mark()
            dve.wait(r)
            r = dve.do(nc.vector.tensor_scalar, w, w, ROUND, 1.0, ALU.subtract, ALU.min).mark()
            dve.wait(r)
            w_quant = dve.do(nc.vector.tensor_scalar, dst, w, -1.0, None, ALU.max).mark()

        load = [st.lane(f"load{i}") for i in range(2)]
        store = [st.lane(f"store{i}") for i in range(2)]
        landed, expanded, x_added, quantised, xq_turned, xq_ready, bc1 = {}, {}, {}, {}, {}, {}, {}
        xn_norm, inv1_ready = {}, {}
        t_free = [None]
        made, h_read, conv_done, silu_done, x_used = {}, {}, {}, {}, {}
        mid = {}
        maxed, max_turned, q2_ready, hq_ready, out_made, finished, stored = {}, {}, {}, {}, {}, {}, {}
        hmax_read, q2b_ready, inv2_ready = {}, {}, {}

        ramp = pool.do(nc.gpsimd.iota, column[:, :], pattern=[[1, TOK]], base=0, channel_multiplier=0,
                       allow_small_or_imprecise_dtypes=True).mark()
        for n in range(2):
            pe.do(nc.tensor.transpose, ex_ps[:, n * SEQS:(n + 1) * SEQS], entries[:, 1 - n:1 - n + TOK],
                  ident[0:SEQS, 0:SEQS])
        bounds_made = pe.mark()
        act.wait(bounds_made)
        bounds_ready = act.do(nc.scalar.copy, bounds[:, :, :],
                              ex_ps[:, 0:2 * SEQS].rearrange("p (a b) -> p a b", a=2)).mark()
        from_left, path_made = {}, {}

        def make_path(g):
            s = g % 2
            if g >= 2:
                sp.wait(expanded[g - 2])
                pool.wait(path_made[g - 2])
            landed[g] = sp.dma(nc.sync.dma_start, load[s], ctx_sb[s][:, :, :],
                               ctx[GB * g:GB * g + GB].rearrange("b t d -> t b d"))
            pool.wait(bounds_ready, ramp)
            for i in range(GB):
                pool.do(nc.gpsimd.tensor_scalar, not_before[s][:, i, :], column[:, :],
                        bounds[:, 1, GB * g + i:GB * g + i + 1], None, ALU.is_ge)
            from_left[g] = pool.mark()
            dve.wait(from_left[g], bounds_ready)
            if g >= 2:
                dve.wait(expanded[g - 2])
            for i in range(GB):
                dve.do(nc.vector.scalar_tensor_tensor, path_sb[s][:, i, :], column[:, :],
                       bounds[:, 0, GB * g + i:GB * g + i + 1], not_before[s][:, i, :], ALU.is_le, ALU.mult)
            path_made[g] = dve.mark()

        def expand(g):
            s = g % 2
            pe.wait(landed[g], path_made[g], bounds_ready)
            for p2 in range(2):
                if (g, p2) != (0, 0):
                    pe.wait(x_added['last'])
                for i in range(2):
                    pe.do(nc.tensor.matmul, ex_ps[:, i * DIM:(i + 1) * DIM], path_sb[s][:, 2 * p2 + i, :],
                          ctx_sb[s][:, 2 * p2 + i, :], start=True, stop=True)
                expanded[g] = pe.mark()
                dve.wait(expanded[g])
                xs = x_all[:, GB * g + 2 * p2:GB * g + 2 * p2 + 2, :].rearrange("p b d -> p (b d)")
                x_added['last'] = dve.do(nc.vector.tensor_tensor, xs, xs, ex_ps[:, :], ALU.add).mark()
            x_added[g] = x_added['last']

        r_rstd = {}

        def quant_a(g):
            xs = [x_all[:, GB * g + i, :] for i in range(GB)]
            dve.wait(x_added[g])
            got = stats(st, xs, raw, mv)
            r_rstd[g] = rsqrt_var(st, mv, var_eps[:, :], rstd[:, :], half, GB, (got,))

        def quant_b(g):
            V = nc.vector
            xs = [x_all[:, GB * g + i, :] for i in range(GB)]
            one = normalise(st, [xn[:, i, :] for i in range(GB)], xs, mv, rstd, (r_rstd[g],))
            dve.wait(one)
            if g:
                dve.wait(inv1_ready[g - 1])
            r = dve.do(V.tensor_reduce, amax[:, :], xn[:, :, :], AX.X, ALU.max, apply_absolute_value=True).mark()
            dve.wait(r)
            r = dve.do(V.tensor_scalar, inv1[:, :], amax[:, :], 1e-5, 1.0 / 127.0, ALU.max, ALU.mult).mark()
            xn_norm[g] = r
            dve.wait(r)
            r = dve.do(V.reciprocal, q1[:, :], inv1[:, :]).mark()
            dve.wait(r)

        def quant_c(g):
            V = nc.vector
            for i in range(GB):
                dve.do(V.tensor_scalar, xn[:, i, :], xn[:, i, :], q1[:, i:i + 1], ROUND, ALU.mult, ALU.add)
            r = dve.mark()
            dve.wait(r)
            if g:
                dve.wait(xq_turned[g - 1])
            quantised[g] = dve.do(V.tensor_scalar, xq[:, :, :], xn[:, :, :], ROUND, 127.0,
                                  ALU.subtract, ALU.min).mark()

        def turn(g):
            s = g % 2
            pe.wait(quantised[g], const)
            if t_free[0]:
                pe.wait(t_free[0])
            for k in range(KD):
                for i in range(GB):
                    pe.do(nc.tensor.transpose, t_ps[:, (k * GB + i) * P:(k * GB + i + 1) * P],
                          xq[:, i, k * P:(k + 1) * P], ident_b[:, :])
            xq_turned[g] = pe.mark()
            act.wait(xq_turned[g])
            if g >= 2:
                act.wait(x_used[g - 2])
            t_free[0] = xq_ready[g] = act.do(nc.scalar.copy, xqT[s][:, :, :],
                                             t_ps[:, :].rearrange("p (k t) -> p k t", k=KD)).mark()
            pe.wait(xn_norm[g], b_free[0])
            for i in range(GB):
                pe.do(nc.tensor.transpose, b_ps[:, i * TOK:(i + 1) * TOK],
                      inv1[:, i:i + 1].broadcast_to([P, P]), ident[:, :])
            inv1_ready[g] = pe.mark()
            act.wait(inv1_ready[g], mean)
            if g >= 2:
                act.wait(h_read[(g - 2) * TILES + TILES - 1])
            b_free[0] = bc1[g] = act.do(nc.scalar.activation, inv1_b[s][:, :], b_ps[:, :], ACT.Copy,
                                        scale=w_mean[:, 0:1]).mark()

        def hidden(n):
            g, m = divmod(n, TILES)
            s, r = g % 2, n % 3
            ps = h_ps[n % 3]
            pe.wait(xq_ready[g], w_quant)
            if n >= 3:
                pe.wait(h_read[n - 3])
            for k in range(KD):
                pe.do(nc.tensor.matmul, ps[:, :], w1q[:, k, m * P:(m + 1) * P], xqT[s][:, k, :],
                      start=k == 0, stop=k == KD - 1)
            made[n] = pe.mark()
            if m == TILES - 1:
                x_used[g] = made[n]
            dve.wait(made[n], bc1[g])
            if n >= 3:
                dve.wait(conv_done[n - 3])
            h_read[n] = dve.do(nc.vector.tensor_tensor, h[r][:, :, :],
                               ps[:, :].rearrange("p (b t) -> p b t", b=GB),
                               inv1_b[s][:, :].rearrange("p (b t) -> p b t", b=GB), ALU.mult).mark()
            act.wait(h_read[n])
            if n >= 3:
                act.wait(silu_done[n - 3])
            mid[n] = act.do(nc.scalar.activation, acc[r][:, :, :], h[r][:, :, :], ACT.Identity,
                            scale=cw[:, m, 1:2], bias=cb[:, m:m + 1]).mark()

        def taps(n):
            g, m = divmod(n, TILES)
            s, r = g % 2, n % 3
            dve.wait(mid[n])
            one = dve.do(nc.vector.scalar_tensor_tensor, acc[r][:, :, 1:], h[r][:, :, 0:TOK - 1],
                         cw[:, m, 0:1], acc[r][:, :, 1:], ALU.mult, ALU.add).mark()
            dve.wait(one)
            conv_done[n] = dve.do(nc.vector.scalar_tensor_tensor, acc[r][:, :, 0:TOK - 1], h[r][:, :, 1:],
                                  cw[:, m, 2:3], acc[r][:, :, 0:TOK - 1], ALU.mult, ALU.add).mark()
            act.wait(conv_done[n])
            if g >= 2:
                act.wait(hq_ready[g - 2, TILES - 1])
            silu_done[n] = act.do(nc.scalar.activation,
                                  act_h[s][:, m, :].rearrange("p (b t) -> p b t", b=GB),
                                  acc[r][:, :, :], ACT.Silu).mark()

        def hidden_max(g, part):
            s = g % 2
            cols = slice(part * 2 * TOK, (part + 1) * 2 * TOK)
            dve.wait(silu_done[g * TILES + TILES - 1])
            if g:
                dve.wait(max_turned[g - 1])
            maxed[g] = dve.do(nc.vector.tensor_reduce, hmax[:, cols],
                              act_h[s][:, :, cols].rearrange("p m t -> p t m"), AX.X, ALU.max,
                              apply_absolute_value=True).mark()

        def hidden_scale(g):
            s = g % 2
            V = nc.vector
            pe.wait(maxed[g], b_free[0])
            for i in range(GB):
                pe.do(nc.tensor.transpose, b_ps[:, i * TOK:(i + 1) * TOK], hmax[:, i * TOK:(i + 1) * TOK],
                      ident[:, :])
            max_turned[g] = pe.mark()
            dve.wait(max_turned[g])
            b_free[0] = r = dve.do(V.tensor_reduce, amax2[:, :], b_ps[:, :].rearrange("p (b t) -> p b t", b=GB),
                                   AX.X, ALU.max).mark()
            dve.wait(r)
            r = dve.do(V.tensor_scalar, amax2[:, :], amax2[:, :], 1e-5, 1.0 / 127.0, ALU.max, ALU.mult).mark()
            dve.wait(r)
            if g:
                dve.wait(q2_ready[g - 1, 'turned'])
            if g >= 2:
                dve.wait(finished[g - 2])
            dve.do(V.tensor_scalar, inv2[s][:, :], amax2[:, :], w_mean[:, 1:2], None, ALU.mult)
            q2_ready[g] = inv2_ready[g] = dve.do(V.reciprocal, q2[:, :], amax2[:, :]).mark()
            dve.wait(q2_ready[g])

        def spread_scale(g):
            pe.wait(q2_ready[g], b_free[0])
            for i in range(GB):
                pe.do(nc.tensor.transpose, b_ps[:, i * TOK:(i + 1) * TOK], q2[:, i:i + 1].broadcast_to([P, P]),
                      ident[:, :])
            q2_ready[g, 'turned'] = pe.mark()
            act.wait(q2_ready[g, 'turned'])
            if g:
                act.wait(*q2b_used[g - 1])
            b_free[0] = q2b_ready[g] = act.do(nc.scalar.copy, q2_b[:, :], b_ps[:, :]).mark()

        scaled, rounded, q2b_used = {}, {}, {}

        def scale_tile(g, m):
            t = act_h[g % 2][:, m, :]
            q, mul = (dve, nc.vector.tensor_tensor) if m in ON_VECTOR else (pool, nc.gpsimd.tensor_tensor)
            q.wait(q2b_ready[g])
            scaled[g, m] = q.do(mul, t, t, q2_b[:, :], ALU.mult).mark()
            q2b_used.setdefault(g, []).append(scaled[g, m])
            act.wait(scaled[g, m])
            rounded[g, m] = act.do(nc.scalar.activation, t, t, ACT.Copy, bias=ROUND).mark()

        def quant_tile(g, m):
            dve.wait(rounded[g, m])
            if g:
                dve.wait(out_made[g - 1])
            hq_ready[g, m] = dve.do(nc.vector.tensor_scalar, hq[:, m, :], act_h[g % 2][:, m, :], ROUND, 127.0,
                                    ALU.subtract, ALU.min).mark()

        def output(g):
            s = g % 2
            pe.wait(*[hq_ready[g, m] for m in range(TILES)])
            if g:
                pe.wait(finished[g - 1])
            for i in range(GB):
                for m in range(TILES):
                    pe.do(nc.tensor.matmul, o_ps[i // 2][:, (i % 2) * DIM:(i % 2 + 1) * DIM],
                          hq[:, m, i * TOK:(i + 1) * TOK], w2q[:, m, :], start=m == 0, stop=m == TILES - 1)
            out_made[g] = pe.mark()
            dve.wait(out_made[g], inv2_ready[g])
            if g >= 2:
                dve.wait(stored[g - 2])
            for i in range(GB):
                dve.do(nc.vector.scalar_tensor_tensor, x_out[s][:, i, :],
                       o_ps[i // 2][:, (i % 2) * DIM:(i % 2 + 1) * DIM], inv2[s][:, i:i + 1],
                       x_all[:, GB * g + i, :], ALU.mult, ALU.add)
            finished[g] = dve.mark()
            sp.wait(finished[g])
            stored[g] = sp.dma(nc.sync.dma_start, store[s], out[GB * g:GB * g + GB].rearrange("b t d -> t b d"),
                               x_out[s][:, :, :])

        make_path(0)
        expand(0)
        quant_a(0)
        quant_b(0)
        quant_c(0)
        turn(0)
        for n in range((NG + 2) * TILES):
            g, m = divmod(n, TILES)
            if n < NG * TILES:
                hidden(n)
            if 1 <= n <= NG * TILES:
                taps(n - 1)
            if g + 1 < NG:
                if m == 0:
                    make_path(g + 1)
                if m == 1:
                    expand(g + 1)
                if m == 2:
                    quant_a(g + 1)
                if m == 3:
                    quant_b(g + 1)
                if m == 4:
                    quant_c(g + 1)
                if m == 5:
                    turn(g + 1)
            if 1 <= g <= NG:
                if m in (0, 1):
                    if m == 0:
                        hidden_max(g - 1, 0)
                    else:
                        hidden_max(g - 1, 1)
                        hidden_scale(g - 1)
                if m == 2:
                    spread_scale(g - 1)
                for j, slot in enumerate((3, 3, 4, 4, 5, 5, 6, 6)):
                    if m == slot:
                        scale_tile(g - 1, j)
                    if m == slot + 1:
                        quant_tile(g - 1, j)
            if m == 0 and 2 <= g <= NG + 1:
                output(g - 2)
        sp.wait(*stored.values())


def build(nc, x, ctx, ctxT, wq, wkv, wo, ln_cols, router, bias, gate, up, down, s_gate, s_up, s_down,
          w1T, w2T, conv_w, conv_b, out):
    dist = nc.dram_tensor("dist", (SEQS, TOK, TOK), F32, kind="Internal").ap()
    with nc.sbuf_tensor("x_all", [P, SEQS, DIM], F32) as x_all, \
            nc.sbuf_tensor("ident", [P, P], F32) as ident, nc.sbuf_tensor("minus_half", [P, 4], F32) as half, \
            nc.sbuf_tensor("path_entries", [SEQS, TOK + 1], F32) as entries:
        attention(nc, x_all, ident, half, x, ctx, wq, wkv, wo, ln_cols)
        experts(nc, x_all, ident, half, router, bias, gate, up, down, s_gate, s_up, s_down)
        distances(nc, x_all, ident, half, ctx, ctxT, dist)
        align(nc, dist, entries)
        conv_ffn(nc, x_all, ident, half, ctx, entries, w1T, w2T, conv_w, conv_b, out)


def kernel(**inputs):
    import concourse.bacc as bacc
    from concourse.bass_utils import run_bass_kernel_spmd

    a = {n: np.asarray(v) for n, v in inputs.items()}
    tiles = CONV_HID // P
    arrays = {
        "x": a["x"],
        "ctx": a["ctx_1024"],
        "ctxT": a["ctx_1024"].transpose(0, 2, 1),
        "wq": a["L0_xattn_Wq"],
        "wkv": a["L0_xattn_Wkv"],
        "wo": a["L0_xattn_Wo"],
        "ln_cols": np.stack([a["L0_xattn_ln1_w"], a["L0_xattn_ln1_b"], a["L0_xattn_ln2_w"],
                             a["L0_xattn_ln2_b"]]).reshape(4, KD, P).transpose(2, 0, 1),
        "router": a["L0_ffn_router_w"].T,
        "bias": np.broadcast_to(a["L0_ffn_correction_bias"], (P, EXPERTS)),
        "gate": a["L0_ffn_gate_w"].transpose(1, 0, 2).reshape(DIM, ROUTED),
        "up": a["L0_ffn_up_w"].transpose(1, 0, 2).reshape(DIM, ROUTED),
        "down": a["L0_ffn_down_w"].reshape(ROUTED, DIM),
        "s_gate": a["L0_ffn_shared_gate_w"].T,
        "s_up": a["L0_ffn_shared_up_w"].T,
        "s_down": a["L0_ffn_shared_down_w"].T,
        "w1T": a["L1_ffn_w1"].T,
        "w2T": a["L1_ffn_w2"].T,
        "conv_w": a["L1_ffn_conv_w"].reshape(tiles, P, 3).transpose(1, 0, 2),
        "conv_b": a["L1_ffn_conv_b"].reshape(tiles, P).T,
    }
    arrays = {f"in_{n}": np.ascontiguousarray(v) for n, v in arrays.items()}
    nc = bacc.Bacc("TRN2", target_bir_lowering=False, num_devices=1)
    args = [nc.dram_tensor(n, v.shape, mybir.dt.from_np(v.dtype), kind="ExternalInput").ap()
            for n, v in arrays.items()]
    out = nc.dram_tensor("out", (SEQS, TOK, DIM), F32, kind="ExternalOutput").ap()
    build(nc, *args, out)
    r = run_bass_kernel_spmd(nc, [arrays], core_ids=[0])
    return r.results[0]["out"]
```

```python
from contextlib import ExitStack

import numpy as np

from concourse import mybir

F32 = mybir.dt.float32
F32R = mybir.dt.float32r
BF16 = mybir.dt.bfloat16
ALU = mybir.AluOpType
ACT = mybir.ActivationFunctionType
AX = mybir.AxisListType

P = 128
SEQS, TOK, DIM = 64, 128, 256
KD = DIM // P
HEADS, HEAD = 16, 64
INNER = HEADS * HEAD
EXPERTS, HID, SHARED = 16, 64, 512
ROUTED = EXPERTS * HID
GROUPS, PICK_GROUPS, PICK = 4, 2, 4
CONV_HID = 1024
EPS = 1e-5
BIG = 1e30
ROUND = 1.5 * 2.0 ** 23
GB = 4
NG = SEQS // GB


class Queue:

    def __init__(self, sem):
        self.sem, self.count, self.items, self.known = sem, 0, [], {}

    def do(self, build, *args, **kwargs):
        self.items.append([build, args, kwargs, None])
        return self

    def mark(self):
        self.count += 1
        self.items[-1][3] = (self.sem, 1)
        return (self.sem, self.count)

    def wait(self, *counts):
        for sem, value in counts:
            if self.known.get(sem.name, 0) < value:
                self.known[sem.name] = value
                self.items.append([None, (sem, value), None, None])
        return self

    def dma(self, build, lane, out, in_):
        lane[1] += 16
        self.items.append([build, (out, in_), {}, (lane[0], 16)])
        return (lane[0], lane[1])

    def replay(self, engine):
        for build, args, kwargs, inc in self.items:
            if build is None:
                engine.wait_ge(*args)
            else:
                made = build(*args, **kwargs)
                if inc:
                    made.then_inc(*inc)


class Stage:

    def __init__(self, nc, name):
        self.nc, self.name, self.ctx = nc, name, ExitStack()

    def __enter__(self):
        self.pe, self.act, self.dve, self.pool, self.sp = (
            Queue(self.sem(n)) for n in ("pe", "act", "dve", "pool", "sp"))
        return self

    def sem(self, n):
        return self.ctx.enter_context(self.nc.semaphore(f"{self.name}_{n}_done"))

    def lane(self, n):
        return [self.sem(n), 0]

    def sb(self, n, shape, dt=F32):
        return self.ctx.enter_context(self.nc.sbuf_tensor(f"{self.name}_{n}", shape, dt))

    def bank(self, n, dt=F32):
        return self.ctx.enter_context(
            self.nc.psum_tensor(f"{self.name}_{n}", [P, 2048 // mybir.dt.size(dt)], dt))

    def __exit__(self, kind, *rest):
        if kind is None:
            with self.nc.Block() as block:
                block.sync(self.sp.replay)
                block.tensor(self.pe.replay)
                block.scalar(self.act.replay)
                block.vector(self.dve.replay)
                block.gpsimd(self.pool.replay)
        return self.ctx.__exit__(kind, *rest)


def split_weight(st, lane, stage, stage_free, src, hi, lo):
    nc = st.nc
    st.sp.wait(*stage_free)
    landed = st.sp.dma(nc.sync.dma_start, lane, stage, src)
    st.dve.wait(landed)
    high = st.dve.do(nc.vector.tensor_copy, hi, stage).mark()
    st.dve.wait(high)
    return st.dve.do(nc.vector.tensor_tensor, lo, stage, hi.bitcast(F32), ALU.subtract).mark()


def rsqrt_var(st, mv, var_eps, rstd, half, n, ready, free=()):
    nc = st.nc
    st.pool.wait(*ready, *free)
    a = st.pool.do(nc.gpsimd.tensor_scalar, var_eps, mv[:, 0:n, 1], EPS, None, ALU.add).mark()
    st.pool.wait(a)
    return st.pool.do(nc.gpsimd.tensor_tensor, rstd, var_eps, half[:, 0:n], ALU.pow).mark()


def stats(st, tiles, raw, mv):
    nc = st.nc
    for n, t in enumerate(tiles):
        st.dve.do(nc.vector.bn_stats, raw[:, n, :], t)
    done = st.dve.mark()
    st.dve.wait(done)
    for n in range(len(tiles)):
        st.dve.do(nc.vector.bn_aggr, mv[:, n, :], raw[:, n, :])
    return st.dve.mark()


def normalise(st, outs, tiles, mv, rstd, ready):
    nc = st.nc
    st.dve.wait(*ready)
    for n, t in enumerate(tiles):
        st.dve.do(nc.vector.tensor_scalar, outs[n], t, mv[:, n, 0:1], rstd[:, n:n + 1],
                  ALU.subtract, ALU.mult)
    return st.dve.mark()


def attention(nc, x_all, ident, half, x, ctx, wq, wkv, wo, ln_cols):
    QUADS, QH = 4, HEADS // 4
    QT = QH * HEAD // P
    QW = QH * HEAD
    LAST = SEQS * QUADS
    with Stage(nc, "attention") as st:
        pe, act, dve, pool, sp = st.pe, st.act, st.dve, st.pool, st.sp
        wq_p = [st.sb(f"wq_{n}", [P, KD, INNER], F32R) for n in ("hi", "lo")]
        wkv_p = [st.sb(f"wkv_{n}", [P, KD, 2 * INNER], F32R) for n in ("hi", "lo")]
        wo_p = [st.sb(f"wo_{n}", [P, INNER // P, DIM], F32R) for n in ("hi", "lo")]
        cols = st.sb("ln_cols", [P, 4, KD])
        ctx_sb = st.sb("ctx", [P, 2, DIM])
        lat = st.sb("latents", [P, 2, DIM])
        raw = st.sb("raw_stats", [P, 4, 6])
        mv = [st.sb(f"mean_var{i}", [P, 4, 2]) for i in range(2)]
        var_eps = [st.sb(f"var_eps{i}", [P, 4]) for i in range(2)]
        rstd = [st.sb(f"rstd{i}", [P, 4]) for i in range(2)]
        kv_full = [st.sb(f"kv_full{i}", [P, 2, TOK]) for i in range(KD)]
        kv_hi = [st.sb(f"kv_hi{i}", [P, KD, 2, 2, TOK], F32R) for i in range(2)]
        kv_lo = [st.sb(f"kv_lo{i}", [P, KD, 2, 2, TOK], F32R) for i in range(2)]
        q_hi, q_lo = ([st.sb(f"q_{n}{i}", [P, QT, 2, TOK], F32R) for i in range(2)] for n in ("hi", "lo"))
        k_hi, k_lo = ([st.sb(f"k_{n}{i}", [P, QT, 2 * TOK], F32R) for i in range(2)] for n in ("hi", "lo"))
        v = [st.sb(f"v{i}", [P, 2, QH, 2, HEAD], F32R) for i in range(3)]
        prob = st.sb("prob", [P, QH, 2 * TOK])
        probT_hi, probT_lo = (st.sb(f"probT_{n}", [P, QH, 2, TOK], F32R) for n in ("hi", "lo"))
        neg_max = st.sb("neg_max", [P, 2, QH])
        sums = st.sb("row_sums", [P, 2, QH])
        inv = st.sb("inv_sums", [P, 2, QH])
        attT_hi, attT_lo = (st.sb(f"attT_{n}", [P, 2, INNER // P, TOK], F32R) for n in ("hi", "lo"))
        proj = [st.bank(f"proj{i}") for i in range(3)]
        scores = [st.bank(f"scores{i}") for i in range(2)]
        turned = [st.bank(f"turned{i}") for i in range(2)]
        heads_out = st.bank("heads_out")

        XC = 8
        ctx_lane = st.lane("ctx_load")
        x_in, ctx_in = {}, {}

        def load_x(c):
            x_in[c] = sp.dma(nc.sync.dma_start, st.lane(f"x_load{c}"), x_all[:, XC * c:XC * c + XC, :],
                             x[XC * c:XC * c + XC].rearrange("b t d -> t b d"))

        w_lane = st.lane("column_load")
        load_x(0)
        w_in = sp.dma(nc.sync.dma_start, w_lane, cols[:, :, :], ln_cols)
        pool.do(nc.gpsimd.memset, half[:, :], -0.5)
        zero = pool.do(nc.gpsimd.memset, ident[:, :], 0.0).mark()
        pool.wait(zero)
        const = pool.do(nc.gpsimd.affine_select, out=ident[:, :], in_=ident[:, :],
                        compare_op=ALU.not_equal, fill=1.0, base=0, pattern=[[-1, P]],
                        channel_multiplier=1).mark()
        STAGES, PER_STAGE = 4, INNER // DIM
        stage_lane = [st.lane(f"stage_load{i}") for i in range(STAGES)]
        staged = []

        def load_weight(src, hi, lo):
            n = len(staged)
            first = SEQS - (n % STAGES + 1) * PER_STAGE
            buf = x_all[:, first:first + PER_STAGE, :]
            if len(src.shape) == 2:
                buf = buf.rearrange("p m n -> p (m n)")
            free = staged[n - STAGES:n - STAGES + 1] if n >= STAGES else ()
            staged.append(split_weight(st, stage_lane[n % STAGES], buf, free, src, hi, lo))

        r_one, turned_in, normed, kv_ready, kv_used = {}, {}, {}, {}, {}
        q_ready, k_ready, v_ready = {}, {}, {}
        score_done, max_done, exp_done, t_done, t_split, pv_done = {}, {}, {}, {}, {}, {}
        divided, att_read, out_made = {}, {}, {}
        proj_free, n_proj, banks = {}, [0], {}

        def take_proj():
            i = n_proj[0] % len(proj)
            n_proj[0] += 1
            if i in proj_free:
                pe.wait(proj_free[i])
            return i, proj[i]

        def load_ctx(p):
            if p:
                sp.wait(turned_in[2 * p - 2], turned_in[2 * p - 1])
            ctx_in[p] = sp.dma(nc.sync.dma_start, ctx_lane, ctx_sb[:, :, :],
                               ctx[2 * p:2 * p + 2].rearrange("b t d -> t b d"))

        def pair(p):
            return ([x_all[:, 2 * p + e, :] for e in range(2)], [ctx_sb[:, e, :] for e in range(2)],
                    [lat[:, e, :] for e in range(2)])

        def norm_a(p):
            xs, cs, ls = pair(p)
            dve.wait(x_in[2 * p // XC], ctx_in[p])
            got = stats(st, xs + cs, raw, mv[0])
            r_one[p] = rsqrt_var(st, mv[0], var_eps[0][:, :], rstd[0][:, :], half, 4, (got, const))

        def norm_b(p):
            xs, cs, ls = pair(p)
            if p:
                dve.wait(turned_in[2 * p - 1])
            one = normalise(st, ls + cs, xs + cs, mv[0], rstd[0], (r_one[p],))
            dve.wait(one)
            got = stats(st, ls, raw, mv[1])
            r_one[p] = rsqrt_var(st, mv[1], var_eps[1][:, 0:2], rstd[1][:, 0:2], half, 2, (got,))

        def norm_c(p):
            xs, cs, ls = pair(p)
            normed[p] = normalise(st, ls, ls, mv[1], rstd[1], (r_one[p],))

        def turn_inputs(b):
            p, e = divmod(b, 2)
            at, bank = take_proj()
            pe.wait(normed[p], const)
            view = bank[:, :].rearrange("p (k c t) -> p k c t", k=KD, c=2)
            for k in range(KD):
                for c, src in enumerate((ctx_sb, lat)):
                    pe.do(nc.tensor.transpose, view[:, k, c, :], src[:, e, k * P:(k + 1) * P], ident[:, :])
            turned_in[b] = pe.mark()
            act.wait(turned_in[b], w_in)
            if p >= 2:
                act.wait(kv_used[p - 2])
                pool.wait(kv_used[p - 2])
            banks[b] = at, view

        def split_inputs(b, k):
            p, e = divmod(b, 2)
            at, view = banks[b]
            if b:
                act.wait(kv_ready[b - 1, k])
            for c in range(2):
                act.do(nc.scalar.activation, kv_full[k][:, c, :], view[:, k, c, :], ACT.Identity,
                       scale=cols[:, 2 * c, k:k + 1], bias=cols[:, 2 * c + 1, k:k + 1])
            full = proj_free[at] = act.mark()
            act.wait(full)
            hi = kv_hi[p % 2][:, k, :, e, :]
            high = act.do(nc.scalar.activation, hi, kv_full[k][:, :, :], ACT.Copy).mark()
            pool.wait(high)
            kv_ready[b, k] = kv_ready[b] = pool.do(
                nc.gpsimd.tensor_tensor, kv_lo[p % 2][:, k, :, e, :], kv_full[k][:, :, :], hi.bitcast(F32),
                ALU.subtract).mark()

        def three_pass(out, left, right):
            n = 0
            for k in range(KD):
                for l, r in ((0, 0), (0, 1), (1, 0)):
                    pe.do(nc.tensor.matmul, out, left[l](k), right[r](k), start=n == 0, stop=n == 3 * KD - 1)
                    n += 1

        def split_out(made, view, hi, lo, used, scale):
            act.wait(made, *used)
            high = act.do(nc.scalar.activation, hi, view, ACT.Copy, scale=scale).mark()
            dve.wait(high)
            return dve.do(nc.vector.scalar_tensor_tensor, lo, view, scale, hi.bitcast(F32), ALU.mult,
                          ALU.subtract).mark()

        def columns(w, lo, hi):
            return [lambda k, t=t: t[:, k, lo:hi] for t in w]

        def unit(n):
            return n // (2 * QUADS), n % (2 * QUADS) // 2, n % 2

        def kv_of(p, index):
            return [lambda k, t=t: t[(slice(None), k) + index] for t in (kv_hi[p % 2], kv_lo[p % 2])]

        def project_q(n):
            p, i, e = unit(n)
            u = n // 2
            pe.wait(kv_ready[2 * p + 1], wq_split[i])
            used = [score_done[n - 3]] if n >= 4 else []
            at, bank = take_proj()
            for m in range(QT):
                w = i * QW + m * P
                three_pass(bank[:, m * 2 * TOK:(m + 1) * 2 * TOK], columns(wq_p, w, w + P),
                           kv_of(p, (1,)))
            proj_free[at] = q_ready[u] = split_out(
                pe.mark(), bank[:, :].rearrange("p (m t) -> p m t", m=QT),
                q_hi[u % 2][:, :, :, :].rearrange("p m e t -> p m (e t)"),
                q_lo[u % 2][:, :, :, :].rearrange("p m e t -> p m (e t)"), used, HEAD ** -0.5)

        def project_k(n):
            p, i, e = unit(n)
            at, bank = take_proj()
            pe.wait(kv_ready[2 * p + e], wk_split[i])
            for m in range(QT):
                w = i * QW + m * P
                three_pass(bank[:, m * 2 * TOK:(m + 1) * 2 * TOK], columns(wkv_p, w, w + P),
                           kv_of(p, (slice(None), e)))
            proj_free[at] = k_ready[n] = split_out(
                pe.mark(), bank[:, :].rearrange("p (m t) -> p m t", m=QT), k_hi[n % 2][:, :, :],
                k_lo[n % 2][:, :, :], [score_done[n - 2]] if n >= 2 else [], 1.0)

        def project_v(n):
            p, i, e = unit(n)
            at, bank = take_proj()
            pe.wait(wv_split[i])
            w = INNER + i * QW
            for t in range(2):
                three_pass(bank[:, t * QW:(t + 1) * QW], kv_of(p, (t, e)), columns(wkv_p, w, w + QW))
            made = pe.mark()
            if i == QUADS - 1:
                kv_used[p] = made
            act.wait(made)
            if n >= 3:
                act.wait(pv_done[n - 3])
            view = bank[:, :].rearrange("p (t h c) -> p t h c", t=2, h=QH)
            high = act.do(nc.scalar.activation, v[n % 3][:, :, :, 0, :], view, ACT.Copy).mark()
            dve.wait(high)
            dve.do(nc.vector.tensor_tensor, v[n % 3][:, :, :, 1, :], view,
                   v[n % 3][:, :, :, 0, :].bitcast(F32), ALU.subtract)
            proj_free[at] = v_ready[n] = dve.mark()

        def score(n):
            p, i, e2 = unit(n)
            u = n // 2
            pe.wait(q_ready[u], k_ready[n])
            if n:
                pe.wait(exp_done[n - 1])
            for h in range(QH):
                m, e = divmod(h, 2)
                r = slice(e * HEAD, (e + 1) * HEAD)
                for j, (q_, k_) in enumerate(((q_hi, k_hi), (q_hi, k_lo), (q_lo, k_hi))):
                    pe.do(nc.tensor.matmul, scores[e][:, m * 256:(m + 1) * 256], q_[u % 2][r, m, e2, :],
                          k_[n % 2][r, m, :], start=j == 0, stop=j == 2)
            score_done[n] = pe.mark()

        def row_max(n):
            dve.wait(score_done[n])
            if n >= 2:
                dve.wait(exp_done[n - 2])
            for e in range(2):
                dve.do(nc.vector.tensor_reduce, neg_max[:, n % 2, 2 * e:2 * e + 2],
                       scores[e][:, :].rearrange("p (h c) -> p h c", h=2), AX.X, ALU.max, negate=True)
            max_done[n] = dve.mark()

        def exponentials(n):
            act.wait(max_done[n])
            if n:
                act.wait(t_done[n - 1, 1])
            for h in range(QH):
                m, e = divmod(h, 2)
                act.do(nc.scalar.activation, prob[:, h, :], scores[e][:, m * 256:(m + 1) * 256], ACT.Exp,
                       bias=neg_max[:, n % 2, 2 * e + m:2 * e + m + 1], accum_out=sums[:, n % 2, h:h + 1])
            exp_done[n] = act.mark()

        def divide(n):
            dve.wait(exp_done[n])
            r = dve.do(nc.vector.reciprocal, inv[:, n % 2, :], sums[:, n % 2, :]).mark()
            pool.wait(r)
            dve.wait(r)
            for h in range(QH):
                on, engine = (pool, nc.gpsimd) if h == QH - 1 else (dve, nc.vector)
                on.do(engine.tensor_scalar, prob[:, h, :], prob[:, h, :], inv[:, n % 2, h:h + 1], None, ALU.mult)
            divided[n] = (dve.mark(), pool.mark())

        def turn_probs(n):
            pe.wait(*divided[n])
            for g in range(2):
                if n:
                    pe.wait(t_split[n - 1, g])
                for h in range(2):
                    for t in range(2):
                        pe.do(nc.tensor.transpose, turned[g][:, (2 * h + t) * P:(2 * h + t + 1) * P],
                              prob[:, 2 * g + h, t * P:(t + 1) * P], ident[:, :])
                t_done[n, g] = pe.mark()

        def split_probs(n):
            for g in range(2):
                flat = [t[:, 2 * g:2 * g + 2].rearrange("p h t c -> p (h t c)") for t in (probT_hi, probT_lo)]
                t_split[n, g] = split_out(t_done[n, g], turned[g][:, :], *flat, [pv_done[n - 1]] if n else [], 1.0)

        def weigh_values(n):
            pe.wait(t_split[n, 0], t_split[n, 1], v_ready[n])
            if n:
                pe.wait(att_read[n - 1])
            for h in range(QH):
                out = heads_out[0:HEAD, h * TOK:(h + 1) * TOK]
                j = 0
                for t in range(2):
                    for part, prob_part in ((0, probT_hi), (1, probT_hi), (0, probT_lo)):
                        pe.do(nc.tensor.matmul, out, v[n % 3][:, t, h, part, :], prob_part[:, h, t, :],
                              start=j == 0, stop=j == 5)
                        j += 1
            pv_done[n] = pe.mark()

        def split_heads(n):
            p, i, e = unit(n)
            act.wait(pv_done[n])
            if p:
                act.wait(out_made[2 * p + e - 2])
            ends = [(heads_out[0:HEAD, :].rearrange("p (m o t) -> p m o t", o=2, t=TOK)[:, :, o, :],
                     *(t[o * HEAD:(o + 1) * HEAD, e, QT * i:QT * i + QT, :] for t in (attT_hi, attT_lo)))
                    for o in range(2)]
            for view, hi, lo in ends:
                act.do(nc.scalar.activation, hi, view, ACT.Copy)
            high = act.mark()
            dve.wait(high)
            for view, hi, lo in ends:
                dve.do(nc.vector.tensor_tensor, lo, view, hi.bitcast(F32), ALU.subtract)
            att_read[n] = dve.mark()

        def output(b):
            e = b % 2
            pe.wait(att_read[b // 2 * 2 * QUADS + 2 * (QUADS - 1) + e], wo_split)
            at, bank = take_proj()
            n = 0
            for m in range(INNER // P):
                for l, r in ((attT_hi, 0), (attT_hi, 1), (attT_lo, 0)):
                    pe.do(nc.tensor.matmul, bank[:, 0:DIM], l[:, e, m, :], wo_p[r][:, m, :],
                          start=n == 0, stop=n == 3 * INNER // P - 1)
                    n += 1
            out_made[b] = pe.mark()
            dve.wait(out_made[b])
            proj_free[at] = dve.do(nc.vector.tensor_tensor, x_all[:, b, :], x_all[:, b, :],
                                   bank[:, 0:DIM], ALU.add).mark()

        load_ctx(0)
        norm_a(0)
        norm_b(0)
        norm_c(0)

        def load_block(src, dst, c, width):
            for k in range(KD):
                w = slice(c, c + width)
                load_weight(src[k * P:(k + 1) * P, w], dst[0][:, k, w], dst[1][:, k, w])
            return staged[-1]

        for b in range(2):
            turn_inputs(b)

        def split_part(n):
            split_inputs(n // 2, n % 2)

        for n in range(2):
            split_part(n)
        wq_split = [load_block(wq, wq_p, 0, INNER)] * QUADS
        for n in range(2, 4):
            split_part(n)
        wk_split = [load_block(wkv, wkv_p, 0, INNER)] * QUADS
        wv_split = [load_block(wkv, wkv_p, INNER, INNER)] * QUADS
        wo_v = wo.rearrange("(m p) n -> p m n", p=P)
        FREE_XC = (SEQS - STAGES * PER_STAGE) // XC
        for c in range(1, FREE_XC):
            load_x(c)
        load_ctx(1)
        project_q(0)
        project_k(0)
        project_v(0)
        for n in range(LAST + 4):
            p, i, e = unit(n)
            slot = 2 * i + e
            if n == 1:
                for m in range(0, INNER // P, 4):
                    load_weight(wo_v[:, m:m + 4, :], wo_p[0][:, m:m + 4, :], wo_p[1][:, m:m + 4, :])
                wo_split = staged[-1]
                sp.wait(wo_split)
                for c in range(FREE_XC, SEQS // XC):
                    load_x(c)
            if n < LAST:
                score(n)
                row_max(n)
            if n + 1 < LAST:
                project_k(n + 1)
                if e == 1:
                    project_q(n + 1)
            if 1 <= n <= LAST:
                turn_probs(n - 1)
            if 2 <= n <= LAST + 1:
                weigh_values(n - 2)
            if n < LAST:
                exponentials(n)
                divide(n)
            if 1 <= n <= LAST:
                split_probs(n - 1)
            if 2 <= n <= LAST + 1:
                split_heads(n - 2)
            late = 2 * p + 2 + (slot - 3) // 2 if p + 1 < SEQS // 2 and slot in (3, 5) else None
            if late is not None:
                turn_inputs(late)
                for k in range(KD):
                    split_inputs(late, k)
            if n + 1 < LAST:
                project_v(n + 1)
            if p and slot in (1, 2):
                output(2 * p - 2 + slot - 1)
            if p + 1 < SEQS // 2:
                if slot == 0:
                    norm_a(p + 1)
                if slot == 1:
                    norm_b(p + 1)
                if slot == 2:
                    norm_c(p + 1)
                if slot == 6 and p + 2 < SEQS // 2:
                    load_ctx(p + 2)


def experts(nc, x_all, ident, half, router, bias, gate, up, down, s_gate, s_up, s_down):
    TILES = ROUTED // P
    STILES = SHARED // P
    with Stage(nc, "experts") as st:
        pe, act, dve, pool, sp = st.pe, st.act, st.dve, st.pool, st.sp
        gate_w = [st.sb(f"gate_{n}", [P, KD, ROUTED + SHARED], F32R) for n in ("hi", "lo")]
        up_w = [st.sb(f"up_{n}", [P, KD, ROUTED + SHARED], F32R) for n in ("hi", "lo")]
        down_w = [st.sb(f"down_{n}", [P, TILES + STILES, DIM], F32R) for n in ("hi", "lo")]
        router_w = st.sb("router", [P, KD, EXPERTS])
        bias_w = st.sb("bias", [P, EXPERTS])
        below = st.sb("below", [P, EXPERTS, EXPERTS])
        xn = st.sb("xn", [P, GB, DIM])
        raw = st.sb("raw_stats", [P, GB, 6])
        mv = st.sb("mean_var", [P, GB, 2])
        var_eps = st.sb("var_eps", [P, GB])
        rstd = st.sb("rstd", [P, GB])
        xT = st.sb("xT", [P, KD, GB * TOK])
        xT_hi = [st.sb(f"xT_hi{i}", [P, KD, GB * TOK], F32R) for i in range(2)]
        xT_lo = [st.sb(f"xT_lo{i}", [P, KD, GB * TOK], F32R) for i in range(2)]
        STAGES = 3
        stage = [st.sb(f"weight_stage{i}", [P, 4 * DIM])[:, :] for i in range(STAGES - 1)]
        select = st.sb("select", [2 * EXPERTS, ROUTED], F32R)
        comb_parts = st.sb("combine_parts", [P, GB, 2, EXPERTS])
        comb_hi = st.sb("combine_hi", [P, GB, EXPERTS], F32R)
        combT = [st.sb(f"combine_turned{i}", [2 * EXPERTS, GB * TOK], F32R) for i in range(2)]
        silu = [st.sb(f"silu{i}", [P, GB * TOK]) for i in range(2)]
        weighed_both = st.sb("weighed", [P, 2, GB * TOK])
        weighed = [weighed_both[:, i, :] for i in range(2)]
        stage.append(weighed_both[:, :, :].rearrange("p s t -> p (s t)"))
        hid_hi = [st.sb(f"hidden_hi{i}", [P, GB * TOK], F32R) for i in range(3)]
        hid_lo = [st.sb(f"hidden_lo{i}", [P, GB * TOK], F32R) for i in range(3)]
        sc, sb_, tmp = (st.sb(n, [P, GB, EXPERTS]) for n in ("score", "biased", "small"))
        pq = st.sb("pair", [P, 2, GB * GROUPS, 2])
        tops = st.sb("tops", [P, 4, GB * GROUPS])
        gs = st.sb("group_score", [P, GB, GROUPS])
        gcmp = st.sb("group_compare", [P, 2, GB, GROUPS, GROUPS])
        gmask = st.sb("group_mask", [P, GB, GROUPS])
        gneg = st.sb("group_neg", [P, GB, GROUPS])
        masked = st.sb("masked", [P, GB, EXPERTS])
        cmp_ge = st.sb("compare_ge", [P, GB, EXPERTS, EXPERTS], BF16)
        cmp_gt = st.sb("compare_gt", [P, GB, EXPERTS, EXPERTS], BF16)
        rank = st.sb("rank", [P, GB, EXPERTS])
        comb = st.sb("combine", [P, GB, EXPERTS])
        wsum = st.sb("weight_sum", [P, 2, GB])
        misc = st.bank("misc")
        g_ps = [st.bank(f"gate{i}") for i in range(2)]
        u_ps = [st.bank(f"up{i}") for i in range(2)]
        c_ps = st.bank("combine_spread")
        out_ps = [st.bank(f"out{i}") for i in range(2)]

        w_lane = st.lane("weight_load")
        for src, dst in ((router.rearrange("(k p) n -> p k n", p=P), router_w[:, :, :]), (bias, bias_w[:, :])):
            w_in = sp.dma(nc.sync.dma_start, w_lane, dst, src)
        ones = pool.do(nc.gpsimd.memset, below[:, :, :], 1.0).mark()
        pool.wait(ones)
        const = pool.do(nc.gpsimd.affine_select, out=below[:, :, :], in_=below[:, :, :],
                        compare_op=ALU.is_gt, fill=0.0, base=0, pattern=[[1, EXPERTS], [-1, EXPERTS]],
                        channel_multiplier=0).mark()
        made_in = xT[0:2 * EXPERTS, :, :].rearrange("p k t -> p (k t)")
        zero = pool.do(nc.gpsimd.memset, made_in, 0.0).mark()
        pool.wait(zero)
        view = made_in.rearrange("p (e h) -> p e h", e=EXPERTS)
        for part in range(2):
            filled = pool.do(nc.gpsimd.affine_select, out=view, in_=view, compare_op=ALU.not_equal, fill=1.0,
                             base=part * EXPERTS, pattern=[[1, EXPERTS], [0, HID]], channel_multiplier=-1).mark()
            pool.wait(filled)
        select_made = pool.do(nc.gpsimd.tensor_copy, select[:, :], made_in).mark()
        stage_lane = [st.lane(f"stage_load{i}") for i in range(STAGES)]
        staged = []
        for src, (hi, lo), at, width in ((gate, gate_w, 0, ROUTED), (up, up_w, 0, ROUTED),
                                         (s_gate, gate_w, ROUTED, SHARED), (s_up, up_w, ROUTED, SHARED)):
            for k in range(KD):
                n = len(staged)
                w = slice(at, at + width)
                staged.append(split_weight(st, stage_lane[n % STAGES], stage[n % STAGES][:, 0:width],
                                           staged[n - STAGES:n - STAGES + 1] if n >= STAGES else (),
                                           src[k * P:(k + 1) * P, :], hi[:, k, w], lo[:, k, w]))
        gate_up_split = staged[-1]
        for src, at, tiles in ((down, 0, TILES), (s_down, TILES, STILES)):
            view = src.rearrange("(m p) n -> p m n", p=P)
            for m in range(0, tiles, 4):
                n = len(staged)
                w = slice(at + m, at + m + 4)
                buf = stage[n % STAGES].rearrange("p (m n) -> p m n", m=4)
                staged.append(split_weight(st, stage_lane[n % STAGES], buf, staged[n - STAGES:n - STAGES + 1],
                                           view[:, m:m + 4, :], down_w[0][:, w, :], down_w[1][:, w, :]))
        w_split = staged[-1]

        normed, x_ready, routed, parts_turned, combT_made = {}, {}, {}, {}, {}
        misc_free = [None]
        full_read = {}
        x_used, xn_used, comb_used, out_added = {}, {}, {}, {}

        def norm(g):
            xs = [x_all[:, GB * g + i, :] for i in range(GB)]
            got = stats(st, xs, raw, mv)
            r = rsqrt_var(st, mv, var_eps[:, :], rstd[:, :], half, GB, (got,))
            if g:
                dve.wait(xn_used[g - 1])
            normed[g] = normalise(st, [xn[:, i, :] for i in range(GB)], xs, mv, rstd, (r,))

        def turn(g, k):
            pe.wait(normed[g])
            if misc_free[0]:
                pe.wait(misc_free[0])
            for i in range(GB):
                pe.do(nc.tensor.transpose, misc[:, i * P:(i + 1) * P], xn[:, i, k * P:(k + 1) * P], ident[:, :])
            xn_used[g] = pe.mark()
            act.wait(xn_used[g], select_made)
            if g:
                act.wait(full_read[g - 1], x_ready[g - 1])
            misc_free[0] = act.do(nc.scalar.copy, xT[:, k, :], misc[:, :]).mark()

        def split_x(g):
            s = g % 2
            act.wait(misc_free[0])
            if g >= 2:
                act.wait(x_used[g - 2])
            high = act.do(nc.scalar.activation, xT_hi[s][:, :, :], xT[:, :, :], ACT.Copy).mark()
            pool.wait(high)
            x_ready[g] = pool.do(nc.gpsimd.tensor_tensor, xT_lo[s][:, :, :], xT[:, :, :],
                                 xT_hi[s][:, :, :].bitcast(F32), ALU.subtract).mark()

        def route_scores(g):
            pe.wait(misc_free[0], w_in)
            for i in range(GB):
                for k in range(KD):
                    pe.do(nc.tensor.matmul, misc[:, i * EXPERTS:(i + 1) * EXPERTS],
                          xT[:, k, i * TOK:(i + 1) * TOK], router_w[:, k, :], start=k == 0, stop=k == KD - 1)
            full_read[g] = pe.mark()
            act.wait(full_read[g])
            if g:
                act.wait(routed[g - 1])
            misc_free[0] = act.do(nc.scalar.activation, tmp[:, :, :],
                                  misc[:, 0:GB * EXPERTS].rearrange("p (b e) -> p b e", b=GB),
                                  ACT.Tanh, scale=0.5).mark()

        def chain(build, *a, **k):
            done = dve.do(build, *a, **k).mark()
            dve.wait(done)
            return done

        def route(g):
            V = nc.vector
            tt, ts = V.tensor_tensor, V.tensor_scalar
            dve.wait(misc_free[0], w_in, const)
            chain(ts, sc[:, :, :], tmp[:, :, :], 0.5, 0.5, ALU.mult, ALU.add)
            chain(tt, sb_[:, :, :], sc[:, :, :], bias_w[:, :].unsqueeze(1).broadcast_to([P, GB, EXPERTS]), ALU.add)
            quad = sb_[:, :, :].rearrange("p b (g a c) -> p (b g) a c", g=GROUPS, a=2)
            dve.do(tt, pq[:, 0, :, :], quad[:, :, :, 0], quad[:, :, :, 1], ALU.max)
            chain(tt, pq[:, 1, :, :], quad[:, :, :, 0], quad[:, :, :, 1], ALU.min)
            dve.do(tt, tops[:, 0, :], pq[:, 0, :, 0], pq[:, 0, :, 1], ALU.max)
            dve.do(tt, tops[:, 1, :], pq[:, 0, :, 0], pq[:, 0, :, 1], ALU.min)
            chain(tt, tops[:, 2, :], pq[:, 1, :, 0], pq[:, 1, :, 1], ALU.max)
            chain(tt, tops[:, 3, :], tops[:, 1, :], tops[:, 2, :], ALU.max)
            chain(tt, gs[:, :, :].rearrange("p b g -> p (b g)"), tops[:, 0, :], tops[:, 3, :], ALU.add)
            yield

            def ranks(value, n, ge, gt, out):
                for i in range(GB):
                    e = value[:, i, :].unsqueeze(2).broadcast_to([P, n, n])
                    j = value[:, i, :].unsqueeze(1).broadcast_to([P, n, n])
                    dve.do(tt, ge[:, i], j, e, ALU.is_ge)
                    last = dve.do(tt, gt[:, i], j, e, ALU.is_gt)
                last = dve.mark()
                dve.wait(last)
                if n == EXPERTS:
                    yield
                for i in range(GB):
                    dve.do(tt, ge[:, i], ge[:, i], below[:, 0:n, 0:n], ALU.mult)
                last = dve.mark()
                dve.wait(last)
                chain(tt, ge, ge, gt, ALU.max)
                chain(V.tensor_reduce, out, ge, AX.X, ALU.add)

            yield from ranks(gs[:, :, :], GROUPS, gcmp[:, 0], gcmp[:, 1], gmask[:, :, :])
            chain(ts, gmask[:, :, :], gmask[:, :, :], PICK_GROUPS - 0.5, None, ALU.is_lt)
            chain(ts, gneg[:, :, :], gmask[:, :, :], 1.0, BIG, ALU.subtract, ALU.mult)
            g4 = lambda t: t[:, :, :].rearrange("p b g -> p (b g)").unsqueeze(2).broadcast_to(
                [P, GB * GROUPS, EXPERTS // GROUPS])
            flat = lambda t: t[:, :, :].rearrange("p b (g c) -> p (b g) c", g=GROUPS)
            chain(tt, flat(masked), flat(sb_), g4(gmask), ALU.mult)
            chain(tt, flat(masked), flat(masked), g4(gneg), ALU.add)
            yield
            yield from ranks(masked[:, :, :], EXPERTS, cmp_ge[:, :], cmp_gt[:, :], rank[:, :, :])
            yield
            chain(ts, rank[:, :, :], rank[:, :, :], PICK - 0.5, None, ALU.is_lt)
            chain(tt, comb[:, :, :], sc[:, :, :], rank[:, :, :], ALU.mult)
            chain(V.tensor_reduce, wsum[:, 0, :], comb[:, :, :], AX.X, ALU.add)
            chain(ts, wsum[:, 0, :], wsum[:, 0, :], 1e-20, None, ALU.add)
            chain(V.reciprocal, wsum[:, 1, :], wsum[:, 0, :])
            chain(tt, comb[:, :, :], comb[:, :, :],
                  wsum[:, 1, :].unsqueeze(2).broadcast_to([P, GB, EXPERTS]), ALU.mult)
            chain(V.tensor_copy, comb_hi[:, :, :], comb[:, :, :])
            if g:
                dve.wait(parts_turned[g - 1])
            chain(V.tensor_copy, comb_parts[:, :, 0, :], comb_hi[:, :, :].bitcast(F32))
            routed[g] = chain(tt, comb_parts[:, :, 1, :], comb[:, :, :], comb_hi[:, :, :].bitcast(F32), ALU.subtract)
            yield

        def turn_weights(g):
            pe.wait(routed[g], misc_free[0])
            for i in range(GB):
                pe.do(nc.tensor.transpose, misc[0:2 * EXPERTS, i * TOK:(i + 1) * TOK],
                      comb_parts[:, i].rearrange("p a e -> p (a e)"), ident[:, :])
            parts_turned[g] = pe.mark()
            act.wait(parts_turned[g])
            if g >= 2:
                act.wait(comb_used[g - 2])
            misc_free[0] = combT_made[g] = act.do(
                nc.scalar.activation, combT[g % 2][:, :], misc[0:2 * EXPERTS, :], ACT.Copy).mark()

        hid_ready, hid_used, gate_read, up_read, turn_read, weigh_read = {}, {}, {}, {}, {}, {}
        order = list(range(TILES, TILES + STILES)) + list(range(TILES))
        per = TILES + STILES

        def three_pass(ps, parts, w, r):
            n = 0
            for k in range(KD):
                for l, x_ in ((parts[0], xT_hi[r]), (parts[0], xT_lo[r]), (parts[1], xT_hi[r])):
                    pe.do(nc.tensor.matmul, ps, l[:, k, w], x_[:, k, :], start=n == 0, stop=n == 3 * KD - 1)
                    n += 1
            return pe.mark()

        def up_gate(n):
            g, t = divmod(n, per)
            m = order[t]
            s, r = n % 2, g % 2
            w = slice(m * P, (m + 1) * P)
            pe.wait(x_ready[g], gate_up_split)
            if n >= 2:
                pe.wait(gate_read[n - 2])
            made = three_pass(g_ps[s][:, :], gate_w, w, r)
            act.wait(made)
            if n >= 2:
                act.wait(weigh_read[n - 2])
            gate_read[n] = act.do(nc.scalar.activation, silu[s][:, :], g_ps[s][:, :], ACT.Silu).mark()
            if m < TILES:
                pe.wait(combT_made[g], select_made)
                if turn_read:
                    pe.wait(turn_read['last'])
                pe.do(nc.tensor.matmul, c_ps[:, :], select[:, w], combT[g % 2][:, :], start=True, stop=True)
                c_made = comb_used[g] = pe.mark()
            if n >= 2:
                pe.wait(up_read[n - 2])
            made = three_pass(u_ps[s][:, :], up_w, w, r)
            if t == per - 1:
                x_used[g] = made
            dve.wait(gate_read[n])
            if m < TILES:
                dve.wait(c_made)
                turn_read['last'] = dve.do(nc.vector.tensor_tensor, silu[s][:, :], silu[s][:, :], c_ps[:, :],
                                           ALU.mult).mark()
                dve.wait(turn_read['last'])
            dve.wait(made)
            if n >= 2:
                dve.wait(hid_ready[n - 2])
            up_read[n] = weigh_read[n] = dve.do(nc.vector.tensor_tensor, weighed[s], silu[s][:, :],
                                                u_ps[s][:, :], ALU.mult).mark()
            act.wait(up_read[n])
            if n >= 3:
                act.wait(hid_used[n - 3])
            high = act.do(nc.scalar.activation, hid_hi[n % 3][:, :], weighed[s], ACT.Copy).mark()
            pool.wait(high)
            hid_ready[n] = pool.do(nc.gpsimd.tensor_tensor, hid_lo[n % 3][:, :], weighed[s],
                                   hid_hi[n % 3][:, :].bitcast(F32), ALU.subtract).mark()

        def down_proj(n):
            g, t = divmod(n, per)
            m = order[t]
            pe.wait(hid_ready[n], w_split)
            if t == 0 and g:
                pe.wait(out_added[g - 1])
            for i in range(GB):
                for j, (l, r) in enumerate(((hid_hi, 0), (hid_hi, 1), (hid_lo, 0))):
                    pe.do(nc.tensor.matmul, out_ps[i // 2][:, (i % 2) * DIM:(i % 2 + 1) * DIM],
                          l[n % 3][:, i * TOK:(i + 1) * TOK], down_w[r][:, m, :],
                          start=t == 0 and i % 2 == 0 and j == 0, stop=t == per - 1 and j == 2,
                          skip_group_check=True)
            hid_used[n] = pe.mark()
            if t == per - 1:
                dve.wait(hid_used[n])
                for i in range(2):
                    xs = x_all[:, GB * g + 2 * i:GB * g + 2 * i + 2, :].rearrange("p b d -> p (b d)")
                    dve.do(nc.vector.tensor_tensor, xs, xs, out_ps[i][:, :], ALU.add)
                out_added[g] = dve.mark()

        norm(0)
        for k in range(KD):
            turn(0, k)
        split_x(0)
        route_scores(0)
        for _ in route(0):
            pass
        turn_weights(0)
        for n in range(NG * per + 2):
            g, t = divmod(n, per)
            if n < NG * per:
                up_gate(n)
            if n >= 2:
                down_proj(n - 2)
            if g + 1 < NG:
                if t == 1:
                    norm(g + 1)
                if t in (3, 4):
                    turn(g + 1, t - 3)
                if t == 5:
                    split_x(g + 1)
                    route_scores(g + 1)
                if t == 6:
                    steps = route(g + 1)
                if 6 <= t <= 10:
                    next(steps)
                if t == 11:
                    turn_weights(g + 1)


def distances(nc, x_all, ident, half, ctx, ctxT, dist):
    with Stage(nc, "distance") as st:
        pe, act, dve, pool, sp = st.pe, st.act, st.dve, st.pool, st.sp
        ctx_sb = [st.sb(f"ctx{i}", [P, GB, DIM]) for i in range(3)]
        cT = [st.sb(f"ctxT{i}", [P, KD, GB, TOK]) for i in range(3)]
        junk = st.sb("squares", [P, DIM])
        aa = [st.sb(f"ctx_norm{i}", [P, GB]) for i in range(2)]
        xn = [st.sb(f"xn{i}", [P, GB, DIM]) for i in range(2)]
        raw = st.sb("raw_stats", [P, GB, 6])
        mv = [st.sb(f"mean_var{i}", [P, GB, 2]) for i in range(2)]
        var_eps = [st.sb(f"var_eps{i}", [P, GB]) for i in range(2)]
        rstd = [st.sb(f"rstd{i}", [P, GB]) for i in range(2)]
        xT = [st.sb(f"xT{i}", [P, KD, GB * TOK]) for i in range(2)]
        xT2 = [st.sb(f"xT_square{i}", [P, KD, GB * TOK]) for i in range(2)]
        ones = st.sb("ones", [P, P])
        sq = [st.sb(f"squared_dist{i}", [P, GB, TOK]) for i in range(2)]
        dt_ = [st.sb(f"dist{i}", [P, GB, TOK]) for i in range(2)]
        turned = [st.bank(f"turned{i}") for i in range(2)]
        d_ps = [st.bank(f"dist_ps{i}") for i in range(2)]
        load = [st.lane(f"ctx_load{i}") for i in range(3)]
        store = [st.lane(f"dist_store{i}") for i in range(2)]
        const = pool.do(nc.gpsimd.memset, ones[:, :], 1.0).mark()
        r_rstd, landed, normed, turn_copied, x_turned, made = {}, {}, {}, {}, {}, {}
        aa_done, clamp, rooted, stored, sqd = {}, {}, {}, {}, {}

        def fetch(g):
            s = g % 3
            if g >= 3:
                sp.wait(made[g - 3], aa_done[g - 3])
            sp.dma(nc.sync.dma_start, load[s], ctx_sb[s][:, :, :],
                   ctx[GB * g:GB * g + GB].rearrange("b t d -> t b d"))
            for k in range(KD):
                landed[g] = sp.dma(nc.sync.dma_start, load[s], cT[s][:, k, :, :],
                                   ctxT[GB * g:GB * g + GB, k * P:(k + 1) * P, :].rearrange("b p t -> p b t"))

        def norm(g):
            s = g % 2
            xs = [x_all[:, GB * g + i, :] for i in range(GB)]
            if g >= 2:
                dve.wait(x_turned[g - 2])
            normed[g] = normalise(st, [xn[s][:, i, :] for i in range(GB)], xs, mv[s], rstd[s], (r_rstd[g],))

        def measure(g):
            s = g % 2
            xs = [x_all[:, GB * g + i, :] for i in range(GB)]
            got = stats(st, xs, raw, mv[s])
            r_rstd[g] = rsqrt_var(st, mv[s], var_eps[s][:, :], rstd[s][:, :], half, GB, (got,))

        def turn(g):
            s = g % 2
            for k in range(KD):
                pe.wait(normed[g])
                if g:
                    pe.wait(sqd[g - 1, k])
                for i in range(GB):
                    pe.do(nc.tensor.transpose, turned[k][:, i * P:(i + 1) * P], xn[s][:, i, k * P:(k + 1) * P],
                          ident[:, :])
                x_turned[g] = pe.mark()
                dve.wait(x_turned[g])
                act.wait(x_turned[g])
                if g >= 2:
                    dve.wait(made[g - 2])
                    act.wait(made[g - 2])
                turn_copied[g, k] = dve.do(nc.vector.tensor_scalar, xT[s][:, k, :], turned[k][:, :], -2.0,
                                           None, ALU.mult).mark()
                act.wait(turn_copied[g, k])
                sqd[g, k] = act.do(nc.scalar.activation, xT2[s][:, k, :], turned[k][:, :], ACT.Square).mark()
            act.wait(landed[g])
            if g >= 2:
                act.wait(clamp[g - 2])
            for i in range(GB):
                act.do(nc.scalar.activation, junk[:, :], ctx_sb[g % 3][:, i, :], ACT.Square,
                       accum_out=aa[s][:, i:i + 1])
                aa_done[g] = act.mark()
                act.wait(aa_done[g])

        def multiply(g):
            s = g % 2
            pe.wait(landed[g], turn_copied[g, 0], turn_copied[g, 1], sqd[g, 0], sqd[g, 1], const)
            if g >= 2:
                pe.wait(clamp[g - 2])
            for i in range(GB):
                cols = slice(i * TOK, (i + 1) * TOK)
                for k in range(KD):
                    pe.do(nc.tensor.matmul, d_ps[s][:, cols], ones[:, :], xT2[s][:, k, cols],
                          start=k == 0, stop=False)
                for k in range(KD):
                    pe.do(nc.tensor.matmul, d_ps[s][:, cols], cT[g % 3][:, k, i, :], xT[s][:, k, cols],
                          start=False, stop=k == KD - 1)
            made[g] = pe.mark()
            dve.wait(made[g], aa_done[g])
            if g >= 2:
                dve.wait(rooted[g - 2])
            for i in range(GB):
                dve.do(nc.vector.tensor_scalar, sq[s][:, i, :], d_ps[s][:, i * TOK:(i + 1) * TOK],
                       aa[s][:, i:i + 1], 0.0, ALU.add, ALU.max)
            clamp[g] = dve.mark()
            act.wait(clamp[g])
            if g >= 2:
                act.wait(stored[g - 2])
            rooted[g] = act.do(nc.scalar.activation, dt_[s][:, :, :], sq[s][:, :, :], ACT.Sqrt).mark()
            sp.wait(rooted[g])
            stored[g] = sp.dma(nc.sync.dma_start, store[s],
                               dist[GB * g:GB * g + GB].rearrange("b i j -> i b j"), dt_[s][:, :, :])

        measure(0)
        fetch(0)
        fetch(1)
        norm(0)
        measure(1)
        for g in range(NG + 1):
            if g < NG:
                turn(g)
            if g + 1 < NG:
                norm(g + 1)
            if g + 2 < NG:
                measure(g + 2)
            if g:
                multiply(g - 1)
            if g + 2 < NG:
                fetch(g + 2)
        sp.wait(*stored.values())


def align(nc, dist, entries):
    N, CH = TOK, 8
    with Stage(nc, "align") as st:
        dve, pool, sp = st.dve, st.pool, st.sp
        V = nc.vector
        cost = st.sb("cost", [SEQS, N + 1, N + 1])
        best = [st.sb(f"best{i}", [SEQS, CH, N]) for i in range(2)]
        stay = [st.sb(f"not_left{i}", [SEQS, CH, N], BF16) for i in range(2)]
        code = [st.sb(f"code{i}", [SEQS, CH, N]) for i in range(2)]
        rise = st.sb("rise", [SEQS, N, N], mybir.dt.float16)
        columns = st.sb("columns", [SEQS, CH, N])
        junk = st.sb("products", [SEQS, N])
        load = [st.lane(f"dist_load{i}") for i in range(N // CH)]
        landed = [sp.dma(nc.sync.dma_start, load[c], cost[:, 1 + c * CH:1 + (c + 1) * CH, 1:],
                         dist[:, c * CH:(c + 1) * CH, :]) for c in range(N // CH)]
        pool.do(nc.gpsimd.iota, columns[:, :, :], pattern=[[256, CH], [1, N]], base=0, channel_multiplier=0,
                allow_small_or_imprecise_dtypes=True)
        pool.do(nc.gpsimd.memset, cost[:, :, 0:1], BIG)
        pool.do(nc.gpsimd.memset, cost[:, 0, 1:], BIG)
        pool.do(nc.gpsimd.memset, entries[:, N:N + 1], N - 1.0)
        pool.do(nc.gpsimd.memset, best[0][:, 0, :], BIG)
        edges = pool.mark()
        pool.wait(edges)
        edges = pool.do(nc.gpsimd.memset, best[0][:, 0, 0:1], 0.0).mark()
        dve.wait(edges)

        coded, maxed, risen, read = {}, {}, {}, {}

        def coding(c):
            s = c % 2
            above = cost[:, c * CH:c * CH + CH, :]
            here = cost[:, c * CH + 1:c * CH + CH + 1, :]

            def not_left():
                if c >= 2:
                    dve.wait(coded[c - 2])
                read[c] = dve.do(V.tensor_tensor, stay[s][:, :, :], here[:, :, 0:N], best[s][:, :, :],
                                 ALU.is_ge).mark()

            def diagonal():
                if c >= 2:
                    dve.wait(risen[c - 2])
                done = dve.do(V.tensor_tensor, code[s][:, :, :], above[:, :, 0:N], above[:, :, 1:],
                              ALU.is_le).mark()
                dve.wait(done)

            def column():
                done = dve.do(V.scalar_tensor_tensor, code[s][:, :, :], code[s][:, :, :], -0.75,
                              columns[:, :, :], ALU.mult, ALU.add).mark()
                pool.wait(done)
                coded[c] = pool.do(nc.gpsimd.tensor_tensor, code[s][:, :, :], code[s][:, :, :],
                                   stay[s][:, :, :], ALU.mult).mark()

            def running_max():
                dve.wait(coded[c])
                flat = code[s][:, :, :].rearrange("p r j -> p (r j)")
                maxed[c] = dve.do(V.tensor_tensor_scan, flat, flat, flat, 0.0, ALU.max, ALU.max).mark()
                pool.wait(maxed[c])
                risen[c] = pool.do(nc.gpsimd.tensor_tensor, rise[:, c * CH:(c + 1) * CH, 1:],
                                   code[s][:, :, 1:], code[s][:, :, 0:N - 1], ALU.subtract).mark()

            return [not_left, diagonal, column, None, None, running_max]

        row, between = None, []
        for i in range(N):
            c, r = divmod(i, CH)
            s = c % 2
            if r == 0:
                dve.wait(landed[c])
            if i:
                dve.wait(row)
                if r == 0 and c >= 2:
                    dve.wait(read[c - 2])
                least = dve.do(V.tensor_tensor, best[s][:, r, :], cost[:, i, 1:], cost[:, i, 0:N], ALU.min).mark()
                dve.wait(least)
            row = dve.do(V.tensor_tensor_scan, cost[:, i + 1, 1:], best[s][:, r, :], cost[:, i + 1, 1:], BIG,
                         ALU.min, ALU.add).mark()
            step = between.pop(0) if between else None
            if step:
                step()
            if r == CH - 1:
                between = coding(c)
        dve.wait(row)
        for step in between:
            if step:
                step()
        dve.wait(risen[N // CH - 1])
        for i in reversed(range(N)):
            done = dve.do(V.scalar_tensor_tensor, junk[:, 1:], columns[:, 0, 1:], entries[:, i + 1:i + 2],
                          rise[:, i, 1:], ALU.is_le, ALU.mult, accum_out=entries[:, i:i + 1]).mark()
            dve.wait(done)


def conv_ffn(nc, x_all, ident, half, ctx, entries, w1T, w2T, conv_w, conv_b, out):
    TILES = CONV_HID // P
    with Stage(nc, "conv") as st:
        pe, act, dve, pool, sp = st.pe, st.act, st.dve, st.pool, st.sp
        w1q = st.sb("w1_ternary", [P, KD, CONV_HID], F32R)
        w2q = st.sb("w2_ternary", [P, TILES, DIM], BF16)
        w_sb = st.sb("w_stage", [P, 2, KD * CONV_HID])
        absum = st.sb("abs_sum", [P, 2])
        w_mean = st.sb("w_mean", [P, 2])
        w_inv = st.sb("w_inv", [P, 2])
        ones = st.sb("ones", [P, P])
        cw = st.sb("conv_w", [P, TILES, 3])
        cb = st.sb("conv_b", [P, TILES])
        ctx_sb = [st.sb(f"ctx{i}", [P, GB, DIM]) for i in range(2)]
        column = st.sb("column", [P, TOK])
        bounds = st.sb("path_bounds", [P, 2, SEQS])
        not_before = [st.sb(f"not_before{i}", [P, GB, TOK]) for i in range(2)]
        path_sb = [st.sb(f"path{i}", [P, GB, TOK]) for i in range(2)]
        raw = st.sb("raw_stats", [P, GB, 6])
        mv = st.sb("mean_var", [P, GB, 2])
        var_eps = st.sb("var_eps", [P, GB])
        rstd = st.sb("rstd", [P, GB])
        xn = st.sb("xn", [P, GB, DIM])
        amax = st.sb("x_absmax", [P, GB])
        inv1 = st.sb("x_inv", [P, GB])
        q1 = st.sb("x_scale", [P, GB])
        x_unit = st.sb("x_unit", [P, GB])
        xT_hi, xT_lo = ([st.sb(f"xT_{n}{i}", [P, KD, GB * TOK], F32R) for i in range(2)] for n in ("hi", "lo"))
        acc = [st.sb(f"acc{i}", [P, GB, TOK]) for i in range(3)]
        act_h = [st.sb(f"act_h{i}", [P, TILES, GB * TOK]) for i in range(2)]
        hmax = st.sb("h_absmax_part", [P, GB * TOK])
        amax2 = st.sb("h_absmax", [P, GB])
        inv2 = [st.sb(f"h_inv{i}", [P, GB]) for i in range(2)]
        q2 = st.sb("h_scale", [P, GB])
        q2_b = st.sb("h_scale_b", [P, GB * TOK])
        hq = st.sb("hq", [P, TILES, GB * TOK], BF16)
        x_out = [st.sb(f"x_out{i}", [P, GB, DIM]) for i in range(2)]
        ex_ps = st.bank("expand")
        t_ps = st.bank("turned")
        b_ps = st.bank("broadcast")
        h_ps = [st.bank(f"h_ps{i}") for i in range(3)]
        o_ps = [st.bank(f"out_ps{i}") for i in range(2)]

        w_lane = st.lane("weight_load")
        sp.dma(nc.sync.dma_start, w_lane, w_sb[:, 0, :].rearrange("p (k n) -> p k n", k=KD),
               w1T.rearrange("(k p) n -> p k n", p=P))
        sp.dma(nc.sync.dma_start, w_lane, w_sb[:, 1, :].rearrange("p (m n) -> p m n", m=TILES),
               w2T.rearrange("(m p) n -> p m n", p=P))
        sp.dma(nc.sync.dma_start, w_lane, cw[:, :, :], conv_w)
        w_in = sp.dma(nc.sync.dma_start, w_lane, cb[:, :], conv_b)
        const = pool.do(nc.gpsimd.memset, ones[:, :], 1.0).mark()
        load = [st.lane(f"load{i}") for i in range(2)]
        store = [st.lane(f"store{i}") for i in range(2)]
        landed, expanded, x_added, quantised, x_turned, x_ready = {}, {}, {}, {}, {}, {}
        scaled_up, xn_norm, turned_hi = {}, {}, {}
        t_free = [None]
        made, conv_done, silu_done, x_used = {}, {}, {}, {}
        mid = {}
        maxed, max_turned, q2_ready, hq_ready, out_made, finished, stored = {}, {}, {}, {}, {}, {}, {}
        q2b_ready, inv2_ready, weight = {}, {}, {}
        b_free = [None]

        def weight_means():
            dve.wait(w_in)
            for n in range(2):
                dve.do(nc.vector.tensor_reduce, absum[:, n:n + 1], w_sb[:, n, :], AX.X, ALU.add,
                       apply_absolute_value=True)
            summed = dve.mark()
            pe.wait(summed, const)
            total = pe.do(nc.tensor.matmul, b_ps[:, 0:2], ones[:, :], absum[:, :], start=True, stop=True).mark()
            dve.wait(total)
            b_free[0] = weight['mean'] = dve.do(nc.vector.tensor_scalar, w_mean[:, :], b_ps[:, 0:2],
                                                1.0 / (DIM * CONV_HID), 1e-5, ALU.mult, ALU.max).mark()
            dve.wait(weight['mean'])
            r = dve.do(nc.vector.reciprocal, w_inv[:, :], w_mean[:, :]).mark()
            act.wait(r)
            for n in range(2):
                weight['scaled', n] = act.do(nc.scalar.activation, w_sb[:, n, :], w_sb[:, n, :], ACT.Copy,
                                             scale=w_inv[:, n:n + 1], bias=ROUND).mark()

        def weight_ternary(n, dst):
            w = w_sb[:, n, :]
            dve.wait(weight['scaled', n])
            r = dve.do(nc.vector.tensor_scalar, w, w, ROUND, 1.0, ALU.subtract, ALU.min).mark()
            dve.wait(r)
            weight[n] = dve.do(nc.vector.tensor_scalar, dst, w, -1.0, None, ALU.max).mark()

        ramp = pool.do(nc.gpsimd.iota, column[:, :], pattern=[[1, TOK]], base=0, channel_multiplier=0,
                       allow_small_or_imprecise_dtypes=True).mark()
        for n in range(2):
            pe.do(nc.tensor.transpose, ex_ps[:, n * SEQS:(n + 1) * SEQS], entries[:, 1 - n:1 - n + TOK],
                  ident[0:SEQS, 0:SEQS])
        bounds_made = pe.mark()
        act.wait(bounds_made)
        bounds_ready = act.do(nc.scalar.copy, bounds[:, :, :],
                              ex_ps[:, 0:2 * SEQS].rearrange("p (a b) -> p a b", a=2)).mark()
        from_left, path_made = {}, {}

        def path_left(g):
            s = g % 2
            if g >= 2:
                sp.wait(expanded[g - 2])
                pool.wait(path_made[g - 2])
            landed[g] = sp.dma(nc.sync.dma_start, load[s], ctx_sb[s][:, :, :],
                               ctx[GB * g:GB * g + GB].rearrange("b t d -> t b d"))
            pool.wait(bounds_ready, ramp)
            for i in range(GB):
                pool.do(nc.gpsimd.tensor_scalar, not_before[s][:, i, :], column[:, :],
                        bounds[:, 1, GB * g + i:GB * g + i + 1], None, ALU.is_ge)
            from_left[g] = pool.mark()

        def path_right(g):
            s = g % 2
            dve.wait(from_left[g], bounds_ready)
            if g >= 2:
                dve.wait(expanded[g - 2])
            for i in range(GB):
                dve.do(nc.vector.scalar_tensor_tensor, path_sb[s][:, i, :], column[:, :],
                       bounds[:, 0, GB * g + i:GB * g + i + 1], not_before[s][:, i, :], ALU.is_le, ALU.mult)
            path_made[g] = dve.mark()

        def expand(g):
            s = g % 2
            pe.wait(landed[g], path_made[g], bounds_ready)
            if g:
                pe.wait(x_added[g - 1], t_free[0])
            for bank, first in ((ex_ps, 0), (t_ps, 2)):
                for i in range(2):
                    pe.do(nc.tensor.matmul, bank[:, i * DIM:(i + 1) * DIM], path_sb[s][:, first + i, :],
                          ctx_sb[s][:, first + i, :], start=True, stop=True)
            expanded[g] = pe.mark()

        def add_expanded(g):
            dve.wait(expanded[g])
            for bank, first in ((ex_ps, 0), (t_ps, 2)):
                xs = x_all[:, GB * g + first:GB * g + first + 2, :].rearrange("p b d -> p (b d)")
                dve.do(nc.vector.tensor_tensor, xs, xs, bank[:, :], ALU.add)
            t_free[0] = x_added[g] = dve.mark()

        r_rstd = {}

        def quant_a(g):
            xs = [x_all[:, GB * g + i, :] for i in range(GB)]
            dve.wait(x_added[g])
            got = stats(st, xs, raw, mv)
            r_rstd[g] = rsqrt_var(st, mv, var_eps[:, :], rstd[:, :], half, GB, (got,))

        def quant_b(g):
            xs = [x_all[:, GB * g + i, :] for i in range(GB)]
            if g:
                dve.wait(x_turned[g - 1])
            one = normalise(st, [xn[:, i, :] for i in range(GB)], xs, mv, rstd, (r_rstd[g],))
            dve.wait(one)

        def quant_c(g):
            V = nc.vector
            r = dve.do(V.tensor_reduce, amax[:, :], xn[:, :, :], AX.X, ALU.max, apply_absolute_value=True).mark()
            dve.wait(r)
            r = dve.do(V.tensor_scalar, inv1[:, :], amax[:, :], 1e-5, 1.0 / 127.0, ALU.max, ALU.mult).mark()
            dve.wait(r)
            dve.do(V.reciprocal, q1[:, :], inv1[:, :])
            dve.do(V.tensor_scalar, x_unit[:, :], inv1[:, :], w_mean[:, 0:1], None, ALU.mult)
            xn_norm[g] = dve.mark()
            act.wait(xn_norm[g])
            for i in range(GB):
                act.do(nc.scalar.activation, xn[:, i, :], xn[:, i, :], ACT.Copy, scale=q1[:, i:i + 1], bias=ROUND)
            scaled_up[g] = act.mark()

        def quant_d(g):
            dve.wait(scaled_up[g])
            whole = dve.do(nc.vector.tensor_scalar, xn[:, :, :], xn[:, :, :], ROUND, 127.0,
                           ALU.subtract, ALU.min).mark()
            act.wait(whole)
            for i in range(GB):
                act.do(nc.scalar.activation, xn[:, i, :], xn[:, i, :], ACT.Copy, scale=x_unit[:, i:i + 1])
            quantised[g] = act.mark()

        def turn(g, k):
            pe.wait(quantised[g], t_free[0])
            for i in range(GB):
                pe.do(nc.tensor.transpose, t_ps[:, i * P:(i + 1) * P], xn[:, i, k * P:(k + 1) * P], ident[:, :])
            x_turned[g] = pe.mark()

        def leading_part(g, k):
            s = g % 2
            act.wait(x_turned[g])
            if g >= 2:
                act.wait(x_used[g - 2])
            turned_hi[g, k] = act.do(nc.scalar.activation, xT_hi[s][:, k, :], t_ps[:, :], ACT.Copy).mark()

        def trailing_part(g, k):
            s = g % 2
            dve.wait(turned_hi[g, k])
            t_free[0] = x_ready[g] = dve.do(nc.vector.tensor_tensor, xT_lo[s][:, k, :], t_ps[:, :],
                                            xT_hi[s][:, k, :].bitcast(F32), ALU.subtract).mark()

        def hidden(n):
            g, m = divmod(n, TILES)
            s = g % 2
            ps = h_ps[n % 3]
            pe.wait(x_ready[g], weight[0])
            if n >= 3:
                pe.wait(conv_done[n - 3])
            for k in range(KD):
                for part in (xT_hi, xT_lo):
                    pe.do(nc.tensor.matmul, ps[:, :], w1q[:, k, m * P:(m + 1) * P], part[s][:, k, :],
                          start=k == 0 and part is xT_hi, stop=k == KD - 1 and part is xT_lo)
            made[n] = pe.mark()
            if m == TILES - 1:
                x_used[g] = made[n]

        def middle(n):
            m, r = n % TILES, n % 3
            act.wait(made[n])
            if n >= 3:
                act.wait(silu_done[n - 3])
            mid[n] = act.do(nc.scalar.activation, acc[r][:, :, :], h_ps[r][:, :].rearrange("p (b t) -> p b t", b=GB),
                            ACT.Identity, scale=cw[:, m, 1:2], bias=cb[:, m:m + 1]).mark()

        def taps(n):
            m, r = n % TILES, n % 3
            h = h_ps[r][:, :].rearrange("p (b t) -> p b t", b=GB)
            dve.wait(mid[n])
            one = dve.do(nc.vector.scalar_tensor_tensor, acc[r][:, :, 1:], h[:, :, 0:TOK - 1],
                         cw[:, m, 0:1], acc[r][:, :, 1:], ALU.mult, ALU.add).mark()
            dve.wait(one)
            conv_done[n] = dve.do(nc.vector.scalar_tensor_tensor, acc[r][:, :, 0:TOK - 1], h[:, :, 1:],
                                  cw[:, m, 2:3], acc[r][:, :, 0:TOK - 1], ALU.mult, ALU.add).mark()

        def silu(n):
            g, m = divmod(n, TILES)
            s, r = g % 2, n % 3
            act.wait(conv_done[n])
            if g >= 2:
                act.wait(hq_ready[g - 2, TILES - 1])
            silu_done[n] = act.do(nc.scalar.activation,
                                  act_h[s][:, m, :].rearrange("p (b t) -> p b t", b=GB),
                                  acc[r][:, :, :], ACT.Silu).mark()

        def hidden_max(g, part):
            s = g % 2
            cols = slice(part * 2 * TOK, (part + 1) * 2 * TOK)
            dve.wait(silu_done[g * TILES + TILES - 1])
            if g:
                dve.wait(max_turned[g - 1])
            maxed[g] = dve.do(nc.vector.tensor_reduce, hmax[:, cols],
                              act_h[s][:, :, cols].rearrange("p m t -> p t m"), AX.X, ALU.max,
                              apply_absolute_value=True).mark()

        def turn_max(g):
            pe.wait(maxed[g], b_free[0])
            for i in range(GB):
                pe.do(nc.tensor.transpose, b_ps[:, i * TOK:(i + 1) * TOK], hmax[:, i * TOK:(i + 1) * TOK],
                      ident[:, :])
            max_turned[g] = pe.mark()

        def hidden_scale(g):
            s = g % 2
            V = nc.vector
            dve.wait(max_turned[g])
            b_free[0] = r = dve.do(V.tensor_reduce, amax2[:, :], b_ps[:, :].rearrange("p (b t) -> p b t", b=GB),
                                   AX.X, ALU.max).mark()
            dve.wait(r)
            r = dve.do(V.tensor_scalar, amax2[:, :], amax2[:, :], 1e-5, 1.0 / 127.0, ALU.max, ALU.mult).mark()
            dve.wait(r)
            if g:
                dve.wait(q2_ready[g - 1, 'turned'])
            if g >= 2:
                dve.wait(weighed_out[g - 2])
            dve.do(V.tensor_scalar, inv2[s][:, :], amax2[:, :], w_mean[:, 1:2], None, ALU.mult)
            q2_ready[g] = inv2_ready[g] = dve.do(V.reciprocal, q2[:, :], amax2[:, :]).mark()
            dve.wait(q2_ready[g])

        def spread_scale(g):
            pe.wait(q2_ready[g], b_free[0])
            for i in range(GB):
                pe.do(nc.tensor.transpose, b_ps[:, i * TOK:(i + 1) * TOK], q2[:, i:i + 1].broadcast_to([P, P]),
                      ident[:, :])
            q2_ready[g, 'turned'] = pe.mark()
            act.wait(q2_ready[g, 'turned'])
            if g:
                act.wait(scaled[g - 1, TILES - 1])
            b_free[0] = q2b_ready[g] = act.do(nc.scalar.copy, q2_b[:, :], b_ps[:, :]).mark()

        scaled, rounded, weighed_out = {}, {}, {}

        def scale_tile(g, m):
            t = act_h[g % 2][:, m, :]
            pool.wait(q2b_ready[g])
            scaled[g, m] = pool.do(nc.gpsimd.tensor_tensor, t, t, q2_b[:, :], ALU.mult).mark()

        def round_tile(g, m):
            t = act_h[g % 2][:, m, :]
            act.wait(scaled[g, m])
            rounded[g, m] = act.do(nc.scalar.activation, t, t, ACT.Copy, bias=ROUND).mark()

        def quant_tile(g, m):
            dve.wait(rounded[g, m])
            if g:
                dve.wait(out_made[g - 1])
            hq_ready[g, m] = dve.do(nc.vector.tensor_scalar, hq[:, m, :], act_h[g % 2][:, m, :], ROUND, 127.0,
                                    ALU.subtract, ALU.min).mark()

        def output(g, half_):
            s = g % 2
            bank = o_ps[half_]
            pe.wait(*[hq_ready[g, m] for m in range(TILES)], weight[1])
            if g:
                pe.wait(weighed_out[g - 1])
            for i in range(2):
                for m in range(TILES):
                    pe.do(nc.tensor.matmul, bank[:, i * DIM:(i + 1) * DIM],
                          hq[:, m, (2 * half_ + i) * TOK:(2 * half_ + i + 1) * TOK], w2q[:, m, :],
                          start=m == 0, stop=m == TILES - 1)
            out_made[g] = pe.mark()
            act.wait(out_made[g], inv2_ready[g])
            if g >= 2:
                act.wait(stored[g - 2])
            for i in range(2):
                b = 2 * half_ + i
                act.do(nc.scalar.activation, x_out[s][:, b, :], bank[:, i * DIM:(i + 1) * DIM], ACT.Copy,
                       scale=inv2[s][:, b:b + 1])
            weighed_out[g] = act.mark()
            pool.wait(weighed_out[g])
            rows = slice(2 * half_, 2 * half_ + 2)
            finished[g] = pool.do(nc.gpsimd.tensor_tensor, x_out[s][:, rows, :], x_out[s][:, rows, :],
                                  x_all[:, GB * g + 2 * half_:GB * g + 2 * half_ + 2, :], ALU.add).mark()
            if half_:
                sp.wait(finished[g])
                stored[g] = sp.dma(nc.sync.dma_start, store[s],
                                   out[GB * g:GB * g + GB].rearrange("b t d -> t b d"), x_out[s][:, :, :])

        path_left(0)
        path_right(0)
        expand(0)
        add_expanded(0)
        quant_a(0)
        quant_b(0)
        weight_means()
        quant_c(0)
        weight_ternary(0, w1q[:, :, :].rearrange("p k n -> p (k n)"))
        quant_d(0)
        for k in range(KD):
            turn(0, k)
            leading_part(0, k)
            trailing_part(0, k)
        weight_ternary(1, w2q[:, :, :].rearrange("p m n -> p (m n)"))
        path_left(1)
        path_right(1)
        expand(1)

        for n in range((NG + 2) * TILES):
            g, m = divmod(n, TILES)
            tiles = lambda n: [((n // TILES) - 1 if n % TILES >= 5 else (n // TILES) - 2, j)
                               for j in {5: (0, 1), 6: (2, 3), 7: (4, 5), 0: (6, 7)}.get(n % TILES, ())]
            due = [(a, j) for a, j in tiles(n - 1) if 0 <= a < NG]
            if g + 1 < NG and m in (6, 7):
                leading_part(g + 1, m - 6)
            for a, j in due:
                round_tile(a, j)
            if 3 <= n <= NG * TILES + 2:
                silu(n - 3)
            if 1 <= n <= NG * TILES:
                middle(n - 1)
            if n < NG * TILES:
                hidden(n)
            if 2 <= n <= NG * TILES + 1:
                taps(n - 2)
            if g + 1 < NG and m in (6, 7):
                trailing_part(g + 1, m - 6)
            for a, j in tiles(n):
                if 0 <= a < NG:
                    scale_tile(a, j)
            for a, j in due:
                quant_tile(a, j)
            if 2 <= g <= NG + 1 and m in (2, 3):
                output(g - 2, m - 2)
            if 1 <= g <= NG:
                if m == 2:
                    hidden_max(g - 1, 0)
                if m == 3:
                    hidden_max(g - 1, 1)
                    turn_max(g - 1)
                if m == 4:
                    hidden_scale(g - 1)
                    spread_scale(g - 1)
            if g + 1 < NG:
                if m == 0:
                    add_expanded(g + 1)
                    quant_a(g + 1)
                if m == 1:
                    quant_b(g + 1)
                if m == 2:
                    quant_c(g + 1)
                if m == 4:
                    quant_d(g + 1)
                if m in (5, 6):
                    turn(g + 1, m - 5)
                if g + 2 < NG:
                    if m == 3:
                        path_left(g + 2)
                    if m == 5:
                        path_right(g + 2)
                    if m == 7:
                        expand(g + 2)
        sp.wait(*stored.values())


def build(nc, x, ctx, ctxT, wq, wkv, wo, ln_cols, router, bias, gate, up, down, s_gate, s_up, s_down,
          w1T, w2T, conv_w, conv_b, out):
    dist = nc.dram_tensor("dist", (SEQS, TOK, TOK), F32, kind="Internal").ap()
    with nc.sbuf_tensor("x_all", [P, SEQS, DIM], F32) as x_all, \
            nc.sbuf_tensor("ident", [P, P], F32) as ident, nc.sbuf_tensor("minus_half", [P, 4], F32) as half:
        attention(nc, x_all, ident, half, x, ctx, wq, wkv, wo, ln_cols)
        experts(nc, x_all, ident, half, router, bias, gate, up, down, s_gate, s_up, s_down)
        distances(nc, x_all, ident, half, ctx, ctxT, dist)
        with nc.sbuf_tensor("path_entries", [SEQS, TOK + 1], F32) as entries:
            align(nc, dist, entries)
            conv_ffn(nc, x_all, ident, half, ctx, entries, w1T, w2T, conv_w, conv_b, out)


def kernel(**inputs):
    import concourse.bacc as bacc
    from concourse.bass_utils import run_bass_kernel_spmd

    a = {n: np.asarray(v) for n, v in inputs.items()}
    tiles = CONV_HID // P
    arrays = {
        "x": a["x"],
        "ctx": a["ctx_1024"],
        "ctxT": a["ctx_1024"].transpose(0, 2, 1),
        "wq": a["L0_xattn_Wq"],
        "wkv": a["L0_xattn_Wkv"],
        "wo": a["L0_xattn_Wo"],
        "ln_cols": np.stack([a["L0_xattn_ln1_w"], a["L0_xattn_ln1_b"], a["L0_xattn_ln2_w"],
                             a["L0_xattn_ln2_b"]]).reshape(4, KD, P).transpose(2, 0, 1),
        "router": a["L0_ffn_router_w"].T,
        "bias": np.broadcast_to(a["L0_ffn_correction_bias"], (P, EXPERTS)),
        "gate": a["L0_ffn_gate_w"].transpose(1, 0, 2).reshape(DIM, ROUTED),
        "up": a["L0_ffn_up_w"].transpose(1, 0, 2).reshape(DIM, ROUTED),
        "down": a["L0_ffn_down_w"].reshape(ROUTED, DIM),
        "s_gate": a["L0_ffn_shared_gate_w"].T,
        "s_up": a["L0_ffn_shared_up_w"].T,
        "s_down": a["L0_ffn_shared_down_w"].T,
        "w1T": a["L1_ffn_w1"].T,
        "w2T": a["L1_ffn_w2"].T,
        "conv_w": a["L1_ffn_conv_w"].reshape(tiles, P, 3).transpose(1, 0, 2),
        "conv_b": a["L1_ffn_conv_b"].reshape(tiles, P).T,
    }
    arrays = {f"in_{n}": np.ascontiguousarray(v) for n, v in arrays.items()}
    nc = bacc.Bacc("TRN2", target_bir_lowering=False, num_devices=1)
    args = [nc.dram_tensor(n, v.shape, mybir.dt.from_np(v.dtype), kind="ExternalInput").ap()
            for n, v in arrays.items()]
    out = nc.dram_tensor("out", (SEQS, TOK, DIM), F32, kind="ExternalOutput").ap()
    build(nc, *args, out)
    r = run_bass_kernel_spmd(nc, [arrays], core_ids=[0])
    return r.results[0]["out"]
```
